# Optimizing a Trainium2 kernel written in Bass

```python
import numpy as np
import jax
import jax.numpy as jnp

def _softmax(x, axis=-1):
    return jax.nn.softmax(x, axis=axis)

def _gelu(x):
    return jax.nn.gelu(x, approximate=True)

def _silu(x):
    return jax.nn.silu(x)

def _sigmoid(x):
    return jax.nn.sigmoid(x)

def _layernorm(x, axis=-1, eps=1e-05):
    m = jnp.mean(x, axis=axis, keepdims=True)
    v = jnp.var(x, axis=axis, keepdims=True)
    return (x - m) / jnp.sqrt(v + eps)

def _scatter_add(tgt, idx, src, axis=0):
    return tgt.at[idx].add(src)

def _segment_sum(src, seg, n):
    return jax.ops.segment_sum(src, seg, n)
kernel_name = 'mk_decoder_postln_d1_seqx_r4_4ad5f7'

def setup_inputs(seed: int=0):
    np.random.seed(seed)
    _w = jnp.asarray

    def _rec_inputs():
        import jax
        import jax.numpy as jnp
        _rk = jax.random.key(seed)
        x = -0.0002928 + 1 * jax.random.normal(jax.random.fold_in(_rk, 1), (16, 256, 256), jnp.float32)
        _lenS = 256 - jax.random.randint(jax.random.fold_in(_rk, 7), (16,), 0, max(1, 256 // 4) + 1, jnp.int32)
        _lenS2 = 77 - jax.random.randint(jax.random.fold_in(_rk, 8), (16,), 0, max(1, 77 // 4) + 1, jnp.int32)
        _ctx_1024P = jax.random.normal(jax.random.fold_in(_rk, 11), (16, 16, 256), jnp.float32)
        _ctx_1024c = jax.random.dirichlet(jax.random.fold_in(_rk, 511), 0.3 * jnp.ones((16,), jnp.float32), (16, 77))
        _ctx_1024t = jnp.einsum('bsk,bkd->bsd', _ctx_1024c, _ctx_1024P)
        _ctx_1024t = _ctx_1024t * jax.lax.rsqrt(jnp.mean(jnp.square(_ctx_1024t)) + 1e-12) * 0.953939
        ctx_1024 = -1.39393e-06 + 0.999914 * (_ctx_1024t + 0.3 * jax.random.normal(jax.random.fold_in(_rk, 611), (16, 77, 256), jnp.float32))
        _validS = jnp.arange(256)[None, :] < _lenS[:, None]
        _validS2 = jnp.arange(77)[None, :] < _lenS2[:, None]
        _causal = jnp.tril(jnp.ones((256, 256), dtype=bool))
        mask_BxSxS2_if1 = jnp.where(jnp.ones((16, 256, 77), dtype=bool), 1, 0).astype(jnp.int32)
        return (x, ctx_1024, mask_BxSxS2_if1)
    x, ctx_1024, mask_BxSxS2_if1 = _rec_inputs()

    def _L0_attn_setup():
        import jax, jax.numpy as jnp
        import numpy as np
        B, N, D = (2, 2048, 256)
        H, Dh = (16, 64)
        P = H * Dh
        EPS = 1e-06
        DECAY_BIAS_SHIFT = 2.0

        def _elu_plus_one(x):
            return jax.nn.elu(x) + 1.0

        def _ssd_scan(q, k, v, a, eps):
            qT = jnp.moveaxis(q, 2, 0)
            kT = jnp.moveaxis(k, 2, 0)
            vT = jnp.moveaxis(v, 2, 0)
            aT = jnp.moveaxis(a, 2, 0)
            Bb, Hh, _, Dk = q.shape
            Dv = v.shape[-1]
            S0 = jnp.zeros((Bb, Hh, Dk, Dv), q.dtype)
            z0 = jnp.zeros((Bb, Hh, Dk), q.dtype)

            def step(carry, inp):
                S, z = carry
                qt, kt, vt, at = inp
                S = at[..., None, None] * S + kt[..., :, None] * vt[..., None, :]
                z = at[..., None] * z + kt
                num = jnp.einsum('bhk,bhkv->bhv', qt, S)
                den = jnp.einsum('bhk,bhk->bh', qt, z) + eps
                return ((S, z), num / den[..., None])
            _, outT = jax.lax.scan(step, (S0, z0), (qT, kT, vT, aT))
            return jnp.moveaxis(outT, 0, 2)
        key = jax.random.key(seed)
        ks = jax.random.split(key, 7)
        s_in = 1.0 / np.sqrt(D)
        s_out = 1.0 / np.sqrt(P)
        return {'x': jax.random.normal(ks[0], (B, N, D), jnp.float32), 'Wq': jax.random.normal(ks[1], (D, P), jnp.float32) * s_in, 'Wk': jax.random.normal(ks[2], (D, P), jnp.float32) * s_in, 'Wv': jax.random.normal(ks[3], (D, P), jnp.float32) * s_in, 'Wo': jax.random.normal(ks[4], (P, D), jnp.float32) * s_out, 'Wa': jax.random.normal(ks[5], (D, H), jnp.float32) * s_in, 'ba': jnp.zeros((H,), jnp.float32)}
    _L0_attn_all = _L0_attn_setup()
    _L0_attn_in = {k: v for k, v in _L0_attn_all.items() if k in ('Wq', 'Wk', 'Wv', 'Wo', 'Wa', 'ba')}
    del _L0_attn_all

    def _L0_xattn_setup():
        import jax, jax.numpy as jnp
        import numpy as np
        B, S, D, H = (2, 512, 256, 16)
        DK = D // H

        def _split_heads(x):
            b, s, _ = x.shape
            return x.reshape(b, s, H, DK).transpose(0, 2, 1, 3)
        key = jax.random.key(seed)
        ks = jax.random.split(key, 12)
        sc = 0.02
        inp = {'q': jax.random.normal(ks[0], (B, S, D), jnp.float32), 'k': jax.random.normal(ks[1], (B, S, D), jnp.float32), 'v': jax.random.normal(ks[2], (B, S, D), jnp.float32), 'mask': jnp.ones((B, S, S), jnp.int32), 'Wq': jax.random.normal(ks[3], (D, D), jnp.float32) * sc, 'bq': jnp.zeros((D,), jnp.float32), 'Wk': jax.random.normal(ks[4], (D, D), jnp.float32) * sc, 'bk': jnp.zeros((D,), jnp.float32), 'Wv': jax.random.normal(ks[5], (D, D), jnp.float32) * sc, 'bv': jnp.zeros((D,), jnp.float32), 'Wo': jax.random.normal(ks[6], (D, D), jnp.float32) * sc, 'bo': jnp.zeros((D,), jnp.float32)}
        return inp
    _L0_xattn_all = _L0_xattn_setup()
    _L0_xattn_in = {k: v for k, v in _L0_xattn_all.items() if k in ('Wq', 'bq', 'Wk', 'bk', 'Wv', 'bv', 'Wo', 'bo')}
    del _L0_xattn_all

    def _L0_ffn_setup():
        import jax, jax.numpy as jnp
        import numpy as np
        D_MODEL, D_FF, N_EXPERTS, TOP_K = (256, 512, 8, 2)
        B, S = (2, 512)
        key = jax.random.key(seed)
        ks = jax.random.split(key, 6)
        sd = 1.0 / np.sqrt(D_MODEL)
        sf = 1.0 / np.sqrt(D_FF)
        return {'x': jax.random.normal(ks[0], (B, S, D_MODEL), jnp.float32), 'router_w': jax.random.normal(ks[1], (N_EXPERTS, D_MODEL), jnp.float32) * sd, 'gate_w': jax.random.normal(ks[2], (N_EXPERTS, D_MODEL, D_FF), jnp.float32) * sd, 'gate_b': jnp.zeros((N_EXPERTS, D_FF), jnp.float32), 'up_w': jax.random.normal(ks[3], (N_EXPERTS, D_MODEL, D_FF), jnp.float32) * sd, 'up_b': jnp.zeros((N_EXPERTS, D_FF), jnp.float32), 'down_w': jax.random.normal(ks[4], (N_EXPERTS, D_FF, D_MODEL), jnp.float32) * sf, 'down_b': jnp.zeros((N_EXPERTS, D_MODEL), jnp.float32)}
    _L0_ffn_all = _L0_ffn_setup()
    _L0_ffn_in = {k: v for k, v in _L0_ffn_all.items() if k in ('router_w', 'gate_w', 'gate_b', 'up_w', 'up_b', 'down_w', 'down_b')}
    del _L0_ffn_all
    return {'x': x, 'ctx_1024': ctx_1024, 'mask_BxSxS2_if1': mask_BxSxS2_if1, 'L0_attn_Wq': _L0_attn_in['Wq'], 'L0_attn_Wk': _L0_attn_in['Wk'], 'L0_attn_Wv': _L0_attn_in['Wv'], 'L0_attn_Wo': _L0_attn_in['Wo'], 'L0_attn_Wa': _L0_attn_in['Wa'], 'L0_attn_ba': _L0_attn_in['ba'], 'L0_xattn_Wq': _L0_xattn_in['Wq'], 'L0_xattn_bq': _L0_xattn_in['bq'], 'L0_xattn_Wk': _L0_xattn_in['Wk'], 'L0_xattn_bk': _L0_xattn_in['bk'], 'L0_xattn_Wv': _L0_xattn_in['Wv'], 'L0_xattn_bv': _L0_xattn_in['bv'], 'L0_xattn_Wo': _L0_xattn_in['Wo'], 'L0_xattn_bo': _L0_xattn_in['bo'], 'L0_ffn_router_w': _L0_ffn_in['router_w'], 'L0_ffn_gate_w': _L0_ffn_in['gate_w'], 'L0_ffn_gate_b': _L0_ffn_in['gate_b'], 'L0_ffn_up_w': _L0_ffn_in['up_w'], 'L0_ffn_up_b': _L0_ffn_in['up_b'], 'L0_ffn_down_w': _L0_ffn_in['down_w'], 'L0_ffn_down_b': _L0_ffn_in['down_b']}

def reference(x, ctx_1024, mask_BxSxS2_if1, L0_attn_Wq, L0_attn_Wk, L0_attn_Wv, L0_attn_Wo, L0_attn_Wa, L0_attn_ba, L0_xattn_Wq, L0_xattn_bq, L0_xattn_Wk, L0_xattn_bk, L0_xattn_Wv, L0_xattn_bv, L0_xattn_Wo, L0_xattn_bo, L0_ffn_router_w, L0_ffn_gate_w, L0_ffn_gate_b, L0_ffn_up_w, L0_ffn_up_b, L0_ffn_down_w, L0_ffn_down_b):
    import jax
    import jax.numpy as jnp

    def _L0_attn_ref(x, Wq, Wk, Wv, Wo, Wa, ba):
        import jax, jax.numpy as jnp
        import numpy as np
        B, N, D = (2, 2048, 256)
        H, Dh = (16, 64)
        P = H * Dh
        EPS = 1e-06
        DECAY_BIAS_SHIFT = 2.0

        def _elu_plus_one(x):
            return jax.nn.elu(x) + 1.0

        def _ssd_scan(q, k, v, a, eps):
            qT = jnp.moveaxis(q, 2, 0)
            kT = jnp.moveaxis(k, 2, 0)
            vT = jnp.moveaxis(v, 2, 0)
            aT = jnp.moveaxis(a, 2, 0)
            Bb, Hh, _, Dk = q.shape
            Dv = v.shape[-1]
            S0 = jnp.zeros((Bb, Hh, Dk, Dv), q.dtype)
            z0 = jnp.zeros((Bb, Hh, Dk), q.dtype)

            def step(carry, inp):
                S, z = carry
                qt, kt, vt, at = inp
                S = at[..., None, None] * S + kt[..., :, None] * vt[..., None, :]
                z = at[..., None] * z + kt
                num = jnp.einsum('bhk,bhkv->bhv', qt, S)
                den = jnp.einsum('bhk,bhk->bh', qt, z) + eps
                return ((S, z), num / den[..., None])
            _, outT = jax.lax.scan(step, (S0, z0), (qT, kT, vT, aT))
            return jnp.moveaxis(outT, 0, 2)
        b, n, _ = x.shape
        q = (x @ Wq).reshape(b, n, H, Dh).transpose(0, 2, 1, 3)
        k = (x @ Wk).reshape(b, n, H, Dh).transpose(0, 2, 1, 3)
        v = (x @ Wv).reshape(b, n, H, Dh).transpose(0, 2, 1, 3)
        q = _elu_plus_one(q)
        k = _elu_plus_one(k)
        a = jax.nn.sigmoid(x @ Wa + ba + DECAY_BIAS_SHIFT)
        a = a.transpose(0, 2, 1)
        out = _ssd_scan(q, k, v, a, EPS)
        out = out.transpose(0, 2, 1, 3).reshape(b, n, P)
        return out @ Wo

    def _L0_xattn_ref(q, k, v, mask, Wq, bq, Wk, bk, Wv, bv, Wo, bo):
        import jax, jax.numpy as jnp
        import numpy as np
        B, S, D, H = (2, 512, 256, 16)
        DK = D // H

        def _split_heads(x):
            b, s, _ = x.shape
            return x.reshape(b, s, H, DK).transpose(0, 2, 1, 3)
        qh = _split_heads(q @ Wq.T + bq)
        kh = _split_heads(k @ Wk.T + bk)
        vh = _split_heads(v @ Wv.T + bv)
        scale = 1.0 / jnp.sqrt(jnp.float32(DK))
        scores = jnp.einsum('bhqd,bhkd->bhqk', qh, kh) * scale
        scores = jnp.where(mask[:, None, :, :] == 0, jnp.float32(-1000000000.0), scores)
        probs = jax.nn.softmax(scores, axis=-1)
        out = jnp.einsum('bhqk,bhkd->bhqd', probs, vh)
        concat = out.transpose(0, 2, 1, 3).reshape(q.shape[0], -1, D)
        return concat @ Wo.T + bo

    def _L0_ffn_ref(x, router_w, gate_w, gate_b, up_w, up_b, down_w, down_b):
        import jax, jax.numpy as jnp
        import numpy as np
        D_MODEL, D_FF, N_EXPERTS, TOP_K = (256, 512, 8, 2)
        B, S = (2, 512)
        b, s, d = x.shape
        xf = x.reshape(b * s, d)
        n = xf.shape[0]
        router_logits = xf @ router_w.T
        probs = jax.nn.softmax(router_logits, axis=-1)
        topv, topi = jax.lax.top_k(probs, TOP_K)
        mask = jnp.zeros_like(probs).at[jnp.arange(n)[:, None], topi].set(1.0)
        probs = probs * mask
        probs = probs / (probs.sum(axis=-1, keepdims=True) + 1e-09)
        g = jnp.einsum('nd,edf->nef', xf, gate_w) + gate_b
        u = jnp.einsum('nd,edf->nef', xf, up_w) + up_b
        h = jax.nn.silu(g) * u
        expert_out = jnp.einsum('nef,efd->ned', h, down_w) + down_b
        y = jnp.einsum('ne,ned->nd', probs, expert_out)
        return y.reshape(b, s, d)
    x = _layernorm(x + _L0_attn_ref(x, L0_attn_Wq, L0_attn_Wk, L0_attn_Wv, L0_attn_Wo, L0_attn_Wa, L0_attn_ba), axis=-1)
    x = _layernorm(x + _L0_xattn_ref(x, ctx_1024, ctx_1024, mask_BxSxS2_if1, L0_xattn_Wq, L0_xattn_bq, L0_xattn_Wk, L0_xattn_bk, L0_xattn_Wv, L0_xattn_bv, L0_xattn_Wo, L0_xattn_bo), axis=-1)
    x = _layernorm(x + _L0_ffn_ref(x, L0_ffn_router_w, L0_ffn_gate_w, L0_ffn_gate_b, L0_ffn_up_w, L0_ffn_up_b, L0_ffn_down_w, L0_ffn_down_b), axis=-1)
    return x

_drawn_inputs = setup_inputs


def setup_inputs(seed=0):
    import zlib

    import numpy as np

    out = dict(_drawn_inputs(seed))
    spreads = {'L0_attn_ba': (0.0, 0.1),
     'L0_xattn_bq': (0.0, 0.694),
     'L0_xattn_bk': (0.0, 0.8),
     'L0_xattn_bv': (0.0, 0.1),
     'L0_xattn_bo': (0.0, 0.1),
     'L0_ffn_gate_b': (0.0, 0.1),
     'L0_ffn_up_b': (0.0, 0.1),
     'L0_ffn_down_b': (0.0, 0.1)}
    factors = {'L0_xattn_Wq': 4.022, 'L0_xattn_Wk': 3.902}
    for name, (base, spread) in spreads.items():
        noise = np.random.default_rng([zlib.crc32(name.encode()), seed]).standard_normal(out[name].shape)
        drawn = base * np.exp(spread * noise) if base else spread * noise
        out[name] = jnp.asarray(drawn.astype(out[name].dtype))
    for name, factor in factors.items():
        out[name] = (out[name] * factor).astype(out[name].dtype)
    return out
```

```python
from contextlib import ExitStack

import concourse.bass as bass
from concourse import mybir

F32 = mybir.dt.float32
F32R = mybir.dt.float32r
BF16 = mybir.dt.bfloat16
I32 = mybir.dt.int32
U32 = mybir.dt.uint32
ALU = mybir.AluOpType
ACT = mybir.ActivationFunctionType
AX = mybir.AxisListType

P = 128
LN_EPS = 1e-5


class Shapes:

    def __init__(self, x, wq, ctx, gate_w):
        self.counted = []
        self.B, self.N, self.D = x.shape
        self.NB = self.N // P
        self.KC = self.D // P
        self.H = 16
        self.DH = wq.shape[1] // self.H
        self.PAIRS = self.H // 2
        self.S2 = ctx.shape[1]
        self.E, _, self.FF = gate_w.shape

    def semaphore(self, nc, name):
        self.counted.append(nc.alloc_semaphore(name))
        return self.counted[-1]

    def end_stage(self, nc):
        nc.clear_and_free_semaphores(self.counted)
        nc.all_engine_barrier()
        self.counted = []


def linear_attention(nc, sh, x, wq, wk, wv, wo, wa, ba, x1_dram, x_sorted):
    B, N, D, H, DH, NB, KC, PAIRS = sh.B, sh.N, sh.D, sh.H, sh.DH, sh.NB, sh.KC, sh.PAIRS
    PW = H * DH
    HALF = PW // 2
    HEADS_HALF = HALF // DH
    VU = 2 * NB
    CP = 3 * H
    TRI = N + P
    DECAY_SHIFT, EPS, Z_FLOOR = 2.0, 1e-6, -80.0
    with ExitStack() as ctx:
        def sb(name, shape, dt=F32):
            return ctx.enter_context(nc.sbuf_tensor(name, shape, dt))

        def ps(name, shape, dt=F32):
            return ctx.enter_context(nc.psum_tensor(name, shape, dt))

        def sem(name):
            return sh.semaphore(nc, name)

        w_raw = sb("a_w_raw", [P, KC, PW])
        w_hi = [sb(f"a_w_hi{n}", [P, KC, PW], F32R) for n in range(3)]
        w_lo = [sb(f"a_w_lo{n}", [P, KC, PW], F32R) for n in range(3)]
        wo_sb = sb("a_wo", [P, PAIRS, D])
        wa_raw = sb("a_wa_raw", [P, KC, H])
        wa_hi, wa_lo = sb("a_wa_hi", [P, KC, H], F32R), sb("a_wa_lo", [P, KC, H], F32R)
        ba_row, ba_shift = sb("a_ba_row", [1, H]), sb("a_ba_shift", [1, H])
        ident, ident_bf = sb("a_ident", [P, P]), sb("a_ident_bf", [P, P], BF16)
        ones, upto = sb("a_ones", [P, P]), sb("a_upto", [P, P])
        pick_head = sb("a_pick_head", [CP, H, P], BF16)
        x_in, x_res = sb("a_x_in", [P, NB, D]), sb("a_x_res", [P, NB, D])
        xT_hi, xT_lo = sb("a_xT_hi", [P, KC, N], F32R), sb("a_xT_lo", [P, KC, N], F32R)
        z_sb, z_exp, dec = sb("a_z", [P, NB, H]), sb("a_z_exp", [P, NB, H]), sb("a_dec", [P, NB, H])
        c_next, c_now = sb("a_c_next", [P, NB, H]), sb("a_c_now", [P, NB, H])
        c_rest = sb("a_c_rest", [P, NB, H])
        c_parts = sb("a_c_parts", [P, NB, 3, H], BF16)
        cT_next, cT_now = sb("a_cT_next", [CP, N], BF16), sb("a_cT_now", [CP, N], BF16)
        qk_exp = sb("a_qk_exp", [P, 2, N])
        qk = [sb(f"a_qk{g}", [P, 2, N]) for g in range(PAIRS)]
        v_aug = sb("a_v_aug", [P, NB, H, DH + 1])
        decay = [sb(f"a_decay{h}", [P, TRI]) for h in range(2)]
        probs = [sb(f"a_probs{h}", [P, TRI]) for h in range(2)]
        den, rden = sb("a_den", [P, NB, 2]), sb("a_rden", [P, NB, 2])
        o_norm, oT = sb("a_o_norm", [P, NB, 2, DH]), sb("a_oT", [P, NB * P])
        resid = sb("a_resid", [P, NB, D])
        stats, mv = sb("a_stats", [P, NB, 6]), sb("a_mv", [P, NB, 2])
        ln_var, rstd = sb("a_ln_var", [P, NB]), sb("a_rstd", [P, NB])
        eps_col = sb("a_eps_col", [P, 1])
        x1, zeros = sb("a_x1", [P, NB, D]), sb("a_zeros", [P, D])
        ps_mix = ps("a_ps_mix", [P, 512])
        ps_qk = ps("a_ps_qk", [P, 2, N])
        ps_c = ps("a_ps_c", [P, 2, N])
        ps_s = [ps(f"a_ps_s{h}", [P, 512]) for h in range(2)]
        ps_o = ps("a_ps_o", [P, 512])
        ps_t = ps("a_ps_t", [P, 512])
        ps_y = ps("a_ps_y", [P, NB, D])
        o_view = ps_o[:, 0:NB * 2 * (DH + 1)].rearrange("p (b h d) -> p b h d", b=NB, h=2)
        c_view = ps_mix[:, 0:NB * H].rearrange("p (b h) -> p b h", b=NB)
        cT_view = ps_mix[:, :].bitcast(BF16)

        consts_ready = sem("a_consts_ready")
        consts_step = sem("a_consts_step")
        raw_loaded = [sem(f"a_raw_loaded{n}") for n in range(3)]
        small_loaded = sem("a_small_loaded")
        w_hi_done, w_lo_done = sem("a_w_hi_done"), sem("a_w_lo_done")
        x_in_loaded, x_res_loaded, x1_stored = sem("a_x_in_loaded"), sem("a_x_res_loaded"), sem("a_x1_stored")
        rows_zeroed = sem("a_rows_zeroed")
        pool_turns, vec_turns, pe_turns = sem("a_pool_turns"), sem("a_vec_turns"), sem("a_pe_turns")
        xT_made, x_hi_done, x_lo_done = sem("a_xT_made"), sem("a_x_hi_done"), sem("a_x_lo_done")
        z_made, z_kept, z_exp_done, dec_done = sem("a_z_made"), sem("a_z_kept"), sem("a_z_exp_done"), sem("a_dec_done")
        c_made, c_step, c_split = sem("a_c_made"), sem("a_c_step"), sem("a_c_split")
        cT_made, cT_kept, c_switched = sem("a_cT_made"), sem("a_cT_kept"), sem("a_c_switched")
        qk_made, qk_exp_done, qk_exp_capped, qk_done = (
            sem("a_qk_made"), sem("a_qk_exp_done"), sem("a_qk_exp_capped"), sem("a_qk_done"))
        v_made, v_done = sem("a_v_made"), sem("a_v_done")
        c_spread, s_made = sem("a_c_spread"), sem("a_s_made")
        decay_exp = [sem(f"a_decay_exp{h}") for h in range(2)]
        decay_masked = [sem(f"a_decay_masked{h}") for h in range(2)]
        probs_done = [sem(f"a_probs_done{h}") for h in range(2)]
        o_made, den_step, o_normed = sem("a_o_made"), sem("a_den_step"), sem("a_o_normed")
        oT_made, oT_kept, y_added = sem("a_oT_made"), sem("a_oT_kept"), sem("a_y_added")
        resid_done, ln_step, var_ready, rstd_step, x1_ready = (
            sem("a_resid_done"), sem("a_ln_step"), sem("a_var_ready"), sem("a_rstd_step"), sem("a_x1_ready"))

        block = ctx.enter_context(nc.Block())
        x_rows = x.rearrange("b (k p) d -> b p k d", p=P)
        sorted_rows = x_sorted.rearrange("(p r) d -> p r d", p=P)
        cut = sorted_rows.shape[1] // 4
        zero_rows = [sorted_rows[:, n * cut:(n + 1) * cut, :] for n in range(4)]
        assert 4 * cut == sorted_rows.shape[1]
        x1_rows = x1_dram.rearrange("b (k p) d -> b p k d", p=P)

        @block.sync
        def _(sp):
            sp.dma_start(x_in[:], x_rows[0]).then_inc(x_in_loaded, 16)
            sp.dma_start(wa_raw[:], wa.rearrange("(k p) h -> p k h", p=P)).then_inc(small_loaded, 16)
            sp.dma_start(ba_row[:], ba.rearrange("(a h) -> a h", a=1)).then_inc(small_loaded, 16)
            for n, w in enumerate((wq, wk, wv)):
                if n:
                    sp.wait_ge(w_lo_done, n)
                sp.dma_start(w_raw[:], w.rearrange("(k p) n -> p k n", p=P)).then_inc(raw_loaded[n], 16)
            sp.dma_start(wo_sb[:], wo.rearrange("(g p) n -> p g n", p=P)).then_inc(small_loaded, 16)
            sp.wait_ge(consts_ready, 1)
            for rows in zero_rows:
                sp.dma_start(rows, zeros[:].unsqueeze(1).to_broadcast([P, rows.shape[1], D])).then_inc(rows_zeroed, 16)

            def load_x(b):
                sp.wait_ge(xT_made, b)
                sp.dma_start(x_in[:], x_rows[b]).then_inc(x_in_loaded, 16)

            def load_residual(b):
                sp.wait_ge(resid_done, b)
                sp.dma_start(x_res[:], x_rows[b]).then_inc(x_res_loaded, 16)

            def store_x1(b):
                sp.wait_ge(x1_ready, b + 1)
                sp.dma_start(x1_rows[b], x1[:]).then_inc(x1_stored, 16)

            def sequence(b):
                load_x(b + 2)
                load_residual(b)
                store_x1(b - 1)

            load_x(1)
            load_x(2)
            load_residual(0)
            with sp.Fori(1, B - 2) as b:
                sequence(b)
            for b in (B - 2, B - 1):
                load_residual(b)
                store_x1(b - 1)
            store_x1(B - 1)
            sp.wait_ge(x1_stored, 16 * B)
            sp.wait_ge(rows_zeroed, 16 * len(zero_rows))

        @block.gpsimd
        def _(pool):
            pool.memset(ident[:], 0.0).then_inc(consts_step, 1)
            pool.memset(ident_bf[:], 0.0).then_inc(consts_step, 1)
            pool.memset(ones[:], 1.0).then_inc(consts_step, 1)
            pool.memset(pick_head[:], 0.0).then_inc(consts_step, 1)
            pool.memset(v_aug[:], 1.0).then_inc(consts_step, 1)
            pool.memset(eps_col[:], LN_EPS).then_inc(consts_step, 1)
            pool.memset(zeros[:], 0.0).then_inc(consts_step, 1)
            pool.wait_ge(consts_step, 7)
            for m in (ident, ident_bf):
                pool.affine_select(out=m[:], in_=m[:], compare_op=ALU.not_equal, fill=1.0, base=0,
                                   pattern=[[-1, P]], channel_multiplier=1).then_inc(consts_step, 1)
            pool.affine_select(out=upto[:], in_=ones[:], compare_op=ALU.is_ge, fill=0.0, base=0,
                               pattern=[[1, P]], channel_multiplier=-1).then_inc(consts_step, 1)
            for part in range(3):
                if part:
                    pool.wait_ge(consts_step, 10 + part)
                pool.affine_select(out=pick_head[:], in_=pick_head[:], compare_op=ALU.not_equal, fill=1.0,
                                   base=-H * part, pattern=[[-1, H], [0, P]], channel_multiplier=1)\
                    .then_inc(consts_step, 1)
            pool.wait_ge(consts_step, 13)
            pool.memset(den[:], 1.0).then_inc(consts_ready, 1)

            def mask_decay(b, g):
                for h in range(2):
                    pool.wait_ge(decay_exp[h], b * PAIRS + g + 1)
                    pool.sem_inc(pool_turns, 1)
                    d = decay[h][:, :].rearrange("p (t i) -> p t i", i=P)[:, 0:3:2, :]
                    pool.affine_select(out=d, in_=d, compare_op=ALU.is_ge, fill=0.0, base=0,
                                       pattern=[[0, 2], [1, P]], channel_multiplier=-1)\
                        .then_inc(decay_masked[h], 1)

            def cap_exp(b, g):
                pool.wait_ge(qk_exp_done, b * PAIRS + g + 1)
                pool.sem_inc(pool_turns, 1)
                pool.tensor_scalar(qk_exp[:], qk_exp[:], 1.0, 0.0, ALU.min, ALU.max).then_inc(qk_exp_capped, 1)

            def sequence(b, last):
                for g in range(PAIRS):
                    mask_decay(b, g)
                    if not last:
                        cap_exp(b + 1, g)

            for g in range(PAIRS):
                cap_exp(0, g)
            sequence(0, False)
            with pool.Fori(1, B - 1) as b:
                sequence(b, False)
            sequence(B - 1, True)

        @block.scalar
        def _(act):
            for n in range(3):
                act.wait_ge(raw_loaded[n], 16)
                act.copy(w_hi[n][:], w_raw[:]).then_inc(w_hi_done, 1)
            act.wait_ge(small_loaded, 48)
            act.copy(wa_hi[:], wa_raw[:]).then_inc(w_hi_done, 1)
            act.wait_ge(consts_ready, 1)

            def x_hi(b):
                act.wait_ge(xT_made, b + 1)
                act.copy(xT_hi[:], ps_mix[:].rearrange("p (k n) -> p k n", k=KC)).then_inc(x_hi_done, 1)

            def exp_qk(b, g):
                act.wait_ge(qk_made, b * PAIRS + g + 1)
                act.wait_ge(qk_done, b * PAIRS + g)
                act.activation(qk_exp[:], ps_qk[:], ACT.Exp).then_inc(qk_exp_done, 1)

            def log_decay(b):
                act.wait_ge(z_kept, b + 1)
                act.activation(z_exp[:], z_sb[:], ACT.Exp, scale=-1.0).then_inc(z_exp_done, 1)
                act.wait_ge(z_exp_done, b + 1)
                act.activation(dec[:], z_exp[:], ACT.Ln, bias=1.0).then_inc(dec_done, 1)

            def keep_cT(b):
                act.wait_ge(cT_made, b + 1)
                act.wait_ge(c_switched, 2 * b)
                act.copy(cT_next[:], cT_view[0:CP, 0:N]).then_inc(cT_kept, 1)

            def keep_v(b, half, blk):
                act.wait_ge(v_made, b * VU + half * NB + blk + 1)
                act.wait_ge(o_made, (b - 1) * PAIRS + (half + 1) * PAIRS // 2) if not isinstance(b, int) or b else None
                act.copy(v_aug[:, blk, half * HEADS_HALF:(half + 1) * HEADS_HALF, 0:DH],
                         ps_mix[:].rearrange("p (h d) -> p h d", d=DH)).then_inc(v_done, 1)

            def switch_c(b):
                act.wait_ge(cT_kept, b + 1)
                act.wait_ge(c_split, b + 1)
                act.wait_ge(c_spread, b * PAIRS)
                act.wait_ge(decay_exp[1], b * PAIRS)
                act.copy(cT_now[:], cT_next[:]).then_inc(c_switched, 1)
                act.copy(c_now[:], c_next[:]).then_inc(c_switched, 1)
                act.wait_ge(c_switched, 2 * b + 2)

            def exp_decay(b, g):
                act.wait_ge(c_spread, b * PAIRS + g + 1)
                for h in range(2):
                    act.wait_ge(probs_done[h], b * PAIRS + g)
                    head = 2 * g + h
                    act.activation(decay[h][:, 0:N], ps_c[:, h, :], ACT.Exp,
                                   bias=c_now[:, 0, head:head + 1], scale=-1.0)
                    act.activation(decay[h][:, N:TRI], ps_c[:, h, P:N], ACT.Exp,
                                   bias=c_now[:, 1, head:head + 1], scale=-1.0).then_inc(decay_exp[h], 1)

            def keep_oT(b, g):
                act.wait_ge(oT_made, b * PAIRS + g + 1)
                act.wait_ge(y_added, b * PAIRS + g)
                act.copy(oT[:], ps_t[:, 0:NB * P]).then_inc(oT_kept, 1)

            def root(b):
                act.wait_ge(var_ready, b + 1)
                act.activation(ln_var[:], mv[:, :, 1], ACT.Ln, bias=eps_col[:]).then_inc(rstd_step, 1)
                act.wait_ge(rstd_step, 2 * b + 1)
                act.activation(rstd[:], ln_var[:], ACT.Exp, scale=-0.5).then_inc(rstd_step, 1)

            def sequence(b, first, last):
                switch_c(b)
                for g in range(PAIRS):
                    if g == 0 and not last:
                        x_hi(b + 1)
                    if g >= 2:
                        keep_oT(b, g - 2)
                    exp_decay(b, g)
                    if not last:
                        exp_qk(b + 1, g)
                        if g == 1:
                            log_decay(b + 1)
                    if g == 1 and not first:
                        root(b - 1)
                    if not last:
                        if g == 4:
                            keep_cT(b + 1)
                        if g in (5, 6):
                            keep_v(b + 1, 0, g - 5)
                keep_oT(b, PAIRS - 2)
                if not last:
                    for blk in range(NB):
                        keep_v(b + 1, 1, blk)
                keep_oT(b, PAIRS - 1)

            x_hi(0)
            for g in range(PAIRS):
                exp_qk(0, g)
            log_decay(0)
            keep_cT(0)
            for half in range(2):
                for blk in range(NB):
                    keep_v(0, half, blk)
            sequence(0, True, False)
            with act.Fori(1, B - 1) as b:
                sequence(b, False, False)
            sequence(B - 1, False, True)
            root(B - 1)

        @block.vector
        def _(vec):
            for n in range(3):
                vec.wait_ge(w_hi_done, n + 1)
                vec.tensor_tensor(w_lo[n][:], w_raw[:], w_hi[n][:].bitcast(F32), ALU.subtract).then_inc(w_lo_done, 1)
            vec.wait_ge(w_hi_done, 4)
            vec.tensor_tensor(wa_lo[:], wa_raw[:], wa_hi[:].bitcast(F32), ALU.subtract).then_inc(w_lo_done, 1)
            vec.tensor_scalar(ba_shift[:], ba_row[:], DECAY_SHIFT, None, ALU.add).then_inc(w_lo_done, 1)
            vec.wait_ge(consts_ready, 1)

            def x_lo(b):
                vec.wait_ge(x_hi_done, b + 1)
                vec.tensor_tensor(xT_lo[:], ps_mix[:].rearrange("p (k n) -> p k n", k=KC), xT_hi[:].bitcast(F32),
                                  ALU.subtract).then_inc(x_lo_done, 1)

            def keep_z(b):
                vec.wait_ge(z_made, b + 1)
                vec.tensor_scalar(z_sb[:], c_view, Z_FLOOR, None, ALU.max).then_inc(z_kept, 1)

            def split_c(b):
                vec.wait_ge(c_made, b + 1)
                vec.wait_ge(c_switched, 2 * b)
                vec.wait_ge(cT_made, b)
                vec.tensor_copy(c_next[:], c_view).then_inc(c_step, 1)
                vec.tensor_copy(c_parts[:, :, 0, :], c_view).then_inc(c_step, 1)
                vec.wait_ge(c_step, 4 * b + 2)
                vec.tensor_tensor(c_rest[:], c_next[:], c_parts[:, :, 0, :], ALU.subtract).then_inc(c_step, 1)
                vec.wait_ge(c_step, 4 * b + 3)
                vec.tensor_copy(c_parts[:, :, 1, :], c_rest[:]).then_inc(c_step, 1)
                vec.wait_ge(c_step, 4 * b + 4)
                vec.tensor_tensor(c_parts[:, :, 2, :], c_rest[:], c_parts[:, :, 1, :], ALU.subtract)\
                    .then_inc(c_split, 1)

            def finish_qk(b, g):
                vec.wait_ge(qk_exp_capped, b * PAIRS + g + 1)
                if not isinstance(b, int) or b:
                    vec.wait_ge(s_made, (b - 1) * PAIRS + g + 1)
                vec.scalar_tensor_tensor(qk[g][:], ps_qk[:], 0.0, qk_exp[:], ALU.max, ALU.add).then_inc(qk_done, 1)

            def weigh(b, g):
                vec.wait_ge(s_made, b * PAIRS + g + 1)
                vec.wait_ge(o_made, b * PAIRS + g)
                for h in range(2):
                    vec.wait_ge(decay_masked[h], b * PAIRS + g + 1)
                    vec.tensor_tensor(probs[h][:], ps_s[h][:, 0:TRI], decay[h][:], ALU.mult)\
                        .then_inc(probs_done[h], 1)

            def normalise(b, g):
                n = b * PAIRS + g
                vec.wait_ge(o_made, n + 1)
                vec.tensor_scalar(den[:], o_view[:, :, :, DH], EPS, None, ALU.add).then_inc(den_step, 1)
                vec.wait_ge(den_step, 2 * n + 1)
                vec.reciprocal(rden[:], den[:]).then_inc(den_step, 1)
                vec.wait_ge(den_step, 2 * n + 2)
                vec.wait_ge(oT_made, n)
                vec.tensor_tensor(o_norm[:], o_view[:, :, :, 0:DH],
                                  rden[:].unsqueeze(3).to_broadcast([P, NB, 2, DH]), ALU.mult).then_inc(o_normed, 1)

            def add_residual(b):
                vec.wait_ge(y_added, (b + 1) * PAIRS)
                vec.wait_ge(x_res_loaded, 16 * (b + 1))
                vec.tensor_tensor(resid[:], ps_y[:], x_res[:], ALU.add).then_inc(resid_done, 1)
                vec.wait_ge(resid_done, b + 1)
                for blk in range(NB):
                    vec.bn_stats(stats[:, blk, :], resid[:, blk, :]).then_inc(ln_step, 1)
                vec.wait_ge(ln_step, NB * b + NB)
                vec.sem_inc(vec_turns, 1)
                for blk in range(NB):
                    last = vec.bn_aggr(mv[:, blk, :], stats[:, blk, :])
                last.then_inc(var_ready, 1)

            def scale_x1(b):
                vec.wait_ge(rstd_step, 2 * b + 2)
                vec.wait_ge(x1_stored, 16 * b)
                for blk in range(NB):
                    last = vec.tensor_scalar(x1[:, blk, :], resid[:, blk, :], mv[:, blk, 0:1], rstd[:, blk:blk + 1],
                                             ALU.subtract, ALU.mult)
                last.then_inc(x1_ready, 1)

            def sequence(b, first, last):
                for g in range(PAIRS):
                    if g == 2 and not first:
                        scale_x1(b - 1)
                    if not last:
                        if g == 0:
                            x_lo(b + 1)
                        if g == 1:
                            keep_z(b + 1)
                        if g == 3:
                            split_c(b + 1)
                    weigh(b, g)
                    if g >= 1:
                        normalise(b, g - 1)
                    if not last:
                        finish_qk(b + 1, g)
                normalise(b, PAIRS - 1)
                add_residual(b)

            x_lo(0)
            for g in range(PAIRS):
                finish_qk(0, g)
            keep_z(0)
            split_c(0)
            sequence(0, True, False)
            with vec.Fori(1, B - 1) as b:
                sequence(b, False, False)
            sequence(B - 1, False, True)
            scale_x1(B - 1)

        @block.tensor
        def _(pe):
            pe.wait_ge(consts_ready, 1)

            def split_product(out, pairs):
                steps = [(lh, rh, ll, rl) for (lh, ll), (rh, rl) in pairs]
                todo = [p for lh, rh, ll, rl in steps for p in ((lh, rh), (lh, rl), (ll, rh))]
                for n, (l, r) in enumerate(todo):
                    mm = pe.matmul(out, l, r, start=(n == 0), stop=(n == len(todo) - 1))
                return mm

            def turn_x(b):
                pe.wait_ge(x_in_loaded, 16 * (b + 1))
                pe.wait_ge(v_done, VU * b)
                for k in range(KC):
                    for blk in range(NB):
                        mm = pe.transpose(ps_mix[:, k * N + blk * P:k * N + (blk + 1) * P],
                                          x_in[:, blk, k * P:(k + 1) * P], ident[:])
                mm.then_inc(xT_made, 1)

            def project_qk(b, g):
                pe.wait_ge(x_lo_done, b + 1)
                pe.wait_ge(qk_done, b * PAIRS + g)
                cols = slice(g * P, (g + 1) * P)
                for n in range(2):
                    mm = split_product(ps_qk[:, n, :], [
                        ((w_hi[n][:, k, cols], w_lo[n][:, k, cols]), (xT_hi[:, k, :], xT_lo[:, k, :]))
                        for k in range(KC)])
                mm.then_inc(qk_made, 1)

            def project_z(b):
                pe.wait_ge(x_lo_done, b + 1)
                for blk in range(NB):
                    rows = slice(blk * P, (blk + 1) * P)
                    todo = []
                    for k in range(KC):
                        todo += [(xT_hi[:, k, rows], wa_hi[:, k, :]), (xT_hi[:, k, rows], wa_lo[:, k, :]),
                                 (xT_lo[:, k, rows], wa_hi[:, k, :])]
                    for n, (l, r) in enumerate(todo):
                        pe.matmul(c_view[:, blk, :], l, r, start=(n == 0), stop=False)
                    mm = pe.matmul(c_view[:, blk, :], ones[0:1, :], ba_shift[:], start=False, stop=True)
                mm.then_inc(z_made, 1)

            def sum_decay(b):
                pe.wait_ge(dec_done, b + 1)
                pe.matmul(c_view[:, 0, :], upto[:], dec[:, 0, :], start=True, stop=True)
                for blk in range(1, NB):
                    for j in range(blk):
                        pe.matmul(c_view[:, blk, :], ones[:], dec[:, j, :], start=(j == 0), stop=False)
                    mm = pe.matmul(c_view[:, blk, :], upto[:], dec[:, blk, :], start=False, stop=True)
                mm.then_inc(c_made, 1)

            def turn_c(b):
                pe.wait_ge(c_split, b + 1)
                pe.sem_inc(pe_turns, 1)
                for blk in range(NB):
                    mm = pe.transpose(cT_view[0:CP, blk * P:(blk + 1) * P],
                                      c_parts[:, blk, :, :].rearrange("p t h -> p (t h)"), ident_bf[:])
                mm.then_inc(cT_made, 1)

            def project_v(b, half, blk):
                if (half, blk) == (0, 0):
                    pe.wait_ge(cT_kept, b + 1)
                pe.wait_ge(v_done, VU * b + half * NB + blk)
                rows, cols = slice(blk * P, (blk + 1) * P), slice(half * HALF, (half + 1) * HALF)
                split_product(ps_mix[:], [
                    ((xT_hi[:, k, rows], xT_lo[:, k, rows]), (w_hi[2][:, k, cols], w_lo[2][:, k, cols]))
                    for k in range(KC)]).then_inc(v_made, 1)

            def spread_c(b, g):
                pe.wait_ge(c_switched, 2 * b + 2)
                pe.wait_ge(decay_exp[1], b * PAIRS + g)
                for h in range(2):
                    mm = pe.matmul(ps_c[:, h, :], pick_head[:, 2 * g + h, :], cT_now[:], start=True, stop=True)
                mm.then_inc(c_spread, 1)

            def score(b, g):
                pe.wait_ge(qk_done, b * PAIRS + g + 1)
                for h in range(2):
                    pe.wait_ge(probs_done[h], b * PAIRS + g)
                    rows = slice(h * DH, (h + 1) * DH)
                    pe.matmul(ps_s[h][:, 0:N], qk[g][rows, 1, 0:P], qk[g][rows, 0, :], start=True, stop=True)
                    mm = pe.matmul(ps_s[h][:, N:TRI], qk[g][rows, 1, P:N], qk[g][rows, 0, P:N], start=True, stop=True)
                mm.then_inc(s_made, 1)

            def weighted_values(b, g):
                pe.wait_ge(v_done, VU * (b + 1))
                pe.wait_ge(o_normed, b * PAIRS + g)
                for h in range(2):
                    pe.wait_ge(probs_done[h], b * PAIRS + g + 1)
                    v = [v_aug[:, j, 2 * g + h, :] for j in range(NB)]
                    pe.matmul(o_view[:, 0, h, :], probs[h][:, 0:P], v[0], start=True, stop=True)
                    pe.matmul(o_view[:, 1, h, :], probs[h][:, P:N], v[0], start=True, stop=False)
                    mm = pe.matmul(o_view[:, 1, h, :], probs[h][:, N:TRI], v[1], start=False, stop=True)
                mm.then_inc(o_made, 1)

            def turn_o(b, g):
                pe.wait_ge(o_normed, b * PAIRS + g + 1)
                pe.wait_ge(oT_kept, b * PAIRS + g)
                for blk in range(NB):
                    mm = pe.transpose(ps_t[:, blk * P:(blk + 1) * P],
                                      o_norm[:, blk, :, :].rearrange("p h d -> p (h d)"), ident[:])
                mm.then_inc(oT_made, 1)

            def add_y(b, g):
                if g == 0:
                    pe.wait_ge(resid_done, b)
                pe.wait_ge(oT_kept, b * PAIRS + g + 1)
                for blk in range(NB):
                    mm = pe.matmul(ps_y[:, blk, :], oT[:, blk * P:(blk + 1) * P], wo_sb[:, g, :],
                                   start=(g == 0 and blk == 0), stop=(g == PAIRS - 1), skip_group_check=True)
                mm.then_inc(y_added, 1)

            def sequence(b, last):
                for g in range(PAIRS):
                    if g == 0 and not last:
                        turn_x(b + 1)
                    if g >= 2:
                        turn_o(b, g - 2)
                    spread_c(b, g)
                    score(b, g)
                    if g >= 1:
                        weighted_values(b, g - 1)
                    if g >= 2:
                        add_y(b, g - 2)
                    if not last:
                        project_qk(b + 1, g)
                        if g == 0:
                            project_z(b + 1)
                        if g == 2:
                            sum_decay(b + 1)
                        if g == 3:
                            turn_c(b + 1)
                        if g in (5, 6):
                            project_v(b + 1, 0, g - 5)
                        if g == PAIRS - 1:
                            project_v(b + 1, 1, 0)
                turn_o(b, PAIRS - 2)
                weighted_values(b, PAIRS - 1)
                add_y(b, PAIRS - 2)
                if not last:
                    project_v(b + 1, 1, 1)
                turn_o(b, PAIRS - 1)
                add_y(b, PAIRS - 1)

            pe.wait_ge(w_lo_done, 5)
            pe.wait_ge(small_loaded, 48)
            turn_x(0)
            for g in range(PAIRS):
                project_qk(0, g)
            project_z(0)
            sum_decay(0)
            turn_c(0)
            for half in range(2):
                for blk in range(NB):
                    project_v(0, half, blk)
            sequence(0, False)
            with pe.Fori(1, B - 1) as b:
                sequence(b, False)
            sequence(B - 1, True)


def cross_attention(nc, sh, x1_dram, ctx_in, mask, wq, bq, wk, bk, wv, bv, wo, bo, router_w, x2_all, logits):
    B, N, D, H, NB, KC, S2 = sh.B, sh.N, sh.D, sh.H, sh.NB, sh.KC, sh.S2
    DK = D // H
    SLOT = 32
    PER = P // SLOT
    TILES = H // PER
    SCALE = float(DK) ** -0.5
    MASKED, OPEN = -1.0e9, 3.0e38
    with ExitStack() as ctx:
        def sb(name, shape, dt=F32):
            return ctx.enter_context(nc.sbuf_tensor(name, shape, dt))

        def ps(name, shape, dt=F32):
            return ctx.enter_context(nc.psum_tensor(name, shape, dt))

        def sem(name):
            return sh.semaphore(nc, name)

        ident = sb("b_ident", [P, P])
        w_raw = [sb(f"b_w_raw{n}", [P, KC, D]) for n in range(4)]
        wqT, wkT = sb("b_wqT", [P, KC, H, SLOT]), sb("b_wkT", [P, KC, H, SLOT])
        wvT, woT = sb("b_wvT", [P, KC, D]), sb("b_woT", [P, KC, D])
        bq_col, bk_col = sb("b_bq_col", [P, TILES]), sb("b_bk_col", [P, TILES])
        bv_rows, bo_rows = sb("b_bv_rows", [P, D]), sb("b_bo_rows", [P, D])
        eps_col = sb("b_eps_col", [P, 1])
        x_in, x_res, x_bo = sb("b_x_in", [P, NB, D]), sb("b_x_res", [P, NB, D]), sb("b_x_bo", [P, NB, D])
        ctx_rows, ctxT = sb("b_ctx_rows", [P, D]), sb("b_ctxT", [P, KC, S2])
        mask_in, mask_cap = sb("b_mask_in", [P, NB, S2], I32), sb("b_mask_cap", [P, NB, S2])
        xT = sb("b_xT", [P, KC, N])
        qT, kT, v = sb("b_qT", [P, TILES, N]), sb("b_kT", [P, TILES, S2]), sb("b_v", [P, D])
        probs = [sb(f"b_probs{n}", [P, PER, TILES, S2]) for n in range(NB)]
        top = [sb(f"b_top{n}", [P, H]) for n in range(NB)]
        den = [sb(f"b_den{n}", [P, H]) for n in range(NB)]
        rden = [sb(f"b_rden{n}", [P, H]) for n in range(NB)]
        pT = [sb(f"b_pT{n}", [P, TILES, P]) for n in range(2)]
        o_norm = [sb(f"b_o_norm{n}", [P, D]) for n in range(NB)]
        oT = [sb(f"b_oT{n}", [P, KC, P]) for n in range(NB)]
        resid = sb("b_resid", [P, NB, D])
        stats, mv = sb("b_stats", [P, NB, 6]), sb("b_mv", [P, NB, 2])
        ln_var, rstd = sb("b_ln_var", [P, NB]), sb("b_rstd", [P, NB])
        x2, x2T = sb("b_x2", [P, NB, D]), sb("b_x2T", [P, KC, N])
        rw_rows, rwT = sb("b_rw_rows", [sh.E, D]), sb("b_rwT", [P, KC, sh.E])

        ps_s = ps("b_ps_s", [P, PER, 512])
        ps_p = [ps(f"b_ps_p{n}", [P, 512]) for n in range(2)]
        ps_t = ps("b_ps_t", [P, TILES, P])
        ps_o = ps("b_ps_o", [P, 512])

        loaded, consts_step, consts_ready = sem("b_loaded"), sem("b_consts_step"), sem("b_consts_ready")
        w_turned, w_kept = sem("b_w_turned"), sem("b_w_kept")
        x_in_loaded, x_res_loaded = sem("b_x_in_loaded"), sem("b_x_res_loaded")
        ctx_loaded, mask_loaded, x2_stored = sem("b_ctx_loaded"), sem("b_mask_loaded"), sem("b_x2_stored")
        UNITS = ("x2T", "lg", "xT", "cT", "q0", "q1", "k", "v", "oT0", "oT1", "y0", "y1")
        made = {u: sem(f"b_made_{u}") for u in UNITS}
        kept = {u: sem(f"b_kept_{u}") for u in UNITS}
        bank = {u: ps_p[n % 2] for n, u in enumerate(UNITS)}
        vec_turns, pe_turns = sem("b_vec_turns"), sem("b_pe_turns")
        cap_step, cap_ready = sem("b_cap_step"), sem("b_cap_ready")
        s_made, s_kept = sem("b_s_made"), sem("b_s_kept")
        top_done, shifted, exp_done, den_done, rden_done = (
            sem("b_top_done"), sem("b_shifted"), sem("b_exp_done"), sem("b_den_done"), sem("b_rden_done"))
        pT_made, pT_kept, pT_used = sem("b_pT_made"), sem("b_pT_kept"), sem("b_pT_used")
        o_normed = sem("b_o_normed")
        x_bo_done, ln_step, var_ready, rstd_step, x2_ready = (
            sem("b_x_bo_done"), sem("b_ln_step"), sem("b_var_ready"), sem("b_rstd_step"), sem("b_x2_ready"))

        block = ctx.enter_context(nc.Block())
        x1_rows = x1_dram.rearrange("b (k p) d -> b p k d", p=P)
        mask_rows = mask.rearrange("b (k p) s -> b p k s", p=P)
        N_LOADS = 5 + 2 * PER + 2

        @block.sync
        def _(sp):
            sp.dma_start(x_in[:], x1_rows[0]).then_inc(x_in_loaded, 16)
            sp.dma_start(ctx_rows[0:S2, :], ctx_in[0]).then_inc(ctx_loaded, 16)
            for n, w in enumerate((wq, wk, wv, wo)):
                sp.dma_start(w_raw[n][:], w.rearrange("(k p) n -> p k n", p=P)).then_inc(loaded, 16)
            sp.dma_start(rw_rows[:], router_w).then_inc(loaded, 16)
            sp.wait_ge(consts_ready, 1)
            for col, b_in in ((bq_col, bq), (bk_col, bk)):
                for s in range(PER):
                    sp.dma_start(col[s * SLOT:s * SLOT + DK, :],
                                 b_in.rearrange("(t s d) -> s d t", s=PER, d=DK)[s], allow_slow_non_contiguous=True)\
                        .then_inc(loaded, 16)
            for rows, b_in in ((bv_rows, bv), (bo_rows, bo)):
                sp.dma_start(rows[:], b_in.rearrange("(a n) -> a n", a=1).to_broadcast([P, D])).then_inc(loaded, 16)

            def sequence(b, last):
                sp.wait_ge(cap_ready, b)
                sp.dma_start(mask_in[:], mask_rows[b]).then_inc(mask_loaded, 16)
                sp.wait_ge(x_bo_done, b)
                sp.dma_start(x_res[:], x1_rows[b]).then_inc(x_res_loaded, 16)
                if not last:
                    sp.wait_ge(made["xT"], b + 1)
                    sp.dma_start(x_in[:], x1_rows[b + 1]).then_inc(x_in_loaded, 16)
                    sp.wait_ge(made["cT"], b + 1)
                    sp.dma_start(ctx_rows[0:S2, :], ctx_in[b + 1]).then_inc(ctx_loaded, 16)
                sp.wait_ge(x2_ready, b + 1)
                sp.dma_start(x2_all[:, bass.ts(b, NB), :], x2[:]).then_inc(x2_stored, 16)

            sequence(0, False)
            with sp.Fori(1, B - 1) as b:
                sequence(b, False)
            sequence(B - 1, True)
            sp.wait_ge(x2_stored, 16 * B)

        @block.gpsimd
        def _(pool):
            pool.memset(ident[:], 0.0).then_inc(consts_step, 1)
            pool.wait_ge(consts_step, 1)
            pool.affine_select(out=ident[:], in_=ident[:], compare_op=ALU.not_equal, fill=1.0, base=0,
                               pattern=[[-1, P]], channel_multiplier=1).then_inc(consts_step, 1)
            for m in (wqT, wkT, bq_col, bk_col):
                pool.memset(m[:], 0.0).then_inc(consts_step, 1)
            pool.memset(eps_col[:], LN_EPS).then_inc(consts_step, 1)
            pool.wait_ge(consts_step, 7)
            pool.memset(x_bo[:], 0.0).then_inc(consts_ready, 1)
            pool.wait_ge(loaded, 16 * N_LOADS)
            pool.wait_ge(consts_ready, 1)

            def sequence(b):
                pool.wait_ge(x_res_loaded, 16 * (b + 1))
                pool.wait_ge(kept["y1"], b)
                pool.tensor_tensor(x_bo[:], x_res[:], bo_rows[:].unsqueeze(1).to_broadcast([P, NB, D]), ALU.add)\
                    .then_inc(x_bo_done, 1)
                for blk in range(NB):
                    pool.wait_ge(top_done, b * NB + blk + 1)
                    p = probs[blk][:].rearrange("p s t k -> p (s t) k")
                    pool.tensor_tensor(p, p, top[blk][:].unsqueeze(2).to_broadcast([P, H, S2]), ALU.subtract)\
                        .then_inc(shifted, 1)

            sequence(0)
            with pool.Fori(1, B) as b:
                sequence(b)

        @block.scalar
        def _(act):
            act.wait_ge(loaded, 16 * N_LOADS)
            act.wait_ge(consts_ready, 1)
            for n, wT in enumerate((wqT, wkT, wvT, woT)):
                for k in range(KC):
                    act.wait_ge(w_turned, n * KC + k + 1)
                    src = ps_p[k][:, 0:D]
                    if n < 2:
                        act.copy(wT[:, k, :, 0:DK], src.rearrange("p (h d) -> p h d", d=DK)).then_inc(w_kept, 1)
                    else:
                        act.copy(wT[:, k, :], src).then_inc(w_kept, 1)

            act.wait_ge(w_turned, 4 * KC + 1)
            act.copy(rwT[:], ps_t[:, 0, 0:KC * sh.E].rearrange("p (k e) -> p k e", k=KC)).then_inc(w_kept, 1)

            def keep_x2T(b):
                act.wait_ge(made["x2T"], b + 1)
                act.copy(x2T[:], bank["x2T"][:].rearrange("p (k n) -> p k n", k=KC)).then_inc(kept["x2T"], 1)

            def keep_inputs(b):
                act.wait_ge(made["xT"], b + 1)
                act.copy(xT[:], bank["xT"][:].rearrange("p (k n) -> p k n", k=KC)).then_inc(kept["xT"], 1)
                act.wait_ge(made["cT"], b + 1)
                act.copy(ctxT[:], bank["cT"][:, 0:KC * S2].rearrange("p (k n) -> p k n", k=KC)).then_inc(kept["cT"], 1)

            def keep_qk(b):
                for n, u in enumerate(("q0", "q1")):
                    act.wait_ge(made[u], b + 1)
                    half = bank[u][:].rearrange("p (t n) -> p t n", t=TILES // 2)
                    for j in range(TILES // 2):
                        t = n * TILES // 2 + j
                        ins = act.activation(qT[:, t, :], half[:, j, :], ACT.Identity, bias=bq_col[:, t:t + 1])
                    ins.then_inc(kept[u], 1)
                act.wait_ge(made["k"], b + 1)
                for t in range(TILES):
                    ins = act.activation(kT[:, t, :], bank["k"][:, t * S2:(t + 1) * S2], ACT.Identity,
                                         bias=bk_col[:, t:t + 1])
                ins.then_inc(kept["k"], 1)

            def exponentials(b, blk):
                act.wait_ge(shifted, b * NB + blk + 1)
                act.activation(probs[blk][:], probs[blk][:], ACT.Exp).then_inc(exp_done, 1)

            def keep_pT(b, blk):
                for g in range(TILES):
                    n = (b * NB + blk) * TILES + g
                    act.wait_ge(pT_made, n + 1)
                    if not isinstance(n, int) or n >= 2:
                        act.wait_ge(pT_used, n - 1)
                    act.copy(pT[g % 2][0:S2, :, :], ps_t[0:S2, :, :]).then_inc(pT_kept, 1)

            def keep_oT(b, blk):
                u = f"oT{blk}"
                act.wait_ge(made[u], b + 1)
                act.copy(oT[blk][:], bank[u][:, 0:KC * P].rearrange("p (k n) -> p k n", k=KC)).then_inc(kept[u], 1)

            def root(b):
                act.wait_ge(var_ready, b + 1)
                act.activation(ln_var[:], mv[:, :, 1], ACT.Ln, bias=eps_col[:]).then_inc(rstd_step, 1)
                act.wait_ge(rstd_step, 2 * b + 1)
                act.activation(rstd[:], ln_var[:], ACT.Exp, scale=-0.5).then_inc(rstd_step, 1)

            def sequence(b, first, last):
                if not first:
                    keep_x2T(b - 1)
                if not last:
                    keep_inputs(b + 1)
                exponentials(b, 0)
                if not last:
                    act.wait_ge(s_made, NB * (b + 1))
                    keep_qk(b + 1)
                exponentials(b, 1)
                for blk in range(NB):
                    keep_pT(b, blk)
                for blk in range(NB):
                    keep_oT(b, blk)
                root(b)

            keep_inputs(0)
            keep_qk(0)
            sequence(0, True, False)
            with act.Fori(1, B - 1) as b:
                sequence(b, False, False)
            sequence(B - 1, False, True)
            keep_x2T(B - 1)

        @block.vector
        def _(vec):
            vec.wait_ge(loaded, 16 * N_LOADS)
            vec.wait_ge(consts_ready, 1)

            def keep_v(b):
                vec.wait_ge(made["v"], b + 1)
                vec.tensor_tensor(v[0:S2, :], bank["v"][0:S2, 0:D], bv_rows[0:S2, :], ALU.add).then_inc(kept["v"], 1)

            def mask_caps(b):
                vec.wait_ge(mask_loaded, 16 * (b + 1))
                vec.tensor_scalar(mask_cap[:], mask_in[:], 0.0, OPEN, ALU.not_equal, ALU.mult).then_inc(cap_step, 1)
                vec.wait_ge(cap_step, b + 1)
                vec.tensor_scalar(mask_cap[:], mask_cap[:], MASKED, None, ALU.add).then_inc(cap_ready, 1)
                vec.wait_ge(cap_ready, b + 1)

            def keep_scores(b, blk):
                n = b * NB + blk
                vec.wait_ge(s_made, n + 1)
                vec.wait_ge(pT_made, (b * NB + blk) * TILES if blk == 0 else b * NB * TILES)
                for s in range(PER):
                    ins = vec.scalar_tensor_tensor(
                        probs[blk][:, s, :, :], ps_s[:, s, 0:TILES * S2].rearrange("p (t k) -> p t k", t=TILES),
                        SCALE, mask_cap[:, blk, :].unsqueeze(1).to_broadcast([P, TILES, S2]), ALU.mult, ALU.min)
                ins.then_inc(s_kept, 1)
                vec.wait_ge(s_kept, n + 1)
                vec.tensor_reduce(top[blk][:], probs[blk][:].rearrange("p s t k -> p (s t) k"), AX.X, ALU.max)\
                    .then_inc(top_done, 1)

            def sums(b, blk):
                n = b * NB + blk
                vec.wait_ge(exp_done, n + 1)
                vec.tensor_reduce(den[blk][:], probs[blk][:].rearrange("p s t k -> p (s t) k"), AX.X, ALU.add)\
                    .then_inc(den_done, 1)
                vec.wait_ge(den_done, n + 1)
                vec.reciprocal(rden[blk][:], den[blk][:]).then_inc(rden_done, 1)

            def normalise(b, blk):
                n = b * NB + blk
                vec.wait_ge(pT_used, (n + 1) * TILES)
                vec.wait_ge(rden_done, n + 1)
                vec.wait_ge(made[f"oT{blk}"], b)
                vec.tensor_tensor(o_norm[blk][:].rearrange("p (t s d) -> p t s d", s=PER, d=DK),
                                  ps_o[:, 0:D].rearrange("p (t s d) -> p t s d", s=PER, d=DK),
                                  rden[blk][:].rearrange("p (s t) -> p t s", s=PER).unsqueeze(3)
                                  .to_broadcast([P, TILES, PER, DK]), ALU.mult).then_inc(o_normed, 1)

            def keep_logits(b):
                vec.wait_ge(made["lg"], b + 1)
                vec.tensor_copy(logits[:, bass.ts(b, NB), :],
                                bank["lg"][:, 0:NB * sh.E].rearrange("p (n e) -> p n e", n=NB)).then_inc(kept["lg"], 1)

            def layernorm(b):
                vec.wait_ge(x_bo_done, b + 1)
                for blk in range(NB):
                    u = f"y{blk}"
                    vec.wait_ge(made[u], b + 1)
                    vec.tensor_tensor(resid[:, blk, :], bank[u][:, 0:D], x_bo[:, blk, :], ALU.add).then_inc(kept[u], 1)
                vec.wait_ge(kept["y1"], b + 1)
                for blk in range(NB):
                    vec.bn_stats(stats[:, blk, :], resid[:, blk, :]).then_inc(ln_step, 1)
                vec.wait_ge(ln_step, NB * b + NB)
                vec.sem_inc(vec_turns, 1)
                for blk in range(NB):
                    ins = vec.bn_aggr(mv[:, blk, :], stats[:, blk, :])
                ins.then_inc(var_ready, 1)
                vec.wait_ge(rstd_step, 2 * b + 2)
                vec.wait_ge(x2_stored, 16 * b)
                vec.wait_ge(made["x2T"], b)
                for blk in range(NB):
                    ins = vec.tensor_scalar(x2[:, blk, :], resid[:, blk, :], mv[:, blk, 0:1], rstd[:, blk:blk + 1],
                                            ALU.subtract, ALU.mult)
                ins.then_inc(x2_ready, 1)

            def sequence(b, first, last):
                mask_caps(b)
                for blk in range(NB):
                    keep_scores(b, blk)
                if not first:
                    keep_logits(b - 1)
                for blk in range(NB):
                    sums(b, blk)
                for blk in range(NB):
                    normalise(b, blk)
                if not last:
                    keep_v(b + 1)
                layernorm(b)

            keep_v(0)
            sequence(0, True, False)
            with vec.Fori(1, B - 1) as b:
                sequence(b, False, False)
            sequence(B - 1, False, True)
            keep_logits(B - 1)

        @block.tensor
        def _(pe):
            pe.wait_ge(loaded, 16 * N_LOADS)
            pe.wait_ge(consts_ready, 1)
            for n in range(4):
                for k in range(KC):
                    if n:
                        pe.wait_ge(w_kept, (n - 1) * KC + k + 1)
                    for o in range(KC):
                        mm = pe.transpose(ps_p[k][:, o * P:(o + 1) * P], w_raw[n][:, o, k * P:(k + 1) * P], ident[:])
                    mm.then_inc(w_turned, 1)
            for k in range(KC):
                mm = pe.transpose(ps_t[:, 0, k * sh.E:(k + 1) * sh.E], rw_rows[:, k * P:(k + 1) * P],
                                  ident[0:sh.E, 0:sh.E])
            mm.then_inc(w_turned, 1)
            pe.wait_ge(w_kept, 4 * KC + 1)

            def route(b):
                pe.wait_ge(x2_ready, b + 1)
                pe.wait_ge(kept["y0"], b + 1)
                for k in range(KC):
                    for blk in range(NB):
                        mm = pe.transpose(bank["x2T"][:, k * N + blk * P:k * N + (blk + 1) * P],
                                          x2[:, blk, k * P:(k + 1) * P], ident[:])
                mm.then_inc(made["x2T"], 1)
                pe.wait_ge(kept["x2T"], b + 1)
                pe.wait_ge(kept["y1"], b + 1)
                for blk in range(NB):
                    for k in range(KC):
                        mm = pe.matmul(bank["lg"][:, blk * sh.E:(blk + 1) * sh.E], x2T[:, k, blk * P:(blk + 1) * P],
                                       rwT[:, k, :], start=(k == 0), stop=(k == KC - 1))
                mm.then_inc(made["lg"], 1)

            def inputs(b):
                pe.wait_ge(x_in_loaded, 16 * (b + 1))
                if not isinstance(b, int) or b >= 2:
                    pe.wait_ge(kept["x2T"], b - 1)
                for k in range(KC):
                    for blk in range(NB):
                        mm = pe.transpose(bank["xT"][:, k * N + blk * P:k * N + (blk + 1) * P],
                                          x_in[:, blk, k * P:(k + 1) * P], ident[:])
                mm.then_inc(made["xT"], 1)
                pe.wait_ge(ctx_loaded, 16 * (b + 1))
                if not isinstance(b, int) or b >= 2:
                    pe.wait_ge(kept["lg"], b - 1)
                for k in range(KC):
                    pe.sem_inc(pe_turns, 1)
                    mm = pe.transpose(bank["cT"][:, k * S2:(k + 1) * S2],
                                      ctx_rows[0:S2, k * P:(k + 1) * P], ident[0:S2, 0:S2])
                mm.then_inc(made["cT"], 1)

            def project_qk(b):
                for n, (u, before) in enumerate((("q0", "xT"), ("q1", "cT"))):
                    pe.wait_ge(kept["xT"], b + 1)
                    pe.wait_ge(kept[before], b + 1)
                    for j in range(TILES // 2):
                        t = n * TILES // 2 + j
                        for k in range(KC):
                            mm = pe.matmul(bank[u][:, j * N:(j + 1) * N],
                                           wqT[:, k, t * PER:(t + 1) * PER, :].rearrange("p h d -> p (h d)"),
                                           xT[:, k, :], start=(k == 0), stop=(k == KC - 1))
                    mm.then_inc(made[u], 1)
                pe.wait_ge(kept["cT"], b + 1)
                pe.wait_ge(kept["q0"], b + 1)
                for t in range(TILES):
                    for k in range(KC):
                        mm = pe.matmul(bank["k"][:, t * S2:(t + 1) * S2],
                                       wkT[:, k, t * PER:(t + 1) * PER, :].rearrange("p h d -> p (h d)"),
                                       ctxT[:, k, :], start=(k == 0), stop=(k == KC - 1))
                mm.then_inc(made["k"], 1)

            def project_v(b):
                pe.wait_ge(kept["cT"], b + 1)
                pe.wait_ge(kept["q1"], b + 1)
                for k in range(KC):
                    mm = pe.matmul(bank["v"][0:S2, 0:D], ctxT[:, k, :], wvT[:, k, :], start=(k == 0), stop=(k == KC - 1))
                mm.then_inc(made["v"], 1)

            def score(b, blk):
                if blk == 0:
                    pe.wait_ge(kept["k"], b + 1)
                    pe.wait_ge(kept["q1"], b + 1)
                pe.wait_ge(s_kept, b * NB + blk)
                for t in range(TILES):
                    for s in range(PER):
                        rows = slice(s * SLOT, s * SLOT + DK)
                        mm = pe.matmul(ps_s[:, s, t * S2:(t + 1) * S2], qT[rows, t, blk * P:(blk + 1) * P],
                                       kT[rows, t, :], start=True, stop=True)
                mm.then_inc(s_made, 1)

            def weighted_values(b, blk):
                pe.wait_ge(kept["v"], b + 1)
                pe.wait_ge(o_normed, b * NB + blk)
                n0 = (b * NB + blk) * TILES

                def values(g):
                    pe.wait_ge(pT_kept, n0 + g + 1)
                    for s in range(PER):
                        h = g * PER + s
                        mm = pe.matmul(ps_o[:, h * DK:(h + 1) * DK], pT[g % 2][0:S2, s, :],
                                       v[0:S2, h * DK:(h + 1) * DK], start=True, stop=True)
                    mm.then_inc(pT_used, 1)
                    return mm

                pe.wait_ge(exp_done, b * NB + blk + 1)
                for g in range(TILES):
                    pe.wait_ge(pT_kept, n0 + g)
                    for s in range(PER):
                        mm = pe.transpose(ps_t[0:S2, s, :], probs[blk][:, s, g, :], ident[:])
                    mm.then_inc(pT_made, 1)
                    if g:
                        values(g - 1)
                values(TILES - 1)

            def outputs(b, last):
                for blk in range(NB):
                    u = f"oT{blk}"
                    pe.wait_ge(o_normed, b * NB + blk + 1)
                    if last:
                        pe.wait_ge(kept[("x2T", "lg")[blk]], b)
                    else:
                        pe.wait_ge(kept["k" if blk == 0 else "v"], b + 2)
                    for k in range(KC):
                        mm = pe.transpose(bank[u][:, k * P:(k + 1) * P], o_norm[blk][:, k * P:(k + 1) * P], ident[:])
                    mm.then_inc(made[u], 1)
                for blk in range(NB):
                    u = f"y{blk}"
                    pe.wait_ge(kept[f"oT{blk}"], b + 1)
                    for k in range(KC):
                        mm = pe.matmul(bank[u][:, 0:D], oT[blk][:, k, :], woT[:, k, :], start=(k == 0), stop=(k == KC - 1))
                    mm.then_inc(made[u], 1)

            def sequence(b, first, last):
                for blk in range(NB):
                    score(b, blk)
                if not first:
                    route(b - 1)
                if not last:
                    inputs(b + 1)
                    project_qk(b + 1)
                for blk in range(NB):
                    weighted_values(b, blk)
                if not last:
                    project_v(b + 1)
                outputs(b, last)

            inputs(0)
            project_qk(0)
            project_v(0)
            sequence(0, True, False)
            with pe.Fori(1, B - 1) as b:
                sequence(b, False, False)
            sequence(B - 1, False, True)
            route(B - 1)


class Plan:

    def __init__(self, sh):
        self.T = 512
        self.SHIFT = self.T.bit_length() - 1
        self.TOKENS = sh.B * sh.N
        self.BLOCKS = self.TOKENS // P
        self.TILES = (2 * self.TOKENS - sh.E) // self.T + sh.E
        self.ROWS = self.TILES * self.T


def route_tokens(nc, sh, plan, logits, x2_all, x_sorted, slots, gates, tile_table):
    E, D = sh.E, sh.D
    NBK, T, TILES = plan.BLOCKS, plan.T, plan.TILES
    with ExitStack() as ctx:
        def sb(name, shape, dt=F32):
            return ctx.enter_context(nc.sbuf_tensor(name, shape, dt))

        def sem(name):
            return sh.semaphore(nc, name)

        shifted, probs, rest = sb("r_shifted", [P, NBK, E]), sb("r_probs", [P, NBK, E]), sb("r_rest", [P, NBK, E])
        same, key = sb("r_same", [P, NBK, E]), sb("r_key", [P, NBK, E])
        picked = [sb(f"r_picked{k}", [P, NBK, E]) for k in range(2)]
        both = sb("r_both", [P, NBK, E])
        top, tot = [sb(f"r_top{k}", [P, NBK]) for k in range(2)], sb("r_tot", [P, NBK])
        col, rcol = sb("r_col", [P, NBK]), sb("r_rcol", [P, NBK])
        order = sb("r_order", [P, E])
        order_i = sb("r_order_i", [P, E], I32)
        first_row = sb("r_first_row", [P, E])
        tile_no, tile_no_i = sb("r_tile_no", [P, TILES]), sb("r_tile_no_i", [P, TILES], I32)
        before, ones = sb("r_before", [P, P]), sb("r_ones", [P, P])
        sums = [sb(f"r_sums{k}", [P, NBK, E]) for k in range(2)]
        in_block, rank = sb("r_in_block", [P, NBK, E]), sb("r_rank", [P, NBK, E])
        slot_f = sb("r_slot_f", [P, NBK])
        tiles_i, n_tiles = sb("r_tiles_i", [P, E], I32), sb("r_n_tiles", [P, E])
        ends = [sb(f"r_ends{k}", [P, E]) for k in range(2)]
        expert_of = sb("r_expert_of", [P, TILES])
        ps_rank = ctx.enter_context(nc.psum_tensor("r_ps_rank", [P, 2, NBK * E], F32))

        consts_step, consts_ready, step = sem("r_consts_step"), sem("r_consts_ready"), sem("r_step")
        shifted_done, exp_done, picks_ready, ranked = (
            sem("r_shifted_done"), sem("r_exp_done"), sem("r_picks_ready"), sem("r_ranked"))
        slots_ready, scattered = sem("r_slots_ready"), sem("r_scattered")

        block = ctx.enter_context(nc.Block())

        @block.gpsimd
        def _(pool):
            pool.iota(order_i[:], pattern=[[-1, E]], base=E, channel_multiplier=0).then_inc(consts_step, 1)
            pool.iota(tile_no_i[:], pattern=[[1, TILES]], base=0, channel_multiplier=0).then_inc(consts_step, 1)
            pool.memset(ones[:], 1.0).then_inc(consts_step, 1)
            pool.wait_ge(consts_step, 3)
            pool.affine_select(out=before[:], in_=ones[:], compare_op=ALU.is_gt, fill=0.0, base=0,
                               pattern=[[1, P]], channel_multiplier=-1).then_inc(consts_ready, 1)
            pool.wait_ge(slots_ready, 2)
            for n in range(NBK):
                for k in range(2):
                    pool.indirect_dma_start(x_sorted, bass.IndirectOffsetOnAxis(slots[k][:, n:n + 1], 0),
                                            x2_all[:, n, :], None).then_inc(scattered, 16)
            pool.wait_ge(scattered, 16 * 2 * NBK)

        @block.scalar
        def _(act):
            act.wait_ge(shifted_done, 1)
            act.activation(probs[:], shifted[:], ACT.Exp).then_inc(exp_done, 1)

        @block.tensor
        def _(pe):
            pe.wait_ge(picks_ready, 1)
            pe.wait_ge(consts_ready, 1)
            flat = both[:].rearrange("p n e -> p (n e)")
            pe.matmul(ps_rank[:, 0, :], before[:], flat, start=True, stop=True)
            pe.matmul(ps_rank[:, 1, :], ones[:], flat, start=True, stop=True).then_inc(ranked, 1)

        @block.vector
        def _(vec):
            steps = [0]

            def link(ins):
                steps[0] += 1
                ins.then_inc(step, 1)
                vec.wait_ge(step, steps[0])

            def over(cols):
                return cols.unsqueeze(2).to_broadcast([P, NBK, E])

            def each_block(row):
                return row.unsqueeze(1).to_broadcast([P, NBK, E])

            vec.wait_ge(consts_ready, 1)
            link(vec.tensor_copy(order[:], order_i[:]))
            link(vec.tensor_copy(tile_no[:], tile_no_i[:]))
            link(vec.tensor_reduce(col[:], logits[:], AX.X, ALU.max))
            vec.tensor_tensor(shifted[:], logits[:], over(col[:]), ALU.subtract).then_inc(shifted_done, 1)
            vec.wait_ge(exp_done, 1)
            link(vec.tensor_reduce(col[:], probs[:], AX.X, ALU.add))
            link(vec.reciprocal(rcol[:], col[:]))
            link(vec.tensor_tensor(probs[:], probs[:], over(rcol[:]), ALU.mult))
            for k, left in ((0, probs), (1, rest)):
                link(vec.tensor_reduce(top[k][:], left[:], AX.X, ALU.max))
                link(vec.tensor_tensor(same[:], left[:], over(top[k][:]), ALU.is_equal))
                link(vec.tensor_tensor(key[:], same[:], each_block(order[:]), ALU.mult))
                link(vec.tensor_reduce(col[:], key[:], AX.X, ALU.max))
                link(vec.tensor_tensor(picked[k][:], key[:], over(col[:]), ALU.is_equal))
                if k == 0:
                    link(vec.scalar_tensor_tensor(rest[:], picked[0][:], -2.0, probs[:], ALU.mult, ALU.add))
            link(vec.tensor_tensor(both[:], picked[0][:], picked[1][:], ALU.add))
            vec.tensor_tensor(tot[:], top[0][:], top[1][:], ALU.add).then_inc(picks_ready, 1)
            vec.wait_ge(picks_ready, 1)
            link(vec.tensor_scalar(tot[:], tot[:], 1e-9, None, ALU.add))
            link(vec.reciprocal(rcol[:], tot[:]))
            for k in range(2):
                link(vec.tensor_tensor(gates[k][:], top[k][:], rcol[:], ALU.mult))
            vec.wait_ge(ranked, 1)
            link(vec.tensor_copy(in_block[:], ps_rank[:, 0, :].rearrange("p (n e) -> p n e", e=E)))
            link(vec.tensor_copy(sums[0][:], ps_rank[:, 1, :].rearrange("p (n e) -> p n e", e=E)))
            a, b = sums
            d = 1
            while d < NBK:
                link(vec.tensor_copy(b[:, 0:d, :], a[:, 0:d, :]))
                link(vec.tensor_tensor(b[:, d:NBK, :], a[:, d:NBK, :], a[:, 0:NBK - d, :], ALU.add))
                a, b = b, a
                d *= 2
            link(vec.tensor_tensor(rank[:], a[:], ps_rank[:, 1, :].rearrange("p (n e) -> p n e", e=E), ALU.subtract))
            link(vec.tensor_tensor(rank[:], rank[:], in_block[:], ALU.add))
            link(vec.tensor_scalar(n_tiles[:], a[:, NBK - 1, :], float(T - 1), None, ALU.add))
            link(vec.tensor_copy(tiles_i[:], n_tiles[:]))
            link(vec.tensor_scalar(tiles_i[:], tiles_i[:], plan.SHIFT, None, ALU.logical_shift_right))
            link(vec.tensor_copy(n_tiles[:], tiles_i[:]))
            a, b = ends
            link(vec.tensor_copy(a[:], n_tiles[:]))
            d = 1
            while d < E:
                link(vec.tensor_copy(b[:, 0:d], a[:, 0:d]))
                link(vec.tensor_tensor(b[:, d:E], a[:, d:E], a[:, 0:E - d], ALU.add))
                a, b = b, a
                d *= 2
            link(vec.tensor_tensor(first_row[:], a[:], n_tiles[:], ALU.subtract))
            link(vec.tensor_scalar(first_row[:], first_row[:], float(T), None, ALU.mult))
            link(vec.tensor_tensor(rank[:], rank[:], each_block(first_row[:]), ALU.add))
            for k in range(2):
                link(vec.tensor_tensor(key[:], picked[k][:], rank[:], ALU.mult))
                link(vec.tensor_reduce(slot_f[:], key[:], AX.X, ALU.add))
                vec.tensor_copy(slots[k][:], slot_f[:]).then_inc(slots_ready, 1)
                vec.wait_ge(slots_ready, k + 1)
            link(vec.tensor_scalar(expert_of[:], tile_no[:], a[:, 0:1], None, ALU.is_ge))
            for e in range(1, E - 1):
                link(vec.scalar_tensor_tensor(expert_of[:], tile_no[:], a[:, e:e + 1], expert_of[:], ALU.is_ge, ALU.add))
            link(vec.tensor_copy(tile_table[:], expert_of[0:1, :]))


def run_experts(nc, sh, plan, x_sorted, tile_table, gate_w, gate_b, up_w, up_b, down_w, down_b, y_sorted):
    E, D, FF, KC = sh.E, sh.D, sh.FF, sh.KC
    T, TILES = plan.T, plan.TILES
    TB, FC = T // P, FF // P
    with ExitStack() as ctx:
        def sb(name, shape, dt=F32):
            return ctx.enter_context(nc.sbuf_tensor(name, shape, dt))

        def ps(name, shape, dt=F32):
            return ctx.enter_context(nc.psum_tensor(name, shape, dt))

        def sem(name):
            return sh.semaphore(nc, name)

        def sems(name):
            return [sem(f"{name}{n}") for n in range(2)]

        ident = sb("e_ident", [P, P])
        bias_rows, bias_table = sb("e_bias_rows", [2 * E * FC, P]), sb("e_bias_table", [P, 2, E, FC])
        where = sb("e_where", [1, 2], I32)
        gu_raw = [sb(f"e_gu_raw{n}", [P, KC, 2 * FF]) for n in range(2)]
        dn_raw = [sb(f"e_dn_raw{n}", [P, FC, D]) for n in range(2)]
        gu_hi, gu_lo = ([sb(f"e_gu_{x}{n}", [P, KC, 2 * FF], F32R) for n in range(2)] for x in ("hi", "lo"))
        dn_hi, dn_lo = ([sb(f"e_dn_{x}{n}", [P, FC, D], F32R) for n in range(2)] for x in ("hi", "lo"))
        bias = [sb(f"e_bias{n}", [P, 2, FC]) for n in range(2)]
        dn_bias = [sb(f"e_dn_bias{n}", [P, D]) for n in range(2)]
        x_in = [sb(f"e_x_in{n}", [P, TB, D]) for n in range(2)]
        xT_hi, xT_lo = ([sb(f"e_xT_{x}{n}", [P, KC, T], F32R) for n in range(2)] for x in ("hi", "lo"))
        gate = [sb(f"e_gate{n}", [P, T]) for n in range(2)]
        hid = [sb(f"e_hid{n}", [P, T]) for n in range(2)]
        hid_hi, hid_lo = sb("e_hid_hi", [P, FC, T], F32R), sb("e_hid_lo", [P, FC, T], F32R)
        y_out = [sb(f"e_y_out{n}", [P, TB, D]) for n in range(2)]
        ps_x = [ps(f"e_ps_x{k}", [P, T]) for k in range(KC)]
        ps_g, ps_u, ps_y = ([ps(f"e_ps_{x}{n}", [P, 512]) for n in range(2)] for x in "guy")

        consts_step, rows_loaded, table_turned, table_ready = (
            sem("e_consts_step"), sem("e_rows_loaded"), sem("e_table_turned"), sem("e_table_ready"))
        where_loaded, sp_turns, pool_turns = sem("e_where_loaded"), sem("e_sp_turns"), sem("e_pool_turns")
        w_loaded, b_loaded = sems("e_w_loaded"), sems("e_b_loaded")
        x_loaded, y_stored = sems("e_x_loaded"), sems("e_y_stored")
        gu_hi_done, gu_lo_done, dn_hi_done, dn_lo_done = (
            sems("e_gu_hi_done"), sems("e_gu_lo_done"), sems("e_dn_hi_done"), sems("e_dn_lo_done"))
        x_turned, x_hi, x_lo = sem("e_x_turned"), sem("e_x_hi"), sem("e_x_lo")
        gu_made, gate_done, hid_done, hid_hi_done, hid_lo_done = (
            sems("e_gu_made"), sems("e_gate_done"), sems("e_hid_done"), sems("e_hid_hi_done"), sems("e_hid_lo_done"))
        y_made, y_kept = sems("e_y_made"), sems("e_y_kept")

        block = ctx.enter_context(nc.Block())
        W_LOADS, B_LOADS = 3, 2

        def all_tiles(eng, tile):
            for t in range(2):
                tile(t, t, 0)
            with eng.Fori(1, (TILES - 2) // 2) as i:
                for par in range(2):
                    tile(2 * i + par, par, i)
            for t in range((TILES - 2) // 2 * 2, TILES):
                tile(t, t % 2, t // 2)

        def has(t, ahead):
            return not isinstance(t, int) or 0 <= t + ahead < TILES

        @block.sync
        def _(sp):
            for n, b in enumerate((gate_b, up_b)):
                sp.dma_start(bias_rows[n * E * FC:(n + 1) * E * FC, :], b.rearrange("e (f p) -> (e f) p", p=P))\
                    .then_inc(rows_loaded, 16)

            def experts(t, first, count, loads):
                sp.dma_start(where[0:1, 0:count], tile_table[0:1, bass.ds(t + first, count)]).then_inc(where_loaded, 16)
                sp.wait_ge(where_loaded, 16 * loads)
                sp.sem_inc(sp_turns, 1)
                return [sp.value_load(where[0:1, n:n + 1], min_val=0, max_val=E - 1) for n in range(count)]

            def load_weights(e, par):
                for n, w in enumerate((gate_w, up_w)):
                    sp.dma_start(gu_raw[par][:, :, n * FF:(n + 1) * FF],
                                 w[bass.ds(e, 1)].rearrange("a (k p) f -> p (a k) f", p=P)).then_inc(w_loaded[par], 16)
                sp.dma_start(dn_raw[par][:], down_w[bass.ds(e, 1)].rearrange("a (f p) d -> p (a f) d", p=P))\
                    .then_inc(w_loaded[par], 16)

            def load_biases(e, par):
                sp.dma_start(bias[par][:], bias_table[:, :, bass.ds(e, 1), :].rearrange("p n a f -> p n (a f)"))\
                    .then_inc(b_loaded[par], 16)
                sp.dma_start(dn_bias[par][:], down_b[bass.ds(e, 1), :].to_broadcast([P, D])).then_inc(b_loaded[par], 16)

            def load_rows(t, par):
                sp.dma_start(x_in[par][:], x_sorted[bass.ts(t, T), :].rearrange("(k p) d -> p k d", p=P))\
                    .then_inc(x_loaded[par], 16)

            def store(t, par):
                for n in range(2):
                    sp.wait_ge(y_kept[n], (t + 1) * (TB // 2))
                sp.dma_start(y_sorted[bass.ts(t, T), :].rearrange("(k p) d -> p k d", p=P), y_out[par][:])\
                    .then_inc(y_stored[par], 16)

            def tile(t, par, turn):
                if has(t, 2):
                    sp.wait_ge(gu_lo_done[par], turn + 1)
                    sp.wait_ge(dn_lo_done[par], turn + 1)
                    e_next, e = experts(t, 1, 2, t + 2)
                    load_weights(e, par)
                    sp.wait_ge(x_turned, t + 1)
                    load_rows(t + 2, par)
                elif has(t, 1):
                    e_next, = experts(t, 1, 1, t + 2)
                if has(t, -1):
                    store(t - 1, 1 - par)
                if has(t, 1):
                    load_biases(e_next, 1 - par)

            e0, e1 = experts(0, 0, 2, 1)
            load_weights(e0, 0)
            load_rows(0, 0)
            load_weights(e1, 1)
            load_rows(1, 1)
            sp.wait_ge(table_ready, 1)
            load_biases(e0, 0)
            all_tiles(sp, tile)
            store(TILES - 1, (TILES - 1) % 2)
            for par in range(2):
                sp.wait_ge(y_stored[par], 16 * ((TILES + 1 - par) // 2))

        @block.gpsimd
        def _(pool):
            pool.memset(ident[:], 0.0).then_inc(consts_step, 1)
            pool.wait_ge(consts_step, 1)
            pool.affine_select(out=ident[:], in_=ident[:], compare_op=ALU.not_equal, fill=1.0, base=0,
                               pattern=[[-1, P]], channel_multiplier=1).then_inc(consts_step, 1)

            def low_parts(par, turn):
                pool.wait_ge(gu_hi_done[par], turn + 1)
                pool.sem_inc(pool_turns, 1)
                pool.tensor_tensor(gu_lo[par][:], gu_raw[par][:], gu_hi[par][:].bitcast(F32), ALU.subtract)\
                    .then_inc(gu_lo_done[par], 1)
                pool.wait_ge(dn_hi_done[par], turn + 1)
                pool.sem_inc(pool_turns, 1)
                pool.tensor_tensor(dn_lo[par][:], dn_raw[par][:], dn_hi[par][:].bitcast(F32), ALU.subtract)\
                    .then_inc(dn_lo_done[par], 1)

            def tile(t, par, turn):
                if has(t, 1):
                    low_parts(1 - par, turn + par)

            low_parts(0, 0)
            all_tiles(pool, tile)

        @block.scalar
        def _(act):
            def gu_high(t, par, turn):
                act.wait_ge(w_loaded[par], 16 * W_LOADS * (turn + 1))
                if has(t, -2):
                    act.wait_ge(gu_made[1], (t - 1) * (FC // 2))
                act.copy(gu_hi[par][:], gu_raw[par][:]).then_inc(gu_hi_done[par], 1)

            def dn_high(t, par):
                if has(t, -2):
                    act.wait_ge(y_made[1], (t - 1) * (TB // 2))
                act.copy(dn_hi[par][:], dn_raw[par][:]).then_inc(dn_hi_done[par], 1)

            def x_high(t, par):
                act.wait_ge(x_turned, t + 1)
                for k in range(KC):
                    ins = act.copy(xT_hi[par][:, k, :], ps_x[k][:])
                ins.then_inc(x_hi, 1)

            def tile(t, par, turn):
                def gates(f):
                    n, m = f % 2, t * (FC // 2) + f // 2
                    act.wait_ge(gu_made[n], m + 1)
                    act.wait_ge(hid_done[n], m)
                    act.activation(gate[n][:], ps_g[n][:], ACT.Silu, bias=bias[par][:, 0, f:f + 1]).then_inc(gate_done[n], 1)

                def hid_high(f):
                    n, m = f % 2, t * (FC // 2) + f // 2
                    act.wait_ge(hid_done[n], m + 1)
                    act.wait_ge(y_made[1], t * (TB // 2))
                    act.copy(hid_hi[:, f, :], hid[n][:]).then_inc(hid_hi_done[n], 1)

                if has(t, 1):
                    gu_high(t + 1, 1 - par, turn + par)
                act.wait_ge(b_loaded[par], 16 * B_LOADS * (turn + 1))
                gates(0)
                hid_high(0)
                if has(t, 1):
                    x_high(t + 1, 1 - par)
                gates(1)
                if has(t, 1):
                    dn_high(t + 1, 1 - par)
                for f in range(2, FC):
                    gates(f)
                    hid_high(f - 1)
                hid_high(FC - 1)

            act.wait_ge(table_turned, 1)
            act.copy(bias_table[:].rearrange("p n e f -> p (n e f)"), ps_y[0][:, 0:2 * E * FC]).then_inc(table_ready, 1)
            gu_high(0, 0, 0)
            dn_high(0, 0)
            x_high(0, 0)
            all_tiles(act, tile)

        @block.vector
        def _(vec):
            def x_low(t, par):
                vec.wait_ge(x_hi, t + 1)
                for k in range(KC):
                    ins = vec.tensor_tensor(xT_lo[par][:, k, :], ps_x[k][:], xT_hi[par][:, k, :].bitcast(F32), ALU.subtract)
                ins.then_inc(x_lo, 1)

            def keep_y(t, par, turn):
                vec.wait_ge(y_stored[par], 16 * turn)
                for blk in range(TB):
                    n = blk % 2
                    vec.wait_ge(y_made[n], t * (TB // 2) + blk // 2 + 1)
                    vec.tensor_tensor(y_out[par][:, blk, :], ps_y[n][:, 0:D], dn_bias[par][:], ALU.add).then_inc(y_kept[n], 1)

            def tile(t, par, turn):
                def hidden(f):
                    n, m = f % 2, t * (FC // 2) + f // 2
                    vec.wait_ge(gate_done[n], m + 1)
                    vec.wait_ge(hid_lo_done[n], m)
                    vec.scalar_tensor_tensor(hid[n][:], ps_u[n][:], bias[par][:, 1, f:f + 1], gate[n][:],
                                             ALU.add, ALU.mult).then_inc(hid_done[n], 1)

                def hid_low(f):
                    n, m = f % 2, t * (FC // 2) + f // 2
                    vec.wait_ge(hid_hi_done[n], m + 1)
                    vec.tensor_tensor(hid_lo[:, f, :], hid[n][:], hid_hi[:, f, :].bitcast(F32), ALU.subtract)\
                        .then_inc(hid_lo_done[n], 1)

                hidden(0)
                if has(t, -1):
                    keep_y(t - 1, 1 - par, turn - 1 + par)
                hid_low(0)
                if has(t, 1):
                    x_low(t + 1, 1 - par)
                for f in range(1, FC):
                    hidden(f)
                    if f > 1:
                        hid_low(f - 1)
                hid_low(FC - 1)

            x_low(0, 0)
            all_tiles(vec, tile)
            keep_y(TILES - 1, (TILES - 1) % 2, (TILES - 1) // 2)

        @block.tensor
        def _(pe):
            pe.wait_ge(consts_step, 2)
            pe.wait_ge(rows_loaded, 32)
            pe.transpose(ps_y[0][:, 0:2 * E * FC], bias_rows[:], ident[0:2 * E * FC, 0:2 * E * FC]).then_inc(table_turned, 1)
            pe.wait_ge(table_ready, 1)

            def turn_x(t, par, turn):
                pe.wait_ge(x_loaded[par], 16 * (turn + 1))
                pe.wait_ge(x_lo, t)
                for k in range(KC):
                    for blk in range(TB):
                        mm = pe.transpose(ps_x[k][:, blk * P:(blk + 1) * P], x_in[par][:, blk, k * P:(k + 1) * P], ident[:])
                mm.then_inc(x_turned, 1)

            def gate_up(t, par, f):
                n, m = f % 2, t * (FC // 2) + f // 2
                pe.wait_ge(hid_done[n], m)
                for out, first in ((ps_g[n], 0), (ps_u[n], FF)):
                    cols = slice(first + f * P, first + (f + 1) * P)
                    todo = [p for k in range(KC) for p in ((gu_hi, xT_hi, k), (gu_hi, xT_lo, k), (gu_lo, xT_hi, k))]
                    for s, (w, x, k) in enumerate(todo):
                        mm = pe.matmul(out[:], w[par][:, k, cols], x[par][:, k, :], start=(s == 0), stop=(s == len(todo) - 1))
                mm.then_inc(gu_made[n], 1)

            def down(t, par, turn):
                pe.wait_ge(dn_lo_done[par], turn + 1)
                for n in range(2):
                    pe.wait_ge(hid_lo_done[n], (t + 1) * (FC // 2))
                for blk in range(TB):
                    n, rows = blk % 2, slice(blk * P, (blk + 1) * P)
                    pe.wait_ge(y_kept[n], t * (TB // 2) + blk // 2)
                    todo = [p for f in range(FC) for p in ((hid_hi, dn_hi, f), (hid_hi, dn_lo, f), (hid_lo, dn_hi, f))]
                    for s, (h, w, f) in enumerate(todo):
                        mm = pe.matmul(ps_y[n][:, 0:D], h[:, f, rows], w[par][:, f, :], start=(s == 0), stop=(s == len(todo) - 1))
                    mm.then_inc(y_made[n], 1)

            def tile(t, par, turn):
                pe.wait_ge(x_lo, t + 1)
                pe.wait_ge(gu_lo_done[par], turn + 1)
                gate_up(t, par, 0)
                if has(t, -1):
                    down(t - 1, 1 - par, turn - 1 + par)
                if has(t, 1):
                    turn_x(t + 1, 1 - par, turn + par)
                for f in range(1, FC):
                    gate_up(t, par, f)

            turn_x(0, 0, 0)
            all_tiles(pe, tile)
            down(TILES - 1, (TILES - 1) % 2, (TILES - 1) // 2)


def combine(nc, sh, plan, x2_all, slots, gates, y_sorted, out):
    D, NBK = sh.D, plan.BLOCKS
    G = 4
    GROUPS = NBK // G
    with ExitStack() as ctx:
        def sb(name, shape, dt=F32):
            return ctx.enter_context(nc.sbuf_tensor(name, shape, dt))

        def sem(name):
            return sh.semaphore(nc, name)

        def sems(name):
            return [sem(f"{name}{n}") for n in range(2)]

        y = [[sb(f"f_y{par}_{k}", [P, G, D]) for k in range(2)] for par in range(2)]
        resid = [sb(f"f_resid{par}", [P, G, D]) for par in range(2)]
        stats = [sb(f"f_stats{par}", [P, G, 6]) for par in range(2)]
        mv = [sb(f"f_mv{par}", [P, G, 2]) for par in range(2)]
        ln_var, rstd = ([sb(f"f_{x}{par}", [P, G]) for par in range(2)] for x in ("ln_var", "rstd"))
        eps_col = sb("f_eps_col", [P, 1])
        gathered, added, normed, var_ready, stored = (
            sems("f_gathered"), sems("f_added"), sems("f_normed"), sems("f_var_ready"), sems("f_stored"))
        eps_ready, step, ln_step, rstd_ready = sem("f_eps_ready"), sem("f_step"), sem("f_ln_step"), sems("f_rstd_ready")
        vec_turns = sem("f_vec_turns")
        block = ctx.enter_context(nc.Block())
        out_rows = out.rearrange("b (k p) d -> p (b k) d", p=P)

        @block.gpsimd
        def _(pool):
            pool.memset(eps_col[:], LN_EPS).then_inc(eps_ready, 1)
            for i in range(GROUPS):
                par, turn = i % 2, i // 2
                if turn:
                    pool.wait_ge(added[par], turn * G)
                for j in range(G):
                    for k in range(2):
                        n = i * G + j
                        pool.indirect_dma_start(y[par][k][:, j, :], None, y_sorted,
                                                bass.IndirectOffsetOnAxis(slots[k][:, n:n + 1], 0))\
                            .then_inc(gathered[par], 16)

        @block.scalar
        def _(act):
            act.wait_ge(eps_ready, 1)
            with act.Fori(0, GROUPS // 2) as turn:
                for par in range(2):
                    act.wait_ge(var_ready[par], turn + 1)
                    act.activation(ln_var[par][:], mv[par][:, :, 1], ACT.Ln, bias=eps_col[:]).then_inc(ln_step, 1)
                    act.wait_ge(ln_step, turn * 2 + par + 1)
                    act.activation(rstd[par][:], ln_var[par][:], ACT.Exp, scale=-0.5).then_inc(rstd_ready[par], 1)

        @block.vector
        def _(vec):
            def add_rows(turn, par):
                first = (turn * 2 + par) * G
                vec.wait_ge(gathered[par], 16 * 2 * G * (turn + 1))
                vec.wait_ge(stored[par], 16 * turn)
                for j in range(G):
                    n = first + j
                    vec.scalar_tensor_tensor(resid[par][:, j, :], y[par][0][:, j, :], gates[0][:, bass.ds(n, 1)],
                                             x2_all[:, bass.ds(n, 1), :].rearrange("p n d -> p (n d)"),
                                             ALU.mult, ALU.add).then_inc(step, 1)
                for j in range(G):
                    n = first + j
                    vec.wait_ge(step, (turn * 2 + par) * 2 * G + G + j)
                    ins = vec.scalar_tensor_tensor(resid[par][:, j, :], y[par][1][:, j, :], gates[1][:, bass.ds(n, 1)],
                                                   resid[par][:, j, :], ALU.mult, ALU.add)
                    ins.then_inc(step, 1)
                vec.wait_ge(step, (turn * 2 + par + 1) * 2 * G)
                for j in range(G):
                    vec.bn_stats(stats[par][:, j, :], resid[par][:, j, :]).then_inc(added[par], 1)
                vec.wait_ge(added[par], G * (turn + 1))
                vec.sem_inc(vec_turns, 1)
                for j in range(G):
                    ins = vec.bn_aggr(mv[par][:, j, :], stats[par][:, j, :])
                ins.then_inc(var_ready[par], 1)

            def normalise(turn, par):
                vec.wait_ge(rstd_ready[par], turn + 1)
                for j in range(G):
                    ins = vec.tensor_scalar(resid[par][:, j, :], resid[par][:, j, :], mv[par][:, j, 0:1],
                                            rstd[par][:, j:j + 1], ALU.subtract, ALU.mult)
                ins.then_inc(normed[par], 1)

            def pair(turn):
                add_rows(turn, 0)
                add_rows(turn, 1)
                normalise(turn, 0)
                normalise(turn, 1)

            pair(0)
            with vec.Fori(1, GROUPS // 2) as turn:
                pair(turn)

        @block.sync
        def _(sp):
            with sp.Fori(0, GROUPS // 2) as turn:
                for par in range(2):
                    sp.wait_ge(normed[par], turn + 1)
                    sp.dma_start(out_rows[:, bass.ds((turn * 2 + par) * G, G), :], resid[par][:]).then_inc(stored[par], 16)
            for par in range(2):
                sp.wait_ge(stored[par], 16 * GROUPS // 2)


def decoder_layer(nc, x, ctx_1024, mask, Wq, Wk, Wv, Wo, Wa, ba, xWq, xbq, xWk, xbk, xWv, xbv, xWo, xbo,
                  router_w, gate_w, gate_b, up_w, up_b, down_w, down_b, out):
    with ExitStack() as ctx:
        sh = Shapes(x, Wq, ctx_1024, gate_w)
        plan = Plan(sh)
        x1_dram = nc.dram_tensor("x1_rows", list(x.shape), F32).ap()
        x_sorted = nc.dram_tensor("x_sorted", [plan.ROWS, sh.D], F32).ap()
        y_sorted = nc.dram_tensor("y_sorted", [plan.ROWS, sh.D], F32).ap()

        def sb(name, shape, dt=F32):
            return ctx.enter_context(nc.sbuf_tensor(name, shape, dt))

        x2_all = sb("x2_all", [P, plan.BLOCKS, sh.D])
        logits = sb("logits", [P, plan.BLOCKS, sh.E])
        slots = [sb(f"slots{k}", [P, plan.BLOCKS], U32) for k in range(2)]
        gates = [sb(f"gates{k}", [P, plan.BLOCKS]) for k in range(2)]
        tile_table = sb("tile_table", [1, plan.TILES], I32)
        linear_attention(nc, sh, x, Wq, Wk, Wv, Wo, Wa, ba, x1_dram, x_sorted)
        sh.end_stage(nc)
        cross_attention(nc, sh, x1_dram, ctx_1024, mask, xWq, xbq, xWk, xbk, xWv, xbv, xWo, xbo,
                        router_w, x2_all, logits)
        sh.end_stage(nc)
        route_tokens(nc, sh, plan, logits, x2_all, x_sorted, slots, gates, tile_table)
        run_experts(nc, sh, plan, x_sorted, tile_table, gate_w, gate_b, up_w, up_b, down_w, down_b, y_sorted)
        combine(nc, sh, plan, x2_all, slots, gates, y_sorted, out)


_INS = ["x", "ctx_1024", "mask_BxSxS2_if1"] + ["L0_attn_" + n for n in ("Wq", "Wk", "Wv", "Wo", "Wa", "ba")] \
    + ["L0_xattn_" + n for n in ("Wq", "bq", "Wk", "bk", "Wv", "bv", "Wo", "bo")] \
    + ["L0_ffn_" + n for n in ("router_w", "gate_w", "gate_b", "up_w", "up_b", "down_w", "down_b")]


def kernel(**inputs):
    import numpy as _np
    import concourse.bacc as _bacc
    from concourse.bass_utils import run_bass_kernel_spmd as _run

    nc = _bacc.Bacc("TRN2", target_bir_lowering=False, num_devices=1)
    arrays, args = {}, []
    for name in _INS:
        a = _np.ascontiguousarray(inputs[name])
        arrays[f"in_{name}"] = a
        args.append(nc.dram_tensor(f"in_{name}", a.shape, mybir.dt.from_np(a.dtype), kind="ExternalInput").ap())
    args.append(nc.dram_tensor("out", inputs["x"].shape, F32, kind="ExternalOutput").ap())
    decoder_layer(nc, *args)
    return _run(nc, [arrays], core_ids=[0]).results[0]["out"]
```

```python
from contextlib import ExitStack

import concourse.bass as bass
from concourse import mybir

F32 = mybir.dt.float32
F32R = mybir.dt.float32r
BF16 = mybir.dt.bfloat16
I32 = mybir.dt.int32
U32 = mybir.dt.uint32
ALU = mybir.AluOpType
ACT = mybir.ActivationFunctionType
AX = mybir.AxisListType

P = 128
LN_EPS = 1e-5


class Shapes:

    def __init__(self, x, wq, ctx, gate_w):
        self.counted = []
        self.B, self.N, self.D = x.shape
        self.NB = self.N // P
        self.KC = self.D // P
        self.H = 16
        self.DH = wq.shape[1] // self.H
        self.PAIRS = self.H // 2
        self.S2 = ctx.shape[1]
        self.E, _, self.FF = gate_w.shape

    def semaphore(self, nc, name):
        self.counted.append(nc.alloc_semaphore(name))
        return self.counted[-1]

    def end_stage(self, nc):
        nc.clear_and_free_semaphores(self.counted)
        nc.all_engine_barrier()
        self.counted = []


def linear_attention(nc, sh, x, wq, wk, wv, wo, wa, ba, x1_dram, x_sorted):
    B, N, D, H, DH, NB, KC, PAIRS = sh.B, sh.N, sh.D, sh.H, sh.DH, sh.NB, sh.KC, sh.PAIRS
    PW = H * DH
    HALF = PW // 2
    HEADS_HALF = HALF // DH
    VU = 2 * NB
    CP = 3 * H
    TRI = N + P
    DECAY_SHIFT, EPS, Z_FLOOR = 2.0, 1e-6, -80.0
    with ExitStack() as ctx:
        def sb(name, shape, dt=F32):
            return ctx.enter_context(nc.sbuf_tensor(name, shape, dt))

        def ps(name, shape, dt=F32):
            return ctx.enter_context(nc.psum_tensor(name, shape, dt))

        def sem(name):
            return sh.semaphore(nc, name)

        w_raw = sb("a_w_raw", [P, KC, PW])
        w_hi = [sb(f"a_w_hi{n}", [P, KC, PW], F32R) for n in range(3)]
        w_lo = [sb(f"a_w_lo{n}", [P, KC, PW], F32R) for n in range(3)]
        wo_sb = sb("a_wo", [P, PAIRS, D])
        wa_raw = sb("a_wa_raw", [P, KC, H])
        wa_hi, wa_lo = sb("a_wa_hi", [P, KC, H], F32R), sb("a_wa_lo", [P, KC, H], F32R)
        ba_row, ba_shift = sb("a_ba_row", [1, H]), sb("a_ba_shift", [1, H])
        ident, ident_bf = sb("a_ident", [P, P]), sb("a_ident_bf", [P, P], BF16)
        ones, upto = sb("a_ones", [P, P]), sb("a_upto", [P, P])
        pick_head = sb("a_pick_head", [CP, H, P], BF16)
        x_in, x_res = sb("a_x_in", [P, NB, D]), sb("a_x_res", [P, NB, D])
        xT_hi, xT_lo = sb("a_xT_hi", [P, KC, N], F32R), sb("a_xT_lo", [P, KC, N], F32R)
        z_sb, z_exp, dec = sb("a_z", [P, NB, H]), sb("a_z_exp", [P, NB, H]), sb("a_dec", [P, NB, H])
        c_next, c_now = sb("a_c_next", [P, NB, H]), sb("a_c_now", [P, NB, H])
        c_rest = sb("a_c_rest", [P, NB, H])
        c_parts = sb("a_c_parts", [P, NB, 3, H], BF16)
        cT_next, cT_now = sb("a_cT_next", [CP, N], BF16), sb("a_cT_now", [CP, N], BF16)
        qk_exp = sb("a_qk_exp", [P, 2, N])
        qk = [sb(f"a_qk{g}", [P, 2, N]) for g in range(PAIRS)]
        v_aug = [sb(f"a_v_aug{n}", [P, NB, H, DH + 1]) for n in range(2)]
        decay = [sb(f"a_decay{h}", [P, TRI]) for h in range(2)]
        probs = [sb(f"a_probs{h}", [P, TRI]) for h in range(2)]
        den, rden = sb("a_den", [P, NB, 2]), sb("a_rden", [P, NB, 2])
        o_norm, oT = sb("a_o_norm", [P, NB, 2, DH]), sb("a_oT", [P, NB * P])
        resid = sb("a_resid", [P, NB, D])
        stats, mv = sb("a_stats", [P, NB, 6]), sb("a_mv", [P, NB, 2])
        ln_var, rstd = sb("a_ln_var", [P, NB]), sb("a_rstd", [P, NB])
        eps_col = sb("a_eps_col", [P, 1])
        x1, zeros = sb("a_x1", [P, NB, D]), sb("a_zeros", [P, D])
        ps_mix = ps("a_ps_mix", [P, 512])
        ps_qk = ps("a_ps_qk", [P, 2, N])
        ps_c = ps("a_ps_c", [P, 2, N])
        ps_s = [ps(f"a_ps_s{h}", [P, 512]) for h in range(2)]
        ps_o = ps("a_ps_o", [P, 512])
        ps_t = ps("a_ps_t", [P, 512])
        ps_y = ps("a_ps_y", [P, NB, D])
        o_view = ps_o[:, 0:NB * 2 * (DH + 1)].rearrange("p (b h d) -> p b h d", b=NB, h=2)
        c_view = ps_mix[:, 0:NB * H].rearrange("p (b h) -> p b h", b=NB)
        cT_view = ps_mix[:, :].bitcast(BF16)

        consts_ready = sem("a_consts_ready")
        consts_step = sem("a_consts_step")
        raw_loaded = [sem(f"a_raw_loaded{n}") for n in range(3)]
        small_loaded = sem("a_small_loaded")
        w_hi_done, w_lo_done = sem("a_w_hi_done"), sem("a_w_lo_done")
        x_in_loaded, x_res_loaded, x1_stored = sem("a_x_in_loaded"), sem("a_x_res_loaded"), sem("a_x1_stored")
        rows_zeroed = sem("a_rows_zeroed")
        pool_turns, vec_turns, pe_turns = sem("a_pool_turns"), sem("a_vec_turns"), sem("a_pe_turns")
        xT_made, x_hi_done, x_lo_done = sem("a_xT_made"), sem("a_x_hi_done"), sem("a_x_lo_done")
        z_made, z_kept, z_exp_done, dec_done = sem("a_z_made"), sem("a_z_kept"), sem("a_z_exp_done"), sem("a_dec_done")
        c_made, c_step, c_split = sem("a_c_made"), sem("a_c_step"), sem("a_c_split")
        cT_made, cT_kept, c_switched = sem("a_cT_made"), sem("a_cT_kept"), sem("a_c_switched")
        qk_made, qk_exp_done, qk_exp_capped, qk_done = (
            sem("a_qk_made"), sem("a_qk_exp_done"), sem("a_qk_exp_capped"), sem("a_qk_done"))
        v_made, v_done = sem("a_v_made"), sem("a_v_done")
        c_spread, s_made = sem("a_c_spread"), sem("a_s_made")
        decay_exp = [sem(f"a_decay_exp{h}") for h in range(2)]
        decay_masked = [sem(f"a_decay_masked{h}") for h in range(2)]
        probs_done = [sem(f"a_probs_done{h}") for h in range(2)]
        o_made, den_step, o_normed = sem("a_o_made"), sem("a_den_step"), sem("a_o_normed")
        oT_made, oT_kept, y_added = sem("a_oT_made"), sem("a_oT_kept"), sem("a_y_added")
        resid_done, ln_step, var_ready, rstd_step, x1_ready = (
            sem("a_resid_done"), sem("a_ln_step"), sem("a_var_ready"), sem("a_rstd_step"), sem("a_x1_ready"))

        block = ctx.enter_context(nc.Block())
        x_rows = x.rearrange("b (k p) d -> b p k d", p=P)
        sorted_rows = x_sorted.rearrange("(p r) d -> p r d", p=P)
        cut = sorted_rows.shape[1] // 4
        zero_rows = [sorted_rows[:, n * cut:(n + 1) * cut, :] for n in range(4)]
        assert 4 * cut == sorted_rows.shape[1]
        x1_rows = x1_dram.rearrange("b (k p) d -> b p k d", p=P)

        def has(b, ahead):
            return not isinstance(b, int) or 0 <= b + ahead < B

        def all_sequences(eng, sequence):
            sequence(0, 0)
            pairs = (B - 3) // 2
            with eng.Fori(0, pairs) as i:
                for par in (1, 0):
                    sequence(2 * i + 2 - par, par)
            for b in range(2 * pairs + 1, B):
                sequence(b, b % 2)

        def back(b, par, g, steps):
            return (b, par, g - steps) if g >= steps else (b - 1, 1 - par, g - steps + PAIRS)

        def exists(b, g, steps):
            return g >= steps or has(b, -1)

        @block.sync
        def _(sp):
            sp.dma_start(x_in[:], x_rows[0]).then_inc(x_in_loaded, 16)
            sp.dma_start(wa_raw[:], wa.rearrange("(k p) h -> p k h", p=P)).then_inc(small_loaded, 16)
            sp.dma_start(ba_row[:], ba.rearrange("(a h) -> a h", a=1)).then_inc(small_loaded, 16)
            for n, w in enumerate((wq, wk, wv)):
                if n:
                    sp.wait_ge(w_lo_done, n)
                sp.dma_start(w_raw[:], w.rearrange("(k p) n -> p k n", p=P)).then_inc(raw_loaded[n], 16)
            sp.dma_start(wo_sb[:], wo.rearrange("(g p) n -> p g n", p=P)).then_inc(small_loaded, 16)
            sp.wait_ge(consts_ready, 1)
            for rows in zero_rows:
                sp.dma_start(rows, zeros[:].unsqueeze(1).to_broadcast([P, rows.shape[1], D])).then_inc(rows_zeroed, 16)

            def load_x(b):
                sp.wait_ge(xT_made, b)
                sp.dma_start(x_in[:], x_rows[b]).then_inc(x_in_loaded, 16)

            def load_residual(b):
                sp.wait_ge(resid_done, b)
                sp.dma_start(x_res[:], x_rows[b]).then_inc(x_res_loaded, 16)

            def store_x1(b):
                sp.wait_ge(x1_ready, b + 1)
                sp.dma_start(x1_rows[b], x1[:]).then_inc(x1_stored, 16)

            def sequence(b):
                load_x(b + 2)
                load_residual(b)
                store_x1(b - 1)

            load_x(1)
            load_x(2)
            load_residual(0)
            with sp.Fori(1, B - 2) as b:
                sequence(b)
            for b in (B - 2, B - 1):
                load_residual(b)
                store_x1(b - 1)
            store_x1(B - 1)
            sp.wait_ge(x1_stored, 16 * B)
            sp.wait_ge(rows_zeroed, 16 * len(zero_rows))

        @block.gpsimd
        def _(pool):
            pool.memset(ident[:], 0.0).then_inc(consts_step, 1)
            pool.memset(ident_bf[:], 0.0).then_inc(consts_step, 1)
            pool.memset(ones[:], 1.0).then_inc(consts_step, 1)
            pool.memset(pick_head[:], 0.0).then_inc(consts_step, 1)
            for n in range(2):
                pool.memset(v_aug[n][:], 1.0).then_inc(consts_step, 1)
            pool.memset(eps_col[:], LN_EPS).then_inc(consts_step, 1)
            pool.memset(zeros[:], 0.0).then_inc(consts_step, 1)
            pool.wait_ge(consts_step, 8)
            for m in (ident, ident_bf):
                pool.affine_select(out=m[:], in_=m[:], compare_op=ALU.not_equal, fill=1.0, base=0,
                                   pattern=[[-1, P]], channel_multiplier=1).then_inc(consts_step, 1)
            pool.affine_select(out=upto[:], in_=ones[:], compare_op=ALU.is_ge, fill=0.0, base=0,
                               pattern=[[1, P]], channel_multiplier=-1).then_inc(consts_step, 1)
            for part in range(3):
                if part:
                    pool.wait_ge(consts_step, 11 + part)
                pool.affine_select(out=pick_head[:], in_=pick_head[:], compare_op=ALU.not_equal, fill=1.0,
                                   base=-H * part, pattern=[[-1, H], [0, P]], channel_multiplier=1)\
                    .then_inc(consts_step, 1)
            pool.wait_ge(consts_step, 14)
            pool.memset(den[:], 1.0).then_inc(consts_ready, 1)

            def mask_decay(b, g):
                for h in range(2):
                    pool.wait_ge(decay_exp[h], b * PAIRS + g + 1)
                    pool.sem_inc(pool_turns, 1)
                    d = decay[h][:, :].rearrange("p (t i) -> p t i", i=P)[:, 0:3:2, :]
                    pool.affine_select(out=d, in_=d, compare_op=ALU.is_ge, fill=0.0, base=0,
                                       pattern=[[0, 2], [1, P]], channel_multiplier=-1)\
                        .then_inc(decay_masked[h], 1)

            def cap_exp(b, g):
                pool.wait_ge(qk_exp_done, b * PAIRS + g + 1)
                pool.sem_inc(pool_turns, 1)
                pool.tensor_scalar(qk_exp[:], qk_exp[:], 1.0, 0.0, ALU.min, ALU.max).then_inc(qk_exp_capped, 1)

            def sequence(b, par):
                for g in range(PAIRS):
                    mask_decay(b, g)
                    if has(b, 1):
                        cap_exp(b + 1, g)

            for g in range(PAIRS):
                cap_exp(0, g)
            all_sequences(pool, sequence)

        @block.scalar
        def _(act):
            for n in range(3):
                act.wait_ge(raw_loaded[n], 16)
                act.copy(w_hi[n][:], w_raw[:]).then_inc(w_hi_done, 1)
            act.wait_ge(small_loaded, 48)
            act.copy(wa_hi[:], wa_raw[:]).then_inc(w_hi_done, 1)
            act.wait_ge(consts_ready, 1)

            def x_hi(b):
                act.wait_ge(xT_made, b + 1)
                act.copy(xT_hi[:], ps_mix[:].rearrange("p (k n) -> p k n", k=KC)).then_inc(x_hi_done, 1)

            def exp_qk(b, g):
                act.wait_ge(qk_made, b * PAIRS + g + 1)
                act.wait_ge(qk_done, b * PAIRS + g)
                act.activation(qk_exp[:], ps_qk[:], ACT.Exp).then_inc(qk_exp_done, 1)

            def log_decay(b):
                act.wait_ge(z_kept, b + 1)
                act.activation(z_exp[:], z_sb[:], ACT.Exp, scale=-1.0).then_inc(z_exp_done, 1)
                act.wait_ge(z_exp_done, b + 1)
                act.activation(dec[:], z_exp[:], ACT.Ln, bias=1.0).then_inc(dec_done, 1)

            def keep_cT(b):
                act.wait_ge(cT_made, b + 1)
                act.wait_ge(c_switched, 2 * b)
                act.copy(cT_next[:], cT_view[0:CP, 0:N]).then_inc(cT_kept, 1)

            def keep_v(b, par, half, blk):
                act.wait_ge(v_made, b * VU + half * NB + blk + 1)
                if not isinstance(b, int) or b >= 2:
                    act.wait_ge(o_made, (b - 1) * PAIRS)
                act.copy(v_aug[par][:, blk, half * HEADS_HALF:(half + 1) * HEADS_HALF, 0:DH],
                         ps_mix[:].rearrange("p (h d) -> p h d", d=DH)).then_inc(v_done, 1)

            def switch_c(b):
                act.wait_ge(cT_kept, b + 1)
                act.wait_ge(c_split, b + 1)
                act.wait_ge(c_spread, b * PAIRS)
                act.wait_ge(decay_exp[1], b * PAIRS)
                act.copy(cT_now[:], cT_next[:]).then_inc(c_switched, 1)
                act.copy(c_now[:], c_next[:]).then_inc(c_switched, 1)
                act.wait_ge(c_switched, 2 * b + 2)

            def exp_decay(b, g):
                act.wait_ge(c_spread, b * PAIRS + g + 1)
                for h in range(2):
                    act.wait_ge(probs_done[h], b * PAIRS + g)
                    head = 2 * g + h
                    act.activation(decay[h][:, 0:N], ps_c[:, h, :], ACT.Exp,
                                   bias=c_now[:, 0, head:head + 1], scale=-1.0)
                    act.activation(decay[h][:, N:TRI], ps_c[:, h, P:N], ACT.Exp,
                                   bias=c_now[:, 1, head:head + 1], scale=-1.0).then_inc(decay_exp[h], 1)

            def keep_oT(b, g):
                act.wait_ge(oT_made, b * PAIRS + g + 1)
                act.wait_ge(y_added, b * PAIRS + g)
                act.copy(oT[:], ps_t[:, 0:NB * P]).then_inc(oT_kept, 1)

            def root(b):
                act.wait_ge(var_ready, b + 1)
                act.activation(ln_var[:], mv[:, :, 1], ACT.Ln, bias=eps_col[:]).then_inc(rstd_step, 1)
                act.wait_ge(rstd_step, 2 * b + 1)
                act.activation(rstd[:], ln_var[:], ACT.Exp, scale=-0.5).then_inc(rstd_step, 1)

            def sequence(b, par):
                for g in range(PAIRS):
                    if exists(b, g, 2):
                        before, _, pair = back(b, par, g, 2)
                        keep_oT(before, pair)
                    exp_decay(b, g)
                    if has(b, 1):
                        if g == PAIRS - 1:
                            switch_c(b + 1)
                            keep_v(b + 1, 1 - par, 1, 1)
                        if g == 5:
                            keep_cT(b + 1)
                        if g == 6:
                            keep_v(b + 1, 1 - par, 0, 1)
                        exp_qk(b + 1, g)
                        if g == 2:
                            log_decay(b + 1)
                        if g == 5:
                            keep_v(b + 1, 1 - par, 0, 0)
                        if g == 6:
                            keep_v(b + 1, 1 - par, 1, 0)
                    if g == 2 and has(b, -1):
                        root(b - 1)
                if has(b, 2):
                    x_hi(b + 2)

            x_hi(0)
            for g in range(PAIRS):
                exp_qk(0, g)
            log_decay(0)
            keep_cT(0)
            for half in range(2):
                for blk in range(NB):
                    keep_v(0, 0, half, blk)
            x_hi(1)
            switch_c(0)
            all_sequences(act, sequence)
            for g in (PAIRS - 2, PAIRS - 1):
                keep_oT(B - 1, g)
            root(B - 1)

        @block.vector
        def _(vec):
            for n in range(3):
                vec.wait_ge(w_hi_done, n + 1)
                vec.tensor_tensor(w_lo[n][:], w_raw[:], w_hi[n][:].bitcast(F32), ALU.subtract).then_inc(w_lo_done, 1)
            vec.wait_ge(w_hi_done, 4)
            vec.tensor_tensor(wa_lo[:], wa_raw[:], wa_hi[:].bitcast(F32), ALU.subtract).then_inc(w_lo_done, 1)
            vec.tensor_scalar(ba_shift[:], ba_row[:], DECAY_SHIFT, None, ALU.add).then_inc(w_lo_done, 1)
            vec.wait_ge(consts_ready, 1)

            def x_lo(b):
                vec.wait_ge(x_hi_done, b + 1)
                vec.tensor_tensor(xT_lo[:], ps_mix[:].rearrange("p (k n) -> p k n", k=KC), xT_hi[:].bitcast(F32),
                                  ALU.subtract).then_inc(x_lo_done, 1)

            def keep_z(b):
                vec.wait_ge(z_made, b + 1)
                vec.tensor_scalar(z_sb[:], c_view, Z_FLOOR, None, ALU.max).then_inc(z_kept, 1)

            def split_c(b):
                vec.wait_ge(c_made, b + 1)
                vec.wait_ge(c_switched, 2 * b)
                vec.wait_ge(cT_made, b)
                vec.tensor_copy(c_next[:], c_view).then_inc(c_step, 1)
                vec.tensor_copy(c_parts[:, :, 0, :], c_view).then_inc(c_step, 1)
                vec.wait_ge(c_step, 4 * b + 2)
                vec.tensor_tensor(c_rest[:], c_next[:], c_parts[:, :, 0, :], ALU.subtract).then_inc(c_step, 1)
                vec.wait_ge(c_step, 4 * b + 3)
                vec.tensor_copy(c_parts[:, :, 1, :], c_rest[:]).then_inc(c_step, 1)
                vec.wait_ge(c_step, 4 * b + 4)
                vec.tensor_tensor(c_parts[:, :, 2, :], c_rest[:], c_parts[:, :, 1, :], ALU.subtract)\
                    .then_inc(c_split, 1)

            def finish_qk(b, g):
                vec.wait_ge(qk_exp_capped, b * PAIRS + g + 1)
                if not isinstance(b, int) or b:
                    vec.wait_ge(s_made, (b - 1) * PAIRS + g + 1)
                vec.scalar_tensor_tensor(qk[g][:], ps_qk[:], 0.0, qk_exp[:], ALU.max, ALU.add).then_inc(qk_done, 1)

            def weigh(b, g):
                vec.wait_ge(s_made, b * PAIRS + g + 1)
                vec.wait_ge(o_made, b * PAIRS + g)
                for h in range(2):
                    vec.wait_ge(decay_masked[h], b * PAIRS + g + 1)
                    vec.tensor_tensor(probs[h][:], ps_s[h][:, 0:TRI], decay[h][:], ALU.mult)\
                        .then_inc(probs_done[h], 1)

            def normalise(b, g):
                n = b * PAIRS + g
                vec.wait_ge(o_made, n + 1)
                vec.tensor_scalar(den[:], o_view[:, :, :, DH], EPS, None, ALU.add).then_inc(den_step, 1)
                vec.wait_ge(den_step, 2 * n + 1)
                vec.reciprocal(rden[:], den[:]).then_inc(den_step, 1)
                vec.wait_ge(den_step, 2 * n + 2)
                vec.wait_ge(oT_made, n)
                vec.tensor_tensor(o_norm[:], o_view[:, :, :, 0:DH],
                                  rden[:].unsqueeze(3).to_broadcast([P, NB, 2, DH]), ALU.mult).then_inc(o_normed, 1)

            def add_residual(b):
                vec.wait_ge(y_added, (b + 1) * PAIRS)
                vec.wait_ge(x_res_loaded, 16 * (b + 1))
                vec.wait_ge(x1_ready, b)
                vec.tensor_tensor(resid[:], ps_y[:], x_res[:], ALU.add).then_inc(resid_done, 1)
                vec.wait_ge(resid_done, b + 1)
                for blk in range(NB):
                    vec.bn_stats(stats[:, blk, :], resid[:, blk, :]).then_inc(ln_step, 1)
                vec.wait_ge(ln_step, NB * b + NB)
                vec.sem_inc(vec_turns, 1)
                for blk in range(NB):
                    last = vec.bn_aggr(mv[:, blk, :], stats[:, blk, :])
                last.then_inc(var_ready, 1)

            def scale_x1(b):
                vec.wait_ge(rstd_step, 2 * b + 2)
                vec.wait_ge(x1_stored, 16 * b)
                for blk in range(NB):
                    last = vec.tensor_scalar(x1[:, blk, :], resid[:, blk, :], mv[:, blk, 0:1], rstd[:, blk:blk + 1],
                                             ALU.subtract, ALU.mult)
                last.then_inc(x1_ready, 1)

            def sequence(b, par):
                for g in range(PAIRS):
                    if g == 3 and has(b, -1):
                        scale_x1(b - 1)
                    if g == 1 and has(b, 1):
                        keep_z(b + 1)
                    if g == 4 and has(b, 1):
                        split_c(b + 1)
                    weigh(b, g)
                    if exists(b, g, 1):
                        before, _, pair = back(b, par, g, 1)
                        normalise(before, pair)
                    if g == 1 and has(b, -1):
                        add_residual(b - 1)
                    if has(b, 1):
                        finish_qk(b + 1, g)
                if has(b, 2):
                    x_lo(b + 2)

            x_lo(0)
            for g in range(PAIRS):
                finish_qk(0, g)
            keep_z(0)
            split_c(0)
            x_lo(1)
            all_sequences(vec, sequence)
            normalise(B - 1, PAIRS - 1)
            add_residual(B - 1)
            scale_x1(B - 1)

        @block.tensor
        def _(pe):
            pe.wait_ge(consts_ready, 1)

            def split_product(out, pairs):
                steps = [(lh, rh, ll, rl) for (lh, ll), (rh, rl) in pairs]
                todo = [p for lh, rh, ll, rl in steps for p in ((lh, rh), (lh, rl), (ll, rh))]
                for n, (l, r) in enumerate(todo):
                    mm = pe.matmul(out, l, r, start=(n == 0), stop=(n == len(todo) - 1))
                return mm

            def turn_x(b):
                pe.wait_ge(x_in_loaded, 16 * (b + 1))
                pe.wait_ge(v_done, VU * b)
                for k in range(KC):
                    for blk in range(NB):
                        mm = pe.transpose(ps_mix[:, k * N + blk * P:k * N + (blk + 1) * P],
                                          x_in[:, blk, k * P:(k + 1) * P], ident[:])
                mm.then_inc(xT_made, 1)

            def project_qk(b, g):
                pe.wait_ge(x_lo_done, b + 1)
                pe.wait_ge(qk_done, b * PAIRS + g)
                cols = slice(g * P, (g + 1) * P)
                for n in range(2):
                    mm = split_product(ps_qk[:, n, :], [
                        ((w_hi[n][:, k, cols], w_lo[n][:, k, cols]), (xT_hi[:, k, :], xT_lo[:, k, :]))
                        for k in range(KC)])
                mm.then_inc(qk_made, 1)

            def project_z(b):
                pe.wait_ge(x_lo_done, b + 1)
                for blk in range(NB):
                    rows = slice(blk * P, (blk + 1) * P)
                    todo = []
                    for k in range(KC):
                        todo += [(xT_hi[:, k, rows], wa_hi[:, k, :]), (xT_hi[:, k, rows], wa_lo[:, k, :]),
                                 (xT_lo[:, k, rows], wa_hi[:, k, :])]
                    for n, (l, r) in enumerate(todo):
                        pe.matmul(c_view[:, blk, :], l, r, start=(n == 0), stop=False)
                    mm = pe.matmul(c_view[:, blk, :], ones[0:1, :], ba_shift[:], start=False, stop=True)
                mm.then_inc(z_made, 1)

            def sum_decay(b):
                pe.wait_ge(dec_done, b + 1)
                pe.matmul(c_view[:, 0, :], upto[:], dec[:, 0, :], start=True, stop=True)
                for blk in range(1, NB):
                    for j in range(blk):
                        pe.matmul(c_view[:, blk, :], ones[:], dec[:, j, :], start=(j == 0), stop=False)
                    mm = pe.matmul(c_view[:, blk, :], upto[:], dec[:, blk, :], start=False, stop=True)
                mm.then_inc(c_made, 1)

            def turn_c(b):
                pe.wait_ge(c_split, b + 1)
                pe.sem_inc(pe_turns, 1)
                for blk in range(NB):
                    mm = pe.transpose(cT_view[0:CP, blk * P:(blk + 1) * P],
                                      c_parts[:, blk, :, :].rearrange("p t h -> p (t h)"), ident_bf[:])
                mm.then_inc(cT_made, 1)

            def project_v(b, half, blk):
                if (half, blk) == (0, 0):
                    pe.wait_ge(cT_kept, b + 1)
                pe.wait_ge(v_done, VU * b + half * NB + blk)
                rows, cols = slice(blk * P, (blk + 1) * P), slice(half * HALF, (half + 1) * HALF)
                split_product(ps_mix[:], [
                    ((xT_hi[:, k, rows], xT_lo[:, k, rows]), (w_hi[2][:, k, cols], w_lo[2][:, k, cols]))
                    for k in range(KC)]).then_inc(v_made, 1)

            def spread_c(b, g):
                pe.wait_ge(c_switched, 2 * b + 2)
                pe.wait_ge(decay_exp[1], b * PAIRS + g)
                for h in range(2):
                    mm = pe.matmul(ps_c[:, h, :], pick_head[:, 2 * g + h, :], cT_now[:], start=True, stop=True)
                mm.then_inc(c_spread, 1)

            def score(b, g):
                pe.wait_ge(qk_done, b * PAIRS + g + 1)
                for h in range(2):
                    pe.wait_ge(probs_done[h], b * PAIRS + g)
                    rows = slice(h * DH, (h + 1) * DH)
                    pe.matmul(ps_s[h][:, 0:N], qk[g][rows, 1, 0:P], qk[g][rows, 0, :], start=True, stop=True)
                    mm = pe.matmul(ps_s[h][:, N:TRI], qk[g][rows, 1, P:N], qk[g][rows, 0, P:N], start=True, stop=True)
                mm.then_inc(s_made, 1)

            def weighted_values(b, par, g):
                pe.wait_ge(v_done, VU * (b + 1))
                pe.wait_ge(o_normed, b * PAIRS + g)
                for h in range(2):
                    pe.wait_ge(probs_done[h], b * PAIRS + g + 1)
                    v = [v_aug[par][:, j, 2 * g + h, :] for j in range(NB)]
                    pe.matmul(o_view[:, 0, h, :], probs[h][:, 0:P], v[0], start=True, stop=True)
                    pe.matmul(o_view[:, 1, h, :], probs[h][:, P:N], v[0], start=True, stop=False)
                    mm = pe.matmul(o_view[:, 1, h, :], probs[h][:, N:TRI], v[1], start=False, stop=True)
                mm.then_inc(o_made, 1)

            def turn_o(b, g):
                pe.wait_ge(o_normed, b * PAIRS + g + 1)
                pe.wait_ge(oT_kept, b * PAIRS + g)
                for blk in range(NB):
                    mm = pe.transpose(ps_t[:, blk * P:(blk + 1) * P],
                                      o_norm[:, blk, :, :].rearrange("p h d -> p (h d)"), ident[:])
                mm.then_inc(oT_made, 1)

            def add_y(b, g):
                if g == 0:
                    pe.wait_ge(resid_done, b)
                pe.wait_ge(oT_kept, b * PAIRS + g + 1)
                for blk in range(NB):
                    mm = pe.matmul(ps_y[:, blk, :], oT[:, blk * P:(blk + 1) * P], wo_sb[:, g, :],
                                   start=(g == 0 and blk == 0), stop=(g == PAIRS - 1), skip_group_check=True)
                mm.then_inc(y_added, 1)

            def sequence(b, par):
                for g in range(PAIRS):
                    two_back, one_back = exists(b, g, 2), exists(b, g, 1)
                    before, _, pair = back(b, par, g, 2)
                    if two_back:
                        turn_o(before, pair)
                    spread_c(b, g)
                    score(b, g)
                    if has(b, 1) and g == 6:
                        project_v(b + 1, 0, 1)
                    if has(b, 1) and g == PAIRS - 1:
                        project_v(b + 1, 1, 1)
                    if one_back:
                        weighted_values(*back(b, par, g, 1))
                    if two_back:
                        add_y(before, pair)
                    if has(b, 1):
                        project_qk(b + 1, g)
                        if g == 0:
                            project_z(b + 1)
                        if g == 3:
                            sum_decay(b + 1)
                        if g == 4:
                            turn_c(b + 1)
                        if g == 5:
                            project_v(b + 1, 0, 0)
                        if g == 6:
                            project_v(b + 1, 1, 0)
                if has(b, 2):
                    turn_x(b + 2)

            pe.wait_ge(w_lo_done, 5)
            pe.wait_ge(small_loaded, 48)
            turn_x(0)
            for g in range(PAIRS):
                project_qk(0, g)
            project_z(0)
            sum_decay(0)
            turn_c(0)
            for half in range(2):
                for blk in range(NB):
                    project_v(0, half, blk)
            turn_x(1)
            all_sequences(pe, sequence)
            turn_o(B - 1, PAIRS - 2)
            weighted_values(B - 1, (B - 1) % 2, PAIRS - 1)
            add_y(B - 1, PAIRS - 2)
            turn_o(B - 1, PAIRS - 1)
            add_y(B - 1, PAIRS - 1)


def cross_attention(nc, sh, x1_dram, ctx_in, mask, wq, bq, wk, bk, wv, bv, wo, bo, router_w, x2_all, logits):
    B, N, D, H, NB, KC, S2, E = sh.B, sh.N, sh.D, sh.H, sh.NB, sh.KC, sh.S2, sh.E
    DK = D // H
    TH = P // DK
    G = 4
    GROUPS = H // G
    HALVES = TH // G
    GW = G * S2
    SCALE = float(DK) ** -0.5
    MASKED, OPEN = -1.0e9, 3.0e38
    with ExitStack() as ctx:
        def sb(name, shape, dt=F32):
            return ctx.enter_context(nc.sbuf_tensor(name, shape, dt))

        def ps(name, shape, dt=F32):
            return ctx.enter_context(nc.psum_tensor(name, shape, dt))

        def sem(name):
            return sh.semaphore(nc, name)

        ident, head_mask = sb("b_ident", [P, P]), sb("b_head_mask", [P, TH])
        w_raw = [sb(f"b_w_raw{n}", [P, KC, D]) for n in range(4)]
        wT = [sb(f"b_wT{n}", [P, KC, D]) for n in range(4)]
        wqT, wkT, wvT, woT = wT
        bq_col, bk_col = sb("b_bq_col", [P, KC]), sb("b_bk_col", [P, KC])
        bv_rows, bo_rows = sb("b_bv_rows", [P, D]), sb("b_bo_rows", [P, D])
        eps_col = sb("b_eps_col", [P, 1])
        x_in, x_res, x_bo = sb("b_x_in", [P, NB, D]), sb("b_x_res", [P, NB, D]), sb("b_x_bo", [P, NB, D])
        ctx_rows, ctxT = sb("b_ctx_rows", [P, D]), sb("b_ctxT", [P, KC, S2])
        mask_in, mask_cap = sb("b_mask_in", [P, NB, S2], I32), sb("b_mask_cap", [P, NB, S2])
        xT, qT, v = sb("b_xT", [P, KC, N]), sb("b_qT", [P, KC, N]), sb("b_v", [P, D])
        k_blocks = sb("b_k_blocks", [P, KC, TH, S2])
        probs = [sb(f"b_probs{n}", [P, H, S2]) for n in range(NB)]
        top = [sb(f"b_top{n}", [P, H]) for n in range(NB)]
        den = [sb(f"b_den{n}", [P, H]) for n in range(NB)]
        rden = [sb(f"b_rden{n}", [P, H]) for n in range(NB)]
        pT = [sb(f"b_pT{n}", [P, G, P]) for n in range(2)]
        o_norm = [sb(f"b_o_norm{n}", [P, D]) for n in range(NB)]
        oT = sb("b_oT", [P, KC, P])
        resid = sb("b_resid", [P, NB, D])
        stats, mv = sb("b_stats", [P, NB, 6]), sb("b_mv", [P, NB, 2])
        ln_var, rstd = sb("b_ln_var", [P, NB]), sb("b_rstd", [P, NB])
        x2, x2T = sb("b_x2", [P, NB, D]), sb("b_x2T", [P, KC, N])
        rw_rows, rwT = sb("b_rw_rows", [E, D]), sb("b_rwT", [P, KC, E])

        ps_s = ps("b_ps_s", [P, GROUPS, 512])
        ps_o_turns = ps("b_ps_o_turns", [P, 512])
        ps_mix = ps("b_ps_mix", [P, 512])
        ps_t = ps("b_ps_t", [P, G, P])
        ps_o = ps("b_ps_o", [P, 512])
        ps_oT = ps_y = ps_o_turns[:, 0:D]
        ps_lg = ps_o_turns[:, 0:NB * E].rearrange("p (n e) -> p n e", n=NB)
        ps_cT = ps_s[:, 0, 0:KC * S2].rearrange("p (k n) -> p k n", k=KC)
        ps_k = ps_s[:, 1, 0:KC * S2].rearrange("p (k n) -> p k n", k=KC)
        mix_rows = ps_mix[:].rearrange("p (k n) -> p k n", k=KC)

        loaded, consts_step, consts_ready = sem("b_loaded"), sem("b_consts_step"), sem("b_consts_ready")
        w_turned, w_kept = sem("b_w_turned"), sem("b_w_kept")
        x_in_loaded, x_res_loaded = sem("b_x_in_loaded"), sem("b_x_res_loaded")
        ctx_loaded, mask_loaded, x2_stored = sem("b_ctx_loaded"), sem("b_mask_loaded"), sem("b_x2_stored")
        vec_turns, pe_turns = sem("b_vec_turns"), sem("b_pe_turns")
        cap_step, cap_ready = sem("b_cap_step"), sem("b_cap_ready")
        xT_made, cT_made, q_made, k_made = sem("b_xT_made"), sem("b_cT_made"), sem("b_q_made"), sem("b_k_made")
        xT_kept, cT_kept, q_kept, k_kept = sem("b_xT_kept"), sem("b_cT_kept"), sem("b_q_kept"), sem("b_k_kept")
        v_made, x2T_made, lg_made = sem("b_v_made"), sem("b_x2T_made"), sem("b_lg_made")
        v_kept, x2T_kept, lg_kept = sem("b_v_kept"), sem("b_x2T_kept"), sem("b_lg_kept")
        x_bo_done, ln_step, var_ready, rstd_step, x2_ready = (
            sem("b_x_bo_done"), sem("b_ln_step"), sem("b_var_ready"), sem("b_rstd_step"), sem("b_x2_ready"))
        s_made, s_kept, top_done, shifted = sem("b_s_made"), sem("b_s_kept"), sem("b_top_done"), sem("b_shifted")
        exp_done, den_done, rden_done = sem("b_exp_done"), sem("b_den_done"), sem("b_rden_done")
        o_normed, oT_made, oT_kept, y_made, y_kept = (
            sem("b_o_normed"), sem("b_oT_made"), sem("b_oT_kept"), sem("b_y_made"), sem("b_y_kept"))
        pT_made, pT_kept, pT_used = sem("b_pT_made"), sem("b_pT_kept"), sem("b_pT_used")

        block = ctx.enter_context(nc.Block())
        x1_rows = x1_dram.rearrange("b (k p) d -> b p k d", p=P)
        mask_rows = mask.rearrange("b (k p) s -> b p k s", p=P)
        N_LOADS = 5 + 2 + 2

        def unit(b, blk):
            return b * NB + blk

        def all_sequences(eng, sequence):
            sequence(0, True, False)
            with eng.Fori(1, B - 1) as b:
                sequence(b, False, False)
            sequence(B - 1, False, True)

        @block.sync
        def _(sp):
            def load_x(b):
                sp.wait_ge(xT_made, b)
                sp.dma_start(x_in[:], x1_rows[b]).then_inc(x_in_loaded, 16)

            def load_ctx(b):
                sp.wait_ge(cT_made, b)
                sp.dma_start(ctx_rows[0:S2, :], ctx_in[b]).then_inc(ctx_loaded, 16)

            def load_mask(b):
                sp.wait_ge(cap_ready, b)
                sp.dma_start(mask_in[:], mask_rows[b]).then_inc(mask_loaded, 16)

            def load_residual(b):
                sp.wait_ge(x_bo_done, b)
                sp.dma_start(x_res[:], x1_rows[b]).then_inc(x_res_loaded, 16)

            def store_x2(b):
                sp.wait_ge(x2_ready, b + 1)
                sp.dma_start(x2_all[:, bass.ts(b, NB), :], x2[:]).then_inc(x2_stored, 16)

            sp.dma_start(x_in[:], x1_rows[0]).then_inc(x_in_loaded, 16)
            sp.dma_start(ctx_rows[0:S2, :], ctx_in[0]).then_inc(ctx_loaded, 16)
            for n, w in enumerate((wq, wk, wv, wo)):
                sp.dma_start(w_raw[n][:], w.rearrange("(k p) n -> p k n", p=P)).then_inc(loaded, 16)
            sp.dma_start(rw_rows[:], router_w).then_inc(loaded, 16)
            for col, b_in in ((bq_col, bq), (bk_col, bk)):
                sp.dma_start(col[:], b_in.rearrange("(k p) -> p k", p=P), allow_slow_non_contiguous=True)\
                    .then_inc(loaded, 16)
            for rows, b_in in ((bv_rows, bv), (bo_rows, bo)):
                sp.dma_start(rows[:], b_in.rearrange("(a n) -> a n", a=1).to_broadcast([P, D])).then_inc(loaded, 16)
            sp.dma_start(mask_in[:], mask_rows[0]).then_inc(mask_loaded, 16)
            sp.dma_start(x_res[:], x1_rows[0]).then_inc(x_res_loaded, 16)
            load_x(1)
            load_ctx(1)
            load_mask(1)
            load_residual(1)

            def sequence(b):
                load_x(b + 1)
                load_ctx(b + 1)
                load_mask(b + 1)
                load_residual(b + 1)
                store_x2(b - 1)

            with sp.Fori(1, B - 1) as b:
                sequence(b)
            store_x2(B - 2)
            store_x2(B - 1)
            sp.wait_ge(x2_stored, 16 * B)

        @block.gpsimd
        def _(pool):
            pool.memset(ident[:], 0.0).then_inc(consts_step, 1)
            pool.memset(head_mask[:], 1.0).then_inc(consts_step, 1)
            pool.wait_ge(consts_step, 2)
            pool.affine_select(out=ident[:], in_=ident[:], compare_op=ALU.not_equal, fill=1.0, base=0,
                               pattern=[[-1, P]], channel_multiplier=1).then_inc(consts_step, 1)
            pool.affine_select(out=head_mask[:], in_=head_mask[:], compare_op=ALU.is_ge, fill=0.0, base=0,
                               pattern=[[-DK, TH]], channel_multiplier=1).then_inc(consts_step, 1)
            pool.wait_ge(consts_step, 4)
            pool.affine_select(out=head_mask[:], in_=head_mask[:], compare_op=ALU.is_ge, fill=0.0, base=DK - 1,
                               pattern=[[DK, TH]], channel_multiplier=-1).then_inc(consts_step, 1)
            pool.memset(eps_col[:], LN_EPS).then_inc(consts_step, 1)
            pool.wait_ge(consts_step, 6)
            pool.memset(x_bo[:], 0.0).then_inc(consts_ready, 1)
            pool.wait_ge(loaded, 16 * N_LOADS)
            pool.wait_ge(consts_ready, 1)

            def add_bias(b, first):
                pool.wait_ge(x_res_loaded, 16 * (b + 1))
                if not first:
                    pool.wait_ge(y_kept, unit(b, 0))
                pool.tensor_tensor(x_bo[:], x_res[:], bo_rows[:].unsqueeze(1).to_broadcast([P, NB, D]), ALU.add)\
                    .then_inc(x_bo_done, 1)

            def shift(b, blk):
                pool.wait_ge(top_done, unit(b, blk) + 1)
                pool.tensor_tensor(probs[blk][:], probs[blk][:], top[blk][:].unsqueeze(2).to_broadcast([P, H, S2]),
                                   ALU.subtract).then_inc(shifted, 1)

            def sequence(b, first, last):
                shift(b, 1)
                add_bias(b, first)
                if not last:
                    shift(b + 1, 0)

            shift(0, 0)
            all_sequences(pool, sequence)

        @block.scalar
        def _(act):
            act.wait_ge(loaded, 16 * N_LOADS)
            act.wait_ge(consts_ready, 1)
            for n in range(4):
                for k in range(KC):
                    act.wait_ge(w_turned, n * KC + k + 1)
                    act.copy(wT[n][:, k, :], (ps_o_turns, ps_mix)[k][:, 0:D]).then_inc(w_kept, 1)
            act.wait_ge(w_turned, 4 * KC + 1)
            act.copy(rwT[:], ps_t[:, 0, 0:KC * E].rearrange("p (k e) -> p k e", k=KC)).then_inc(w_kept, 1)

            def keep_xT(b):
                act.wait_ge(xT_made, b + 1)
                act.copy(xT[:], mix_rows).then_inc(xT_kept, 1)

            def keep_ctxT(b):
                act.wait_ge(cT_made, b + 1)
                act.copy(ctxT[:], ps_cT).then_inc(cT_kept, 1)

            def keep_q(b):
                act.wait_ge(q_made, b + 1)
                for k in range(KC):
                    ins = act.activation(qT[:, k, :], mix_rows[:, k, :], ACT.Identity, bias=bq_col[:, k:k + 1])
                ins.then_inc(q_kept, 1)

            def keep_x2T(b):
                act.wait_ge(x2T_made, b + 1)
                act.copy(x2T[:], mix_rows).then_inc(x2T_kept, 1)

            def exponentials(b, blk):
                act.wait_ge(shifted, unit(b, blk) + 1)
                act.activation(probs[blk][:], probs[blk][:], ACT.Exp).then_inc(exp_done, 1)

            def keep_pT(b, blk, g):
                n = unit(b, blk) * GROUPS + g
                act.wait_ge(pT_made, n + 1)
                if not isinstance(n, int) or n >= 2:
                    act.wait_ge(pT_used, n - 1)
                act.copy(pT[g % 2][0:S2, :, :], ps_t[0:S2, :, :]).then_inc(pT_kept, 1)

            def root(b):
                act.wait_ge(var_ready, b + 1)
                act.activation(ln_var[:], mv[:, :, 1], ACT.Ln, bias=eps_col[:]).then_inc(rstd_step, 1)
                act.wait_ge(rstd_step, 2 * b + 1)
                act.activation(rstd[:], ln_var[:], ACT.Exp, scale=-0.5).then_inc(rstd_step, 1)

            def sequence(b, first, last):
                if not last:
                    keep_xT(b + 1)
                for g in range(GROUPS):
                    keep_pT(b, 0, g)
                    if not last and g == 1:
                        keep_ctxT(b + 1)
                    if not last and g == 2:
                        keep_q(b + 1)
                exponentials(b, 1)
                if not first:
                    root(b - 1)
                for g in range(GROUPS):
                    keep_pT(b, 1, g)
                    if not first and g == 3:
                        keep_x2T(b - 1)
                if not last:
                    exponentials(b + 1, 0)

            keep_xT(0)
            keep_ctxT(0)
            keep_q(0)
            exponentials(0, 0)
            all_sequences(act, sequence)
            root(B - 1)
            keep_x2T(B - 1)

        @block.vector
        def _(vec):
            vec.wait_ge(loaded, 16 * N_LOADS)
            vec.wait_ge(consts_ready, 1)

            def keep_k(b):
                vec.wait_ge(k_made, b + 1)
                for k in range(KC):
                    ins = vec.scalar_tensor_tensor(
                        k_blocks[:, k, :, :], ps_k[:, k, :].unsqueeze(1).to_broadcast([P, TH, S2]), bk_col[:, k:k + 1],
                        head_mask[:].unsqueeze(2).to_broadcast([P, TH, S2]), ALU.add, ALU.mult)
                ins.then_inc(k_kept, 1)

            def keep_v(b):
                vec.wait_ge(v_made, b + 1)
                vec.tensor_tensor(v[0:S2, :], ps_mix[0:S2, 0:D], bv_rows[0:S2, :], ALU.add).then_inc(v_kept, 1)

            def mask_caps(b):
                vec.wait_ge(mask_loaded, 16 * (b + 1))
                if not isinstance(b, int) or b:
                    vec.wait_ge(s_kept, unit(b, 0))
                vec.tensor_scalar(mask_cap[:], mask_in[:], 0.0, OPEN, ALU.not_equal, ALU.mult).then_inc(cap_step, 1)
                vec.wait_ge(cap_step, b + 1)
                vec.tensor_scalar(mask_cap[:], mask_cap[:], MASKED, None, ALU.add).then_inc(cap_ready, 1)

            def keep_scores(b, blk):
                n = unit(b, blk)
                vec.wait_ge(s_made, n + 1)
                vec.wait_ge(cap_ready, b + 1)
                if not isinstance(n, int) or n >= NB:
                    vec.wait_ge(pT_made, (n - NB + 1) * GROUPS)
                    vec.wait_ge(den_done, n - NB + 1)
                for g in range(GROUPS):
                    ins = vec.scalar_tensor_tensor(
                        probs[blk][:, g * G:(g + 1) * G, :], ps_s[:, g, 0:GW].rearrange("p (h k) -> p h k", h=G), SCALE,
                        mask_cap[:, blk, :].unsqueeze(1).to_broadcast([P, G, S2]), ALU.mult, ALU.min)
                ins.then_inc(s_kept, 1)
                vec.wait_ge(s_kept, n + 1)
                vec.tensor_reduce(top[blk][:], probs[blk][:], AX.X, ALU.max).then_inc(top_done, 1)

            def sums(b, blk):
                n = unit(b, blk)
                vec.wait_ge(exp_done, n + 1)
                vec.tensor_reduce(den[blk][:], probs[blk][:], AX.X, ALU.add).then_inc(den_done, 1)
                vec.wait_ge(den_done, n + 1)
                vec.reciprocal(rden[blk][:], den[blk][:]).then_inc(rden_done, 1)

            def normalise(b, blk):
                n = unit(b, blk)
                vec.wait_ge(pT_used, (n + 1) * GROUPS)
                vec.wait_ge(rden_done, n + 1)
                if not isinstance(n, int) or n >= NB:
                    vec.wait_ge(oT_made, n - NB + 1)
                vec.tensor_tensor(o_norm[blk][:].rearrange("p (h d) -> p h d", d=DK),
                                  ps_o[:, 0:D].rearrange("p (h d) -> p h d", d=DK),
                                  rden[blk][:].unsqueeze(2).to_broadcast([P, H, DK]), ALU.mult).then_inc(o_normed, 1)

            def keep_oT(b, blk):
                vec.wait_ge(oT_made, unit(b, blk) + 1)
                vec.tensor_copy(oT[:], ps_oT.rearrange("p (k n) -> p k n", k=KC)).then_inc(oT_kept, 1)

            def add_residual(b, blk):
                vec.wait_ge(x_bo_done, b + 1)
                vec.wait_ge(y_made, unit(b, blk) + 1)
                if blk == 0 and (not isinstance(b, int) or b):
                    vec.wait_ge(x2_ready, b)
                vec.tensor_tensor(resid[:, blk, :], ps_y, x_bo[:, blk, :], ALU.add).then_inc(y_kept, 1)

            def statistics(b):
                vec.wait_ge(y_kept, unit(b, NB))
                for blk in range(NB):
                    vec.bn_stats(stats[:, blk, :], resid[:, blk, :]).then_inc(ln_step, 1)
                vec.wait_ge(ln_step, NB * b + NB)
                vec.sem_inc(vec_turns, 1)
                for blk in range(NB):
                    ins = vec.bn_aggr(mv[:, blk, :], stats[:, blk, :])
                ins.then_inc(var_ready, 1)

            def scale_x2(b):
                vec.wait_ge(rstd_step, 2 * b + 2)
                if not isinstance(b, int) or b:
                    vec.wait_ge(x2_stored, 16 * b)
                    vec.wait_ge(x2T_made, b)
                for blk in range(NB):
                    ins = vec.tensor_scalar(x2[:, blk, :], resid[:, blk, :], mv[:, blk, 0:1], rstd[:, blk:blk + 1],
                                            ALU.subtract, ALU.mult)
                ins.then_inc(x2_ready, 1)

            def keep_logits(b):
                vec.wait_ge(lg_made, b + 1)
                vec.tensor_copy(logits[:, bass.ts(b, NB), :], ps_lg).then_inc(lg_kept, 1)

            def sequence(b, first, last):
                if not first:
                    keep_oT(b - 1, 1)
                keep_scores(b, 1)
                if not last:
                    mask_caps(b + 1)
                sums(b, 0)
                if not first:
                    add_residual(b - 1, 1)
                    statistics(b - 1)
                if not last:
                    keep_k(b + 1)
                normalise(b, 0)
                keep_oT(b, 0)
                if not last:
                    keep_scores(b + 1, 0)
                if not first:
                    scale_x2(b - 1)
                sums(b, 1)
                add_residual(b, 0)
                normalise(b, 1)
                if not first:
                    keep_logits(b - 1)
                if not last:
                    keep_v(b + 1)

            mask_caps(0)
            keep_k(0)
            keep_v(0)
            keep_scores(0, 0)
            all_sequences(vec, sequence)
            keep_oT(B - 1, 1)
            add_residual(B - 1, 1)
            statistics(B - 1)
            scale_x2(B - 1)
            keep_logits(B - 1)

        @block.tensor
        def _(pe):
            pe.wait_ge(loaded, 16 * N_LOADS)
            pe.wait_ge(consts_ready, 1)
            for n in range(4):
                for k in range(KC):
                    if n:
                        pe.wait_ge(w_kept, (n - 1) * KC + k + 1)
                    for o in range(KC):
                        mm = pe.transpose((ps_o_turns, ps_mix)[k][:, o * P:(o + 1) * P], w_raw[n][:, o, k * P:(k + 1) * P], ident[:])
                    mm.then_inc(w_turned, 1)
            for k in range(KC):
                mm = pe.transpose(ps_t[:, 0, k * E:(k + 1) * E], rw_rows[:, k * P:(k + 1) * P], ident[0:E, 0:E])
            mm.then_inc(w_turned, 1)
            pe.wait_ge(w_kept, 4 * KC + 1)

            def turn_x1(b):
                pe.wait_ge(x_in_loaded, 16 * (b + 1))
                if not isinstance(b, int) or b:
                    pe.wait_ge(v_kept, b)
                for k in range(KC):
                    for blk in range(NB):
                        mm = pe.transpose(mix_rows[:, k, blk * P:(blk + 1) * P], x_in[:, blk, k * P:(k + 1) * P], ident[:])
                mm.then_inc(xT_made, 1)

            def turn_ctx(b):
                pe.wait_ge(ctx_loaded, 16 * (b + 1))
                if not isinstance(b, int) or b:
                    pe.wait_ge(s_kept, unit(b, 0))
                for k in range(KC):
                    pe.sem_inc(pe_turns, 1)
                    mm = pe.transpose(ps_cT[:, k, :], ctx_rows[0:S2, k * P:(k + 1) * P], ident[0:S2, 0:S2])
                mm.then_inc(cT_made, 1)

            def project_qk(b):
                pe.wait_ge(xT_kept, b + 1)
                for t in range(KC):
                    for k in range(KC):
                        mm = pe.matmul(mix_rows[:, t, :], wqT[:, k, t * P:(t + 1) * P], xT[:, k, :],
                                       start=(k == 0), stop=(k == KC - 1))
                mm.then_inc(q_made, 1)
                pe.wait_ge(cT_kept, b + 1)
                for t in range(KC):
                    for k in range(KC):
                        mm = pe.matmul(ps_k[:, t, :], wkT[:, k, t * P:(t + 1) * P], ctxT[:, k, :],
                                       start=(k == 0), stop=(k == KC - 1))
                mm.then_inc(k_made, 1)

            def project_v(b):
                pe.wait_ge(q_kept, b + 1)
                if not isinstance(b, int) or b >= 2:
                    pe.wait_ge(x2T_kept, b - 1)
                for k in range(KC):
                    mm = pe.matmul(ps_mix[0:S2, 0:D], ctxT[:, k, :], wvT[:, k, :], start=(k == 0), stop=(k == KC - 1))
                mm.then_inc(v_made, 1)

            def score(b, blk):
                n = unit(b, blk)
                pe.wait_ge(q_kept, b + 1)
                pe.wait_ge(k_kept, b + 1)
                if not isinstance(n, int) or n:
                    pe.wait_ge(s_kept, n)
                for g in range(GROUPS):
                    t, half = g // HALVES, g % HALVES
                    mm = pe.matmul(ps_s[:, g, 0:GW], qT[:, t, blk * P:(blk + 1) * P],
                                   k_blocks[:, t, half * G:(half + 1) * G, :].rearrange("p h k -> p (h k)"),
                                   start=True, stop=True)
                mm.then_inc(s_made, 1)

            def turn_probs(b, blk, g):
                n = unit(b, blk) * GROUPS + g
                if g == 0:
                    pe.wait_ge(exp_done, unit(b, blk) + 1)
                if not isinstance(n, int) or n:
                    pe.wait_ge(pT_kept, n)
                for s in range(G):
                    mm = pe.transpose(ps_t[0:S2, s, :], probs[blk][:, g * G + s, :], ident[:])
                mm.then_inc(pT_made, 1)

            def weigh_values(b, blk, g):
                n = unit(b, blk)
                if g == 0:
                    pe.wait_ge(v_kept, b + 1)
                    if not isinstance(n, int) or n:
                        pe.wait_ge(o_normed, n)
                pe.wait_ge(pT_kept, n * GROUPS + g + 1)
                for s in range(G):
                    h = g * G + s
                    mm = pe.matmul(ps_o[:, h * DK:(h + 1) * DK], pT[g % 2][0:S2, s, :],
                                   v[0:S2, h * DK:(h + 1) * DK], start=True, stop=True)
                mm.then_inc(pT_used, 1)

            def turn_o(b, blk):
                n = unit(b, blk)
                pe.wait_ge(o_normed, n + 1)
                if not isinstance(n, int) or n:
                    pe.wait_ge(y_kept, n)
                if blk == 1 and (not isinstance(b, int) or b):
                    pe.wait_ge(lg_kept, b)
                for k in range(KC):
                    mm = pe.transpose(ps_oT[:, k * P:(k + 1) * P], o_norm[blk][:, k * P:(k + 1) * P], ident[:])
                mm.then_inc(oT_made, 1)

            def project_o(b, blk):
                n = unit(b, blk)
                pe.wait_ge(oT_kept, n + 1)
                for k in range(KC):
                    mm = pe.matmul(ps_y, oT[:, k, :], woT[:, k, :], start=(k == 0), stop=(k == KC - 1))
                mm.then_inc(y_made, 1)

            def turn_x2(b):
                pe.wait_ge(x2_ready, b + 1)
                if not isinstance(b, int) or b < B - 2:
                    pe.wait_ge(q_kept, b + 3)
                elif b == B - 1:
                    pe.wait_ge(x2T_kept, b)
                for k in range(KC):
                    for blk in range(NB):
                        mm = pe.transpose(mix_rows[:, k, blk * P:(blk + 1) * P], x2[:, blk, k * P:(k + 1) * P], ident[:])
                mm.then_inc(x2T_made, 1)

            def route(b):
                pe.wait_ge(x2T_kept, b + 1)
                pe.wait_ge(y_kept, unit(b, 3) if not isinstance(b, int) or b < B - 1 else unit(B, 0))
                for blk in range(NB):
                    for k in range(KC):
                        mm = pe.matmul(ps_lg[:, blk, :], x2T[:, k, blk * P:(blk + 1) * P], rwT[:, k, :],
                                       start=(k == 0), stop=(k == KC - 1))
                mm.then_inc(lg_made, 1)

            def sequence(b, first, last):
                score(b, 1)
                if not first:
                    turn_o(b - 1, 1)
                if not last:
                    turn_x1(b + 1)
                turn_probs(b, 0, 0)
                if not first:
                    project_o(b - 1, 1)
                for g in range(1, GROUPS):
                    turn_probs(b, 0, g)
                    weigh_values(b, 0, g - 1)
                    if not last and g == 1:
                        turn_ctx(b + 1)
                    if not last and g == 2:
                        project_qk(b + 1)
                weigh_values(b, 0, GROUPS - 1)
                if not last:
                    score(b + 1, 0)
                turn_o(b, 0)
                turn_probs(b, 1, 0)
                project_o(b, 0)
                for g in range(1, GROUPS):
                    turn_probs(b, 1, g)
                    weigh_values(b, 1, g - 1)
                    if not first and g == 3:
                        turn_x2(b - 1)
                weigh_values(b, 1, GROUPS - 1)
                if not first:
                    route(b - 1)
                if not last:
                    project_v(b + 1)

            turn_x1(0)
            turn_ctx(0)
            project_qk(0)
            project_v(0)
            score(0, 0)
            all_sequences(pe, sequence)
            turn_o(B - 1, 1)
            project_o(B - 1, 1)
            turn_x2(B - 1)
            route(B - 1)


class Plan:

    def __init__(self, sh):
        self.T = 512
        self.SHIFT = self.T.bit_length() - 1
        self.TOKENS = sh.B * sh.N
        self.BLOCKS = self.TOKENS // P
        self.TILES = (2 * self.TOKENS - sh.E) // self.T + sh.E
        self.ROWS = self.TILES * self.T


def route_tokens(nc, sh, plan, logits, x2_all, x_sorted, slots, gates, tile_table):
    E, D = sh.E, sh.D
    NBK, T, TILES = plan.BLOCKS, plan.T, plan.TILES
    with ExitStack() as ctx:
        def sb(name, shape, dt=F32):
            return ctx.enter_context(nc.sbuf_tensor(name, shape, dt))

        def sem(name):
            return sh.semaphore(nc, name)

        shifted, probs, rest = sb("r_shifted", [P, NBK, E]), sb("r_probs", [P, NBK, E]), sb("r_rest", [P, NBK, E])
        same, key = sb("r_same", [P, NBK, E]), sb("r_key", [P, NBK, E])
        picked = [sb(f"r_picked{k}", [P, NBK, E]) for k in range(2)]
        both = sb("r_both", [P, NBK, E])
        top, tot = [sb(f"r_top{k}", [P, NBK]) for k in range(2)], sb("r_tot", [P, NBK])
        col, rcol = sb("r_col", [P, NBK]), sb("r_rcol", [P, NBK])
        order = sb("r_order", [P, E])
        order_i = sb("r_order_i", [P, E], I32)
        first_row = sb("r_first_row", [P, E])
        tile_no, tile_no_i = sb("r_tile_no", [P, TILES]), sb("r_tile_no_i", [P, TILES], I32)
        before, ones = sb("r_before", [P, P]), sb("r_ones", [P, P])
        sums = [sb(f"r_sums{k}", [P, NBK, E]) for k in range(2)]
        in_block, rank = sb("r_in_block", [P, NBK, E]), sb("r_rank", [P, NBK, E])
        slot_f = sb("r_slot_f", [P, NBK])
        tiles_i, n_tiles = sb("r_tiles_i", [P, E], I32), sb("r_n_tiles", [P, E])
        ends = [sb(f"r_ends{k}", [P, E]) for k in range(2)]
        expert_of = sb("r_expert_of", [P, TILES])
        ps_rank = ctx.enter_context(nc.psum_tensor("r_ps_rank", [P, 2, NBK * E], F32))

        consts_step, consts_ready, step = sem("r_consts_step"), sem("r_consts_ready"), sem("r_step")
        shifted_done, exp_done, picks_ready, ranked = (
            sem("r_shifted_done"), sem("r_exp_done"), sem("r_picks_ready"), sem("r_ranked"))
        slots_ready, scattered = sem("r_slots_ready"), sem("r_scattered")

        block = ctx.enter_context(nc.Block())

        @block.gpsimd
        def _(pool):
            pool.iota(order_i[:], pattern=[[-1, E]], base=E, channel_multiplier=0).then_inc(consts_step, 1)
            pool.iota(tile_no_i[:], pattern=[[1, TILES]], base=0, channel_multiplier=0).then_inc(consts_step, 1)
            pool.memset(ones[:], 1.0).then_inc(consts_step, 1)
            pool.wait_ge(consts_step, 3)
            pool.affine_select(out=before[:], in_=ones[:], compare_op=ALU.is_gt, fill=0.0, base=0,
                               pattern=[[1, P]], channel_multiplier=-1).then_inc(consts_ready, 1)
            pool.wait_ge(slots_ready, 2)
            for n in range(NBK):
                for k in range(2):
                    pool.indirect_dma_start(x_sorted, bass.IndirectOffsetOnAxis(slots[k][:, n:n + 1], 0),
                                            x2_all[:, n, :], None).then_inc(scattered, 16)
            pool.wait_ge(scattered, 16 * 2 * NBK)

        @block.scalar
        def _(act):
            act.wait_ge(shifted_done, 1)
            act.activation(probs[:], shifted[:], ACT.Exp).then_inc(exp_done, 1)

        @block.tensor
        def _(pe):
            pe.wait_ge(picks_ready, 1)
            pe.wait_ge(consts_ready, 1)
            flat = both[:].rearrange("p n e -> p (n e)")
            pe.matmul(ps_rank[:, 0, :], before[:], flat, start=True, stop=True)
            pe.matmul(ps_rank[:, 1, :], ones[:], flat, start=True, stop=True).then_inc(ranked, 1)

        @block.vector
        def _(vec):
            steps = [0]

            def link(ins):
                steps[0] += 1
                ins.then_inc(step, 1)
                vec.wait_ge(step, steps[0])

            def over(cols):
                return cols.unsqueeze(2).to_broadcast([P, NBK, E])

            def each_block(row):
                return row.unsqueeze(1).to_broadcast([P, NBK, E])

            vec.wait_ge(consts_ready, 1)
            link(vec.tensor_copy(order[:], order_i[:]))
            link(vec.tensor_copy(tile_no[:], tile_no_i[:]))
            link(vec.tensor_reduce(col[:], logits[:], AX.X, ALU.max))
            vec.tensor_tensor(shifted[:], logits[:], over(col[:]), ALU.subtract).then_inc(shifted_done, 1)
            vec.wait_ge(exp_done, 1)
            link(vec.tensor_reduce(col[:], probs[:], AX.X, ALU.add))
            link(vec.reciprocal(rcol[:], col[:]))
            link(vec.tensor_tensor(probs[:], probs[:], over(rcol[:]), ALU.mult))
            for k, left in ((0, probs), (1, rest)):
                link(vec.tensor_reduce(top[k][:], left[:], AX.X, ALU.max))
                link(vec.tensor_tensor(same[:], left[:], over(top[k][:]), ALU.is_equal))
                link(vec.tensor_tensor(key[:], same[:], each_block(order[:]), ALU.mult))
                link(vec.tensor_reduce(col[:], key[:], AX.X, ALU.max))
                link(vec.tensor_tensor(picked[k][:], key[:], over(col[:]), ALU.is_equal))
                if k == 0:
                    link(vec.scalar_tensor_tensor(rest[:], picked[0][:], -2.0, probs[:], ALU.mult, ALU.add))
            link(vec.tensor_tensor(both[:], picked[0][:], picked[1][:], ALU.add))
            vec.tensor_tensor(tot[:], top[0][:], top[1][:], ALU.add).then_inc(picks_ready, 1)
            vec.wait_ge(picks_ready, 1)
            link(vec.tensor_scalar(tot[:], tot[:], 1e-9, None, ALU.add))
            link(vec.reciprocal(rcol[:], tot[:]))
            for k in range(2):
                link(vec.tensor_tensor(gates[k][:], top[k][:], rcol[:], ALU.mult))
            vec.wait_ge(ranked, 1)
            link(vec.tensor_copy(in_block[:], ps_rank[:, 0, :].rearrange("p (n e) -> p n e", e=E)))
            link(vec.tensor_copy(sums[0][:], ps_rank[:, 1, :].rearrange("p (n e) -> p n e", e=E)))
            a, b = sums
            d = 1
            while d < NBK:
                link(vec.tensor_copy(b[:, 0:d, :], a[:, 0:d, :]))
                link(vec.tensor_tensor(b[:, d:NBK, :], a[:, d:NBK, :], a[:, 0:NBK - d, :], ALU.add))
                a, b = b, a
                d *= 2
            link(vec.tensor_tensor(rank[:], a[:], ps_rank[:, 1, :].rearrange("p (n e) -> p n e", e=E), ALU.subtract))
            link(vec.tensor_tensor(rank[:], rank[:], in_block[:], ALU.add))
            link(vec.tensor_scalar(n_tiles[:], a[:, NBK - 1, :], float(T - 1), None, ALU.add))
            link(vec.tensor_copy(tiles_i[:], n_tiles[:]))
            link(vec.tensor_scalar(tiles_i[:], tiles_i[:], plan.SHIFT, None, ALU.logical_shift_right))
            link(vec.tensor_copy(n_tiles[:], tiles_i[:]))
            a, b = ends
            link(vec.tensor_copy(a[:], n_tiles[:]))
            d = 1
            while d < E:
                link(vec.tensor_copy(b[:, 0:d], a[:, 0:d]))
                link(vec.tensor_tensor(b[:, d:E], a[:, d:E], a[:, 0:E - d], ALU.add))
                a, b = b, a
                d *= 2
            link(vec.tensor_tensor(first_row[:], a[:], n_tiles[:], ALU.subtract))
            link(vec.tensor_scalar(first_row[:], first_row[:], float(T), None, ALU.mult))
            link(vec.tensor_tensor(rank[:], rank[:], each_block(first_row[:]), ALU.add))
            for k in range(2):
                link(vec.tensor_tensor(key[:], picked[k][:], rank[:], ALU.mult))
                link(vec.tensor_reduce(slot_f[:], key[:], AX.X, ALU.add))
                vec.tensor_copy(slots[k][:], slot_f[:]).then_inc(slots_ready, 1)
                vec.wait_ge(slots_ready, k + 1)
            link(vec.tensor_scalar(expert_of[:], tile_no[:], a[:, 0:1], None, ALU.is_ge))
            for e in range(1, E - 1):
                link(vec.scalar_tensor_tensor(expert_of[:], tile_no[:], a[:, e:e + 1], expert_of[:], ALU.is_ge, ALU.add))
            link(vec.tensor_copy(tile_table[:], expert_of[0:1, :]))


def run_experts(nc, sh, plan, x_sorted, tile_table, gate_w, gate_b, up_w, up_b, down_w, down_b, y_sorted):
    E, D, FF, KC = sh.E, sh.D, sh.FF, sh.KC
    T, TILES = plan.T, plan.TILES
    TB, FC = T // P, FF // P
    with ExitStack() as ctx:
        def sb(name, shape, dt=F32):
            return ctx.enter_context(nc.sbuf_tensor(name, shape, dt))

        def ps(name, shape, dt=F32):
            return ctx.enter_context(nc.psum_tensor(name, shape, dt))

        def sem(name):
            return sh.semaphore(nc, name)

        def sems(name):
            return [sem(f"{name}{n}") for n in range(2)]

        ident = sb("e_ident", [P, P])
        bias_rows, bias_table = sb("e_bias_rows", [2 * E * FC, P]), sb("e_bias_table", [P, 2, E, FC])
        where = sb("e_where", [1, 2], I32)
        gu_raw = [sb(f"e_gu_raw{n}", [P, KC, 2 * FF]) for n in range(2)]
        dn_raw = [sb(f"e_dn_raw{n}", [P, FC, D]) for n in range(2)]
        gu_hi, gu_lo = ([sb(f"e_gu_{x}{n}", [P, KC, 2 * FF], F32R) for n in range(2)] for x in ("hi", "lo"))
        dn_hi, dn_lo = ([sb(f"e_dn_{x}{n}", [P, FC, D], F32R) for n in range(2)] for x in ("hi", "lo"))
        bias = [sb(f"e_bias{n}", [P, 2, FC]) for n in range(2)]
        dn_bias = [sb(f"e_dn_bias{n}", [P, D]) for n in range(2)]
        x_in = [sb(f"e_x_in{n}", [P, TB, D]) for n in range(2)]
        xT_hi, xT_lo = ([sb(f"e_xT_{x}{n}", [P, KC, T], F32R) for n in range(2)] for x in ("hi", "lo"))
        gate = [sb(f"e_gate{n}", [P, T]) for n in range(2)]
        hid = [sb(f"e_hid{n}", [P, T]) for n in range(2)]
        hid_hi, hid_lo = sb("e_hid_hi", [P, FC, T], F32R), sb("e_hid_lo", [P, FC, T], F32R)
        y_out = [sb(f"e_y_out{n}", [P, TB, D]) for n in range(2)]
        ps_x = [ps(f"e_ps_x{k}", [P, T]) for k in range(KC)]
        ps_g, ps_u, ps_y = ([ps(f"e_ps_{x}{n}", [P, 512]) for n in range(2)] for x in "guy")

        consts_step, rows_loaded, table_turned, table_ready = (
            sem("e_consts_step"), sem("e_rows_loaded"), sem("e_table_turned"), sem("e_table_ready"))
        where_loaded, sp_turns, pool_turns = sem("e_where_loaded"), sem("e_sp_turns"), sem("e_pool_turns")
        w_loaded, b_loaded = sems("e_w_loaded"), sems("e_b_loaded")
        x_loaded, y_stored = sems("e_x_loaded"), sems("e_y_stored")
        gu_hi_done, gu_lo_done, dn_hi_done, dn_lo_done = (
            sems("e_gu_hi_done"), sems("e_gu_lo_done"), sems("e_dn_hi_done"), sems("e_dn_lo_done"))
        x_turned, x_hi, x_lo = sem("e_x_turned"), sem("e_x_hi"), sem("e_x_lo")
        gu_made, gate_done, hid_done, hid_hi_done, hid_lo_done = (
            sems("e_gu_made"), sems("e_gate_done"), sems("e_hid_done"), sems("e_hid_hi_done"), sems("e_hid_lo_done"))
        y_made, y_kept = sems("e_y_made"), sems("e_y_kept")

        block = ctx.enter_context(nc.Block())
        W_LOADS, B_LOADS = 3, 2

        def all_tiles(eng, tile):
            for t in range(2):
                tile(t, t, 0)
            with eng.Fori(1, (TILES - 2) // 2) as i:
                for par in range(2):
                    tile(2 * i + par, par, i)
            for t in range((TILES - 2) // 2 * 2, TILES):
                tile(t, t % 2, t // 2)

        def has(t, ahead):
            return not isinstance(t, int) or 0 <= t + ahead < TILES

        @block.sync
        def _(sp):
            for n, b in enumerate((gate_b, up_b)):
                sp.dma_start(bias_rows[n * E * FC:(n + 1) * E * FC, :], b.rearrange("e (f p) -> (e f) p", p=P))\
                    .then_inc(rows_loaded, 16)

            def experts(t, first, count, loads):
                sp.dma_start(where[0:1, 0:count], tile_table[0:1, bass.ds(t + first, count)]).then_inc(where_loaded, 16)
                sp.wait_ge(where_loaded, 16 * loads)
                sp.sem_inc(sp_turns, 1)
                return [sp.value_load(where[0:1, n:n + 1], min_val=0, max_val=E - 1) for n in range(count)]

            def load_weights(e, par):
                for n, w in enumerate((gate_w, up_w)):
                    sp.dma_start(gu_raw[par][:, :, n * FF:(n + 1) * FF],
                                 w[bass.ds(e, 1)].rearrange("a (k p) f -> p (a k) f", p=P)).then_inc(w_loaded[par], 16)
                sp.dma_start(dn_raw[par][:], down_w[bass.ds(e, 1)].rearrange("a (f p) d -> p (a f) d", p=P))\
                    .then_inc(w_loaded[par], 16)

            def load_biases(e, par):
                sp.dma_start(bias[par][:], bias_table[:, :, bass.ds(e, 1), :].rearrange("p n a f -> p n (a f)"))\
                    .then_inc(b_loaded[par], 16)
                sp.dma_start(dn_bias[par][:], down_b[bass.ds(e, 1), :].to_broadcast([P, D])).then_inc(b_loaded[par], 16)

            def load_rows(t, par):
                sp.dma_start(x_in[par][:], x_sorted[bass.ts(t, T), :].rearrange("(k p) d -> p k d", p=P))\
                    .then_inc(x_loaded[par], 16)

            def store(t, par):
                for n in range(2):
                    sp.wait_ge(y_kept[n], (t + 1) * (TB // 2))
                sp.dma_start(y_sorted[bass.ts(t, T), :].rearrange("(k p) d -> p k d", p=P), y_out[par][:])\
                    .then_inc(y_stored[par], 16)

            def tile(t, par, turn):
                if has(t, 2):
                    sp.wait_ge(gu_lo_done[par], turn + 1)
                    sp.wait_ge(dn_lo_done[par], turn + 1)
                    e_next, e = experts(t, 1, 2, t + 2)
                    load_weights(e, par)
                    sp.wait_ge(x_turned, t + 1)
                    load_rows(t + 2, par)
                elif has(t, 1):
                    e_next, = experts(t, 1, 1, t + 2)
                if has(t, -1):
                    store(t - 1, 1 - par)
                if has(t, 1):
                    load_biases(e_next, 1 - par)

            e0, e1 = experts(0, 0, 2, 1)
            load_weights(e0, 0)
            load_rows(0, 0)
            load_weights(e1, 1)
            load_rows(1, 1)
            sp.wait_ge(table_ready, 1)
            load_biases(e0, 0)
            all_tiles(sp, tile)
            store(TILES - 1, (TILES - 1) % 2)
            for par in range(2):
                sp.wait_ge(y_stored[par], 16 * ((TILES + 1 - par) // 2))

        @block.gpsimd
        def _(pool):
            pool.memset(ident[:], 0.0).then_inc(consts_step, 1)
            pool.wait_ge(consts_step, 1)
            pool.affine_select(out=ident[:], in_=ident[:], compare_op=ALU.not_equal, fill=1.0, base=0,
                               pattern=[[-1, P]], channel_multiplier=1).then_inc(consts_step, 1)

            def low_parts(par, turn):
                pool.wait_ge(gu_hi_done[par], turn + 1)
                pool.sem_inc(pool_turns, 1)
                pool.tensor_tensor(gu_lo[par][:], gu_raw[par][:], gu_hi[par][:].bitcast(F32), ALU.subtract)\
                    .then_inc(gu_lo_done[par], 1)
                pool.wait_ge(dn_hi_done[par], turn + 1)
                pool.sem_inc(pool_turns, 1)
                pool.tensor_tensor(dn_lo[par][:], dn_raw[par][:], dn_hi[par][:].bitcast(F32), ALU.subtract)\
                    .then_inc(dn_lo_done[par], 1)

            def tile(t, par, turn):
                if has(t, 1):
                    low_parts(1 - par, turn + par)

            low_parts(0, 0)
            all_tiles(pool, tile)

        @block.scalar
        def _(act):
            def gu_high(t, par, turn):
                act.wait_ge(w_loaded[par], 16 * W_LOADS * (turn + 1))
                if has(t, -2):
                    act.wait_ge(gu_made[1], (t - 1) * (FC // 2))
                act.copy(gu_hi[par][:], gu_raw[par][:]).then_inc(gu_hi_done[par], 1)

            def dn_high(t, par):
                if has(t, -2):
                    act.wait_ge(y_made[1], (t - 1) * (TB // 2))
                act.copy(dn_hi[par][:], dn_raw[par][:]).then_inc(dn_hi_done[par], 1)

            def x_high(t, par):
                act.wait_ge(x_turned, t + 1)
                for k in range(KC):
                    ins = act.copy(xT_hi[par][:, k, :], ps_x[k][:])
                ins.then_inc(x_hi, 1)

            def tile(t, par, turn):
                def gates(f):
                    n, m = f % 2, t * (FC // 2) + f // 2
                    act.wait_ge(gu_made[n], m + 1)
                    act.wait_ge(hid_done[n], m)
                    act.activation(gate[n][:], ps_g[n][:], ACT.Silu, bias=bias[par][:, 0, f:f + 1]).then_inc(gate_done[n], 1)

                def hid_high(f):
                    n, m = f % 2, t * (FC // 2) + f // 2
                    act.wait_ge(hid_done[n], m + 1)
                    act.wait_ge(y_made[1], t * (TB // 2))
                    act.copy(hid_hi[:, f, :], hid[n][:]).then_inc(hid_hi_done[n], 1)

                if has(t, 1):
                    gu_high(t + 1, 1 - par, turn + par)
                act.wait_ge(b_loaded[par], 16 * B_LOADS * (turn + 1))
                gates(0)
                hid_high(0)
                if has(t, 1):
                    x_high(t + 1, 1 - par)
                gates(1)
                if has(t, 1):
                    dn_high(t + 1, 1 - par)
                for f in range(2, FC):
                    gates(f)
                    hid_high(f - 1)
                hid_high(FC - 1)

            act.wait_ge(table_turned, 1)
            act.copy(bias_table[:].rearrange("p n e f -> p (n e f)"), ps_y[0][:, 0:2 * E * FC]).then_inc(table_ready, 1)
            gu_high(0, 0, 0)
            dn_high(0, 0)
            x_high(0, 0)
            all_tiles(act, tile)

        @block.vector
        def _(vec):
            def x_low(t, par):
                vec.wait_ge(x_hi, t + 1)
                for k in range(KC):
                    ins = vec.tensor_tensor(xT_lo[par][:, k, :], ps_x[k][:], xT_hi[par][:, k, :].bitcast(F32), ALU.subtract)
                ins.then_inc(x_lo, 1)

            def keep_y(t, par, turn):
                vec.wait_ge(y_stored[par], 16 * turn)
                for blk in range(TB):
                    n = blk % 2
                    vec.wait_ge(y_made[n], t * (TB // 2) + blk // 2 + 1)
                    vec.tensor_tensor(y_out[par][:, blk, :], ps_y[n][:, 0:D], dn_bias[par][:], ALU.add).then_inc(y_kept[n], 1)

            def tile(t, par, turn):
                def hidden(f):
                    n, m = f % 2, t * (FC // 2) + f // 2
                    vec.wait_ge(gate_done[n], m + 1)
                    vec.wait_ge(hid_lo_done[n], m)
                    vec.scalar_tensor_tensor(hid[n][:], ps_u[n][:], bias[par][:, 1, f:f + 1], gate[n][:],
                                             ALU.add, ALU.mult).then_inc(hid_done[n], 1)

                def hid_low(f):
                    n, m = f % 2, t * (FC // 2) + f // 2
                    vec.wait_ge(hid_hi_done[n], m + 1)
                    vec.tensor_tensor(hid_lo[:, f, :], hid[n][:], hid_hi[:, f, :].bitcast(F32), ALU.subtract)\
                        .then_inc(hid_lo_done[n], 1)

                hidden(0)
                if has(t, -1):
                    keep_y(t - 1, 1 - par, turn - 1 + par)
                hid_low(0)
                if has(t, 1):
                    x_low(t + 1, 1 - par)
                for f in range(1, FC):
                    hidden(f)
                    if f > 1:
                        hid_low(f - 1)
                hid_low(FC - 1)

            x_low(0, 0)
            all_tiles(vec, tile)
            keep_y(TILES - 1, (TILES - 1) % 2, (TILES - 1) // 2)

        @block.tensor
        def _(pe):
            pe.wait_ge(consts_step, 2)
            pe.wait_ge(rows_loaded, 32)
            pe.transpose(ps_y[0][:, 0:2 * E * FC], bias_rows[:], ident[0:2 * E * FC, 0:2 * E * FC]).then_inc(table_turned, 1)
            pe.wait_ge(table_ready, 1)

            def turn_x(t, par, turn):
                pe.wait_ge(x_loaded[par], 16 * (turn + 1))
                pe.wait_ge(x_lo, t)
                for k in range(KC):
                    for blk in range(TB):
                        mm = pe.transpose(ps_x[k][:, blk * P:(blk + 1) * P], x_in[par][:, blk, k * P:(k + 1) * P], ident[:])
                mm.then_inc(x_turned, 1)

            def gate_up(t, par, f):
                n, m = f % 2, t * (FC // 2) + f // 2
                pe.wait_ge(hid_done[n], m)
                for out, first in ((ps_g[n], 0), (ps_u[n], FF)):
                    cols = slice(first + f * P, first + (f + 1) * P)
                    todo = [p for k in range(KC) for p in ((gu_hi, xT_hi, k), (gu_hi, xT_lo, k), (gu_lo, xT_hi, k))]
                    for s, (w, x, k) in enumerate(todo):
                        mm = pe.matmul(out[:], w[par][:, k, cols], x[par][:, k, :], start=(s == 0), stop=(s == len(todo) - 1))
                mm.then_inc(gu_made[n], 1)

            def down(t, par, turn):
                pe.wait_ge(dn_lo_done[par], turn + 1)
                for n in range(2):
                    pe.wait_ge(hid_lo_done[n], (t + 1) * (FC // 2))
                for blk in range(TB):
                    n, rows = blk % 2, slice(blk * P, (blk + 1) * P)
                    pe.wait_ge(y_kept[n], t * (TB // 2) + blk // 2)
                    todo = [p for f in range(FC) for p in ((hid_hi, dn_hi, f), (hid_hi, dn_lo, f), (hid_lo, dn_hi, f))]
                    for s, (h, w, f) in enumerate(todo):
                        mm = pe.matmul(ps_y[n][:, 0:D], h[:, f, rows], w[par][:, f, :], start=(s == 0), stop=(s == len(todo) - 1))
                    mm.then_inc(y_made[n], 1)

            def tile(t, par, turn):
                pe.wait_ge(x_lo, t + 1)
                pe.wait_ge(gu_lo_done[par], turn + 1)
                gate_up(t, par, 0)
                if has(t, -1):
                    down(t - 1, 1 - par, turn - 1 + par)
                if has(t, 1):
                    turn_x(t + 1, 1 - par, turn + par)
                for f in range(1, FC):
                    gate_up(t, par, f)

            turn_x(0, 0, 0)
            all_tiles(pe, tile)
            down(TILES - 1, (TILES - 1) % 2, (TILES - 1) // 2)


def combine(nc, sh, plan, x2_all, slots, gates, y_sorted, out):
    D, NBK = sh.D, plan.BLOCKS
    G = 4
    GROUPS = NBK // G
    with ExitStack() as ctx:
        def sb(name, shape, dt=F32):
            return ctx.enter_context(nc.sbuf_tensor(name, shape, dt))

        def sem(name):
            return sh.semaphore(nc, name)

        def sems(name):
            return [sem(f"{name}{n}") for n in range(2)]

        y = [[sb(f"f_y{par}_{k}", [P, G, D]) for k in range(2)] for par in range(2)]
        resid = [sb(f"f_resid{par}", [P, G, D]) for par in range(2)]
        stats = [sb(f"f_stats{par}", [P, G, 6]) for par in range(2)]
        mv = [sb(f"f_mv{par}", [P, G, 2]) for par in range(2)]
        ln_var, rstd = ([sb(f"f_{x}{par}", [P, G]) for par in range(2)] for x in ("ln_var", "rstd"))
        eps_col = sb("f_eps_col", [P, 1])
        gathered, added, normed, var_ready, stored = (
            sems("f_gathered"), sems("f_added"), sems("f_normed"), sems("f_var_ready"), sems("f_stored"))
        eps_ready, step, ln_step, rstd_ready = sem("f_eps_ready"), sem("f_step"), sem("f_ln_step"), sems("f_rstd_ready")
        vec_turns = sem("f_vec_turns")
        block = ctx.enter_context(nc.Block())
        out_rows = out.rearrange("b (k p) d -> p (b k) d", p=P)

        @block.gpsimd
        def _(pool):
            pool.memset(eps_col[:], LN_EPS).then_inc(eps_ready, 1)
            for i in range(GROUPS):
                par, turn = i % 2, i // 2
                if turn:
                    pool.wait_ge(added[par], turn * G)
                for j in range(G):
                    for k in range(2):
                        n = i * G + j
                        pool.indirect_dma_start(y[par][k][:, j, :], None, y_sorted,
                                                bass.IndirectOffsetOnAxis(slots[k][:, n:n + 1], 0))\
                            .then_inc(gathered[par], 16)

        @block.scalar
        def _(act):
            act.wait_ge(eps_ready, 1)
            with act.Fori(0, GROUPS // 2) as turn:
                for par in range(2):
                    act.wait_ge(var_ready[par], turn + 1)
                    act.activation(ln_var[par][:], mv[par][:, :, 1], ACT.Ln, bias=eps_col[:]).then_inc(ln_step, 1)
                    act.wait_ge(ln_step, turn * 2 + par + 1)
                    act.activation(rstd[par][:], ln_var[par][:], ACT.Exp, scale=-0.5).then_inc(rstd_ready[par], 1)

        @block.vector
        def _(vec):
            def add_rows(turn, par):
                first = (turn * 2 + par) * G
                vec.wait_ge(gathered[par], 16 * 2 * G * (turn + 1))
                vec.wait_ge(stored[par], 16 * turn)
                for j in range(G):
                    n = first + j
                    vec.scalar_tensor_tensor(resid[par][:, j, :], y[par][0][:, j, :], gates[0][:, bass.ds(n, 1)],
                                             x2_all[:, bass.ds(n, 1), :].rearrange("p n d -> p (n d)"),
                                             ALU.mult, ALU.add).then_inc(step, 1)
                for j in range(G):
                    n = first + j
                    vec.wait_ge(step, (turn * 2 + par) * 2 * G + G + j)
                    ins = vec.scalar_tensor_tensor(resid[par][:, j, :], y[par][1][:, j, :], gates[1][:, bass.ds(n, 1)],
                                                   resid[par][:, j, :], ALU.mult, ALU.add)
                    ins.then_inc(step, 1)
                vec.wait_ge(step, (turn * 2 + par + 1) * 2 * G)
                for j in range(G):
                    vec.bn_stats(stats[par][:, j, :], resid[par][:, j, :]).then_inc(added[par], 1)
                vec.wait_ge(added[par], G * (turn + 1))
                vec.sem_inc(vec_turns, 1)
                for j in range(G):
                    ins = vec.bn_aggr(mv[par][:, j, :], stats[par][:, j, :])
                ins.then_inc(var_ready[par], 1)

            def normalise(turn, par):
                vec.wait_ge(rstd_ready[par], turn + 1)
                for j in range(G):
                    ins = vec.tensor_scalar(resid[par][:, j, :], resid[par][:, j, :], mv[par][:, j, 0:1],
                                            rstd[par][:, j:j + 1], ALU.subtract, ALU.mult)
                ins.then_inc(normed[par], 1)

            def pair(turn):
                add_rows(turn, 0)
                add_rows(turn, 1)
                normalise(turn, 0)
                normalise(turn, 1)

            pair(0)
            with vec.Fori(1, GROUPS // 2) as turn:
                pair(turn)

        @block.sync
        def _(sp):
            with sp.Fori(0, GROUPS // 2) as turn:
                for par in range(2):
                    sp.wait_ge(normed[par], turn + 1)
                    sp.dma_start(out_rows[:, bass.ds((turn * 2 + par) * G, G), :], resid[par][:]).then_inc(stored[par], 16)
            for par in range(2):
                sp.wait_ge(stored[par], 16 * GROUPS // 2)


def decoder_layer(nc, x, ctx_1024, mask, Wq, Wk, Wv, Wo, Wa, ba, xWq, xbq, xWk, xbk, xWv, xbv, xWo, xbo,
                  router_w, gate_w, gate_b, up_w, up_b, down_w, down_b, out):
    with ExitStack() as ctx:
        sh = Shapes(x, Wq, ctx_1024, gate_w)
        plan = Plan(sh)
        x1_dram = nc.dram_tensor("x1_rows", list(x.shape), F32).ap()
        x_sorted = nc.dram_tensor("x_sorted", [plan.ROWS, sh.D], F32).ap()
        y_sorted = nc.dram_tensor("y_sorted", [plan.ROWS, sh.D], F32).ap()

        def sb(name, shape, dt=F32):
            return ctx.enter_context(nc.sbuf_tensor(name, shape, dt))

        x2_all = sb("x2_all", [P, plan.BLOCKS, sh.D])
        logits = sb("logits", [P, plan.BLOCKS, sh.E])
        slots = [sb(f"slots{k}", [P, plan.BLOCKS], U32) for k in range(2)]
        gates = [sb(f"gates{k}", [P, plan.BLOCKS]) for k in range(2)]
        tile_table = sb("tile_table", [1, plan.TILES], I32)
        linear_attention(nc, sh, x, Wq, Wk, Wv, Wo, Wa, ba, x1_dram, x_sorted)
        sh.end_stage(nc)
        cross_attention(nc, sh, x1_dram, ctx_1024, mask, xWq, xbq, xWk, xbk, xWv, xbv, xWo, xbo,
                        router_w, x2_all, logits)
        sh.end_stage(nc)
        route_tokens(nc, sh, plan, logits, x2_all, x_sorted, slots, gates, tile_table)
        run_experts(nc, sh, plan, x_sorted, tile_table, gate_w, gate_b, up_w, up_b, down_w, down_b, y_sorted)
        combine(nc, sh, plan, x2_all, slots, gates, y_sorted, out)


_INS = ["x", "ctx_1024", "mask_BxSxS2_if1"] + ["L0_attn_" + n for n in ("Wq", "Wk", "Wv", "Wo", "Wa", "ba")] \
    + ["L0_xattn_" + n for n in ("Wq", "bq", "Wk", "bk", "Wv", "bv", "Wo", "bo")] \
    + ["L0_ffn_" + n for n in ("router_w", "gate_w", "gate_b", "up_w", "up_b", "down_w", "down_b")]


def kernel(**inputs):
    import numpy as _np
    import concourse.bacc as _bacc
    from concourse.bass_utils import run_bass_kernel_spmd as _run

    nc = _bacc.Bacc("TRN2", target_bir_lowering=False, num_devices=1)
    arrays, args = {}, []
    for name in _INS:
        a = _np.ascontiguousarray(inputs[name])
        arrays[f"in_{name}"] = a
        args.append(nc.dram_tensor(f"in_{name}", a.shape, mybir.dt.from_np(a.dtype), kind="ExternalInput").ap())
    args.append(nc.dram_tensor("out", inputs["x"].shape, F32, kind="ExternalOutput").ap())
    decoder_layer(nc, *args)
    return _run(nc, [arrays], core_ids=[0]).results[0]["out"]
```

```python
from contextlib import ExitStack

import concourse.bass as bass
from concourse import mybir

F32 = mybir.dt.float32
F32R = mybir.dt.float32r
BF16 = mybir.dt.bfloat16
I32 = mybir.dt.int32
U32 = mybir.dt.uint32
ALU = mybir.AluOpType
ACT = mybir.ActivationFunctionType
AX = mybir.AxisListType

P = 128
LN_EPS = 1e-5


class Shapes:

    def __init__(self, x, wq, ctx, gate_w):
        self.counted = []
        self.B, self.N, self.D = x.shape
        self.NB = self.N // P
        self.KC = self.D // P
        self.H = 16
        self.DH = wq.shape[1] // self.H
        self.PAIRS = self.H // 2
        self.S2 = ctx.shape[1]
        self.E, _, self.FF = gate_w.shape

    def semaphore(self, nc, name):
        self.counted.append(nc.alloc_semaphore(name))
        return self.counted[-1]

    def end_stage(self, nc):
        nc.clear_and_free_semaphores(self.counted)
        nc.all_engine_barrier()
        self.counted = []


def linear_attention(nc, sh, x, wq, wk, wv, wo, wa, ba, x1_dram):
    B, N, D, H, DH, NB, KC, PAIRS = sh.B, sh.N, sh.D, sh.H, sh.DH, sh.NB, sh.KC, sh.PAIRS
    PW = H * DH
    HALF = PW // 2
    HEADS_HALF = HALF // DH
    VU = 2 * NB
    CP = 3 * H
    TRI = N + P
    DECAY_SHIFT, EPS, Z_FLOOR = 2.0, 1e-6, -80.0
    with ExitStack() as ctx:
        def sb(name, shape, dt=F32):
            return ctx.enter_context(nc.sbuf_tensor(name, shape, dt))

        def ps(name, shape, dt=F32):
            return ctx.enter_context(nc.psum_tensor(name, shape, dt))

        def sem(name):
            return sh.semaphore(nc, name)

        w_raw = [sb(f"a_w_raw{n}", [P, KC, PW]) for n in range(2)]
        w_hi = [sb(f"a_w_hi{n}", [P, KC, PW], F32R) for n in range(3)]
        w_lo = [sb(f"a_w_lo{n}", [P, KC, PW], F32R) for n in range(3)]
        wo_hi, wo_lo = sb("a_wo_hi", [P, PAIRS, D], F32R), sb("a_wo_lo", [P, PAIRS, D], F32R)
        wa_raw = sb("a_wa_raw", [P, KC, H])
        wa_hi, wa_lo = sb("a_wa_hi", [P, KC, H], F32R), sb("a_wa_lo", [P, KC, H], F32R)
        ba_col, ba_shift = sb("a_ba_col", [H, 1]), sb("a_ba_shift", [H, 1])
        ident, ident_bf = sb("a_ident", [P, P]), sb("a_ident_bf", [P, P], BF16)
        ones, upto = sb("a_ones", [P, P]), sb("a_upto", [P, P])
        pick_head = sb("a_pick_head", [CP, H, P], BF16)
        x_in, x_res = sb("a_x_in", [P, NB, D]), sb("a_x_res", [P, NB, D])
        xT_hi, xT_lo = sb("a_xT_hi", [P, KC, N], F32R), sb("a_xT_lo", [P, KC, N], F32R)
        z_sb, z_exp, decT = sb("a_z", [H, N]), sb("a_z_exp", [H, N]), sb("a_decT", [H, N])
        dec = sb("a_dec", [P, NB, H])
        c_next, c_now = sb("a_c_next", [P, NB, H]), sb("a_c_now", [P, NB, H])
        c_rest = sb("a_c_rest", [P, NB, H])
        c_parts = sb("a_c_parts", [P, NB, 3, H], BF16)
        cT_next, cT_now = sb("a_cT_next", [CP, N], BF16), sb("a_cT_now", [CP, N], BF16)
        qk_exp, qk_relu = sb("a_qk_exp", [P, 2, N]), sb("a_qk_relu", [P, 2, N])
        qk = sb("a_qk", [P, 2, N])
        qk_hi, qk_lo = ([sb(f"a_qk_{x}{g}", [P, 2, N], F32R) for g in range(PAIRS)] for x in ("hi", "lo"))
        v_aug = [sb(f"a_v_aug{n}", [P, NB, H, DH + 1]) for n in range(2)]
        decay = [sb(f"a_decay{h}", [P, TRI]) for h in range(2)]
        probs = [sb(f"a_probs{h}", [P, TRI]) for h in range(2)]
        den, rden = sb("a_den", [P, NB, 2]), sb("a_rden", [P, NB, 2])
        o_norm = sb("a_o_norm", [P, NB, 2, DH])
        oT_hi, oT_lo = ([sb(f"a_oT_{x}{n}", [P, NB * P], F32R) for n in range(2)] for x in ("hi", "lo"))
        resid = sb("a_resid", [P, NB, D])
        stats, mv = sb("a_stats", [P, NB, 6]), sb("a_mv", [P, NB, 2])
        ln_var, rstd = sb("a_ln_var", [P, NB]), sb("a_rstd", [P, NB])
        eps_col = sb("a_eps_col", [P, 1])
        x1 = sb("a_x1", [P, NB, D])
        ps_mix = ps("a_ps_mix", [P, 512])
        ps_qk = ps("a_ps_qk", [P, 2, N])
        ps_c = ps("a_ps_c", [P, 2, N])
        ps_s = [ps(f"a_ps_s{h}", [P, 512]) for h in range(2)]
        ps_o = ps("a_ps_o", [P, 512])
        ps_t = ps("a_ps_t", [P, 512])
        ps_y = ps("a_ps_y", [P, NB, D])
        o_view = ps_o[:, 0:NB * 2 * (DH + 1)].rearrange("p (b h d) -> p b h d", b=NB, h=2)
        c_view = ps_mix[:, 0:NB * H].rearrange("p (b h) -> p b h", b=NB)
        cT_view = ps_mix[:, :].bitcast(BF16)
        zT_view = ps_mix[0:H, 0:N]

        ident_ready, consts_ready = sem("a_ident_ready"), sem("a_consts_ready")
        consts_step = sem("a_consts_step")
        raw_loaded = [sem(f"a_raw_loaded{n}") for n in range(4)]
        small_loaded = sem("a_small_loaded")
        w_hi_done, w_lo_done = sem("a_w_hi_done"), sem("a_w_lo_done")
        wa_hi_done, wa_lo_done = sem("a_wa_hi_done"), sem("a_wa_lo_done")
        x_in_loaded, x_res_loaded, x1_stored = sem("a_x_in_loaded"), sem("a_x_res_loaded"), sem("a_x1_stored")
        pool_turns, vec_turns, pe_turns = sem("a_pool_turns"), sem("a_vec_turns"), sem("a_pe_turns")
        xT_made, x_hi_done, x_lo_done = sem("a_xT_made"), sem("a_x_hi_done"), sem("a_x_lo_done")
        z_made, z_kept, z_exp_done, dec_done = sem("a_z_made"), sem("a_z_kept"), sem("a_z_exp_done"), sem("a_dec_done")
        dec_turned, dec_kept = sem("a_dec_turned"), sem("a_dec_kept")
        c_made, c_step, c_split = sem("a_c_made"), sem("a_c_step"), sem("a_c_split")
        cT_made, cT_kept, c_switched = sem("a_cT_made"), sem("a_cT_kept"), sem("a_c_switched")
        qk_made, qk_kept, qk_done, qk_hi_done, qk_lo_done = (
            sem("a_qk_made"), sem("a_qk_kept"), sem("a_qk_done"), sem("a_qk_hi_done"), sem("a_qk_lo_done"))
        v_made, v_done = sem("a_v_made"), sem("a_v_done")
        c_spread, s_made = sem("a_c_spread"), sem("a_s_made")
        decay_exp = [sem(f"a_decay_exp{h}") for h in range(2)]
        decay_masked = [sem(f"a_decay_masked{h}") for h in range(2)]
        probs_done = [sem(f"a_probs_done{h}") for h in range(2)]
        o_made, den_step, o_normed = sem("a_o_made"), sem("a_den_step"), sem("a_o_normed")
        oT_made, oT_hi_done, oT_lo_done, y_added = (
            sem("a_oT_made"), sem("a_oT_hi_done"), sem("a_oT_lo_done"), sem("a_y_added"))
        resid_done, ln_step, var_ready, rstd_step, x1_ready = (
            sem("a_resid_done"), sem("a_ln_step"), sem("a_var_ready"), sem("a_rstd_step"), sem("a_x1_ready"))

        block = ctx.enter_context(nc.Block())
        x_rows = x.rearrange("b (k p) d -> b p k d", p=P)
        x1_rows = x1_dram.rearrange("b (k p) d -> b p k d", p=P)

        def raw_view(n):
            return w_raw[n % 2][:] if n < 3 else w_raw[n % 2][:].rearrange("p k (g n) -> p (k g) n", n=D)

        w_parts = [(w_hi[n], w_lo[n]) for n in range(3)] + [(wo_hi, wo_lo)]

        def has(b, ahead):
            return not isinstance(b, int) or 0 <= b + ahead < B

        def all_sequences(eng, sequence):
            sequence(0, 0)
            pairs = (B - 3) // 2
            with eng.Fori(0, pairs) as i:
                for par in (1, 0):
                    sequence(2 * i + 2 - par, par)
            for b in range(2 * pairs + 1, B):
                sequence(b, b % 2)

        def back(b, par, g, steps):
            return (b, par, g - steps) if g >= steps else (b - 1, 1 - par, g - steps + PAIRS)

        def projected_before(b, g):
            return (b + 1, g - 1) if g else (b, PAIRS - 1)

        def exists(b, g, steps):
            return g >= steps or has(b, -1)

        @block.sync
        def _(sp):
            sp.dma_start(x_in[:], x_rows[0]).then_inc(x_in_loaded, 16)
            sp.dma_start(wa_raw[:], wa.rearrange("(k p) h -> p k h", p=P)).then_inc(small_loaded, 16)
            sp.dma_start(ba_col[:], ba.rearrange("(h a) -> h a", a=1)).then_inc(small_loaded, 16)
            for n, w in enumerate((wq, wk, wv, wo)):
                if n >= 2:
                    sp.wait_ge(w_lo_done, n - 1)
                sp.dma_start(raw_view(n), w.rearrange("(k p) n -> p k n", p=P)).then_inc(raw_loaded[n], 16)
            def load_x(b):
                sp.wait_ge(xT_made, b)
                sp.dma_start(x_in[:], x_rows[b]).then_inc(x_in_loaded, 16)

            def load_residual(b):
                sp.wait_ge(resid_done, b)
                sp.dma_start(x_res[:], x_rows[b]).then_inc(x_res_loaded, 16)

            def store_x1(b):
                sp.wait_ge(x1_ready, b + 1)
                sp.dma_start(x1_rows[b], x1[:]).then_inc(x1_stored, 16)

            def sequence(b):
                load_x(b + 2)
                load_residual(b)
                store_x1(b - 1)

            load_x(1)
            load_residual(0)
            load_x(2)
            with sp.Fori(1, B - 2) as b:
                sequence(b)
            for b in (B - 2, B - 1):
                load_residual(b)
                store_x1(b - 1)
            store_x1(B - 1)
            sp.wait_ge(x1_stored, 16 * B)

        @block.gpsimd
        def _(pool):
            pool.memset(ident[:], 0.0).then_inc(consts_step, 1)
            pool.wait_ge(consts_step, 1)
            pool.affine_select(out=ident[:], in_=ident[:], compare_op=ALU.not_equal, fill=1.0, base=0,
                               pattern=[[-1, P]], channel_multiplier=1).then_inc(ident_ready, 1)
            pool.memset(ident_bf[:], 0.0).then_inc(consts_step, 1)
            pool.memset(ones[:], 1.0).then_inc(consts_step, 1)
            pool.memset(pick_head[:], 0.0).then_inc(consts_step, 1)
            for n in range(2):
                pool.memset(v_aug[n][:], 1.0).then_inc(consts_step, 1)
            pool.memset(eps_col[:], LN_EPS).then_inc(consts_step, 1)
            pool.wait_ge(consts_step, 7)
            pool.affine_select(out=ident_bf[:], in_=ident_bf[:], compare_op=ALU.not_equal, fill=1.0, base=0,
                               pattern=[[-1, P]], channel_multiplier=1).then_inc(consts_step, 1)
            pool.affine_select(out=upto[:], in_=ones[:], compare_op=ALU.is_ge, fill=0.0, base=0,
                               pattern=[[1, P]], channel_multiplier=-1).then_inc(consts_step, 1)
            for part in range(3):
                if part:
                    pool.wait_ge(consts_step, 9 + part)
                pool.affine_select(out=pick_head[:], in_=pick_head[:], compare_op=ALU.not_equal, fill=1.0,
                                   base=-H * part, pattern=[[-1, H], [0, P]], channel_multiplier=1)\
                    .then_inc(consts_step, 1)
            pool.wait_ge(consts_step, 12)
            pool.memset(den[:], 1.0).then_inc(consts_ready, 1)

            def mask_decay(b, g):
                for h in range(2):
                    pool.wait_ge(decay_exp[h], b * PAIRS + g + 1)
                    pool.sem_inc(pool_turns, 1)
                    d = decay[h][:, :].rearrange("p (t i) -> p t i", i=P)[:, 0:3:2, :]
                    pool.affine_select(out=d, in_=d, compare_op=ALU.is_ge, fill=0.0, base=0,
                                       pattern=[[0, 2], [1, P]], channel_multiplier=-1)\
                        .then_inc(decay_masked[h], 1)

            def split_qk(b, g):
                pool.wait_ge(qk_done, b * PAIRS + g + 1)
                if not isinstance(b, int) or b:
                    pool.wait_ge(s_made, (b - 1) * PAIRS + g + 1)
                pool.sem_inc(pool_turns, 1)
                pool.tensor_copy(qk_hi[g][:], qk[:]).then_inc(qk_hi_done, 1)
                pool.wait_ge(qk_hi_done, b * PAIRS + g + 1)
                pool.sem_inc(pool_turns, 1)
                pool.tensor_tensor(qk_lo[g][:], qk[:], qk_hi[g][:].bitcast(F32), ALU.subtract).then_inc(qk_lo_done, 1)

            def sequence(b, par):
                for g in range(PAIRS):
                    mask_decay(b, g)
                    if g == 0 or has(b, 1):
                        split_qk(*projected_before(b, g))

            for g in range(PAIRS - 1):
                split_qk(0, g)
            all_sequences(pool, sequence)

        @block.scalar
        def _(act):
            def high_weights(n):
                act.wait_ge(raw_loaded[n], 16)
                act.copy(w_parts[n][0][:], raw_view(n)).then_inc(w_hi_done, 1)

            def x_hi(b):
                act.wait_ge(xT_made, b + 1)
                act.copy(xT_hi[:], ps_mix[:].rearrange("p (k n) -> p k n", k=KC)).then_inc(x_hi_done, 1)

            def exp_qk(b, g):
                act.wait_ge(qk_made, b * PAIRS + g + 1)
                act.wait_ge(qk_done, b * PAIRS + g)
                act.activation(qk_exp[:], ps_qk[:], ACT.Exp)
                act.activation(qk_relu[:], ps_qk[:], ACT.Relu).then_inc(qk_kept, 1)

            def log_decay(b):
                act.wait_ge(z_kept, b + 1)
                act.activation(z_exp[:], z_sb[:], ACT.Exp, scale=-1.0).then_inc(z_exp_done, 1)
                act.wait_ge(z_exp_done, b + 1)
                act.activation(decT[:], z_exp[:], ACT.Ln, bias=1.0).then_inc(dec_done, 1)

            def keep_cT(b):
                act.wait_ge(cT_made, b + 1)
                act.wait_ge(c_switched, 2 * b)
                act.copy(cT_next[:], cT_view[0:CP, 0:N]).then_inc(cT_kept, 1)

            def keep_v(b, par, half, blk):
                act.wait_ge(v_made, b * VU + half * NB + blk + 1)
                if not isinstance(b, int) or b >= 2:
                    act.wait_ge(o_made, (b - 1) * PAIRS)
                act.copy(v_aug[par][:, blk, half * HEADS_HALF:(half + 1) * HEADS_HALF, 0:DH],
                         ps_mix[:].rearrange("p (h d) -> p h d", d=DH)).then_inc(v_done, 1)

            def switch_c(b):
                act.wait_ge(cT_kept, b + 1)
                act.wait_ge(c_split, b + 1)
                act.wait_ge(c_spread, b * PAIRS)
                act.wait_ge(decay_exp[1], b * PAIRS)
                act.copy(cT_now[:], cT_next[:]).then_inc(c_switched, 1)
                act.copy(c_now[:], c_next[:]).then_inc(c_switched, 1)
                act.wait_ge(c_switched, 2 * b + 2)

            def exp_decay(b, g):
                act.wait_ge(c_spread, b * PAIRS + g + 1)
                for h in range(2):
                    act.wait_ge(probs_done[h], b * PAIRS + g)
                    head = 2 * g + h
                    act.activation(decay[h][:, 0:N], ps_c[:, h, :], ACT.Exp,
                                   bias=c_now[:, 0, head:head + 1], scale=-1.0)
                    act.activation(decay[h][:, N:TRI], ps_c[:, h, P:N], ACT.Exp,
                                   bias=c_now[:, 1, head:head + 1], scale=-1.0).then_inc(decay_exp[h], 1)

            def high_oT(b, g):
                act.wait_ge(oT_made, b * PAIRS + g + 1)
                if not isinstance(b, int) or b or g >= 2:
                    act.wait_ge(y_added, b * PAIRS + g - 1)
                act.copy(oT_hi[g % 2][:], ps_t[:, 0:NB * P]).then_inc(oT_hi_done, 1)

            def root(b):
                act.wait_ge(var_ready, b + 1)
                act.activation(ln_var[:], mv[:, :, 1], ACT.Ln, bias=eps_col[:]).then_inc(rstd_step, 1)
                act.wait_ge(rstd_step, 2 * b + 1)
                act.activation(rstd[:], ln_var[:], ACT.Exp, scale=-0.5).then_inc(rstd_step, 1)

            def sequence(b, par):
                for g in range(PAIRS):
                    exp_decay(b, g)
                    if g == 3 and has(b, 1):
                        log_decay(b + 1)
                    if g == 3 and has(b, -1):
                        root(b - 1)
                    if has(b, 1):
                        if g == PAIRS - 1:
                            keep_cT(b + 1)
                            switch_c(b + 1)
                        if g in (1, 2):
                            keep_v(b + 1, 1 - par, g - 1, 0)
                    if exists(b, g, 2):
                        before, _, pair = back(b, par, g, 2)
                        high_oT(before, pair)
                    if has(b, 1):
                        exp_qk(b + 1, g)
                        if g in (1, 2):
                            keep_v(b + 1, 1 - par, g - 1, 1)
                if has(b, 2):
                    x_hi(b + 2)

            high_weights(0)
            act.wait_ge(small_loaded, 32)
            act.copy(wa_hi[:], wa_raw[:]).then_inc(wa_hi_done, 1)
            high_weights(1)
            x_hi(0)
            act.wait_ge(consts_ready, 1)
            for g in range(PAIRS):
                exp_qk(0, g)
                if g in (0, 1):
                    high_weights(2 + g)
                if 1 <= g <= VU:
                    keep_v(0, 0, (g - 1) // NB, (g - 1) % NB)
                if g == VU + 1:
                    log_decay(0)
            keep_cT(0)
            x_hi(1)
            switch_c(0)
            all_sequences(act, sequence)
            for g in (PAIRS - 2, PAIRS - 1):
                high_oT(B - 1, g)
            root(B - 1)

        @block.vector
        def _(vec):
            def low_weights(n):
                hi, lo = w_parts[n]
                vec.wait_ge(w_hi_done, n + 1)
                vec.tensor_tensor(lo[:], raw_view(n), hi[:].bitcast(F32), ALU.subtract).then_inc(w_lo_done, 1)

            def x_lo(b):
                vec.wait_ge(x_hi_done, b + 1)
                vec.tensor_tensor(xT_lo[:], ps_mix[:].rearrange("p (k n) -> p k n", k=KC), xT_hi[:].bitcast(F32),
                                  ALU.subtract).then_inc(x_lo_done, 1)

            def keep_z(b):
                vec.wait_ge(z_made, b + 1)
                vec.tensor_scalar(z_sb[:], zT_view, ba_shift[:, 0:1], Z_FLOOR, ALU.add, ALU.max).then_inc(z_kept, 1)

            def keep_dec(b):
                vec.wait_ge(dec_turned, b + 1)
                vec.tensor_copy(dec[:], c_view).then_inc(dec_kept, 1)

            def split_c(b):
                vec.wait_ge(c_made, b + 1)
                vec.wait_ge(c_switched, 2 * b)
                vec.wait_ge(cT_made, b)
                vec.tensor_copy(c_next[:], c_view).then_inc(c_step, 1)
                vec.tensor_copy(c_parts[:, :, 0, :], c_view).then_inc(c_step, 1)
                vec.wait_ge(c_step, 4 * b + 2)
                vec.tensor_tensor(c_rest[:], c_next[:], c_parts[:, :, 0, :], ALU.subtract).then_inc(c_step, 1)
                vec.wait_ge(c_step, 4 * b + 3)
                vec.tensor_copy(c_parts[:, :, 1, :], c_rest[:]).then_inc(c_step, 1)
                vec.wait_ge(c_step, 4 * b + 4)
                vec.tensor_tensor(c_parts[:, :, 2, :], c_rest[:], c_parts[:, :, 1, :], ALU.subtract)\
                    .then_inc(c_split, 1)

            def finish_qk(b, g):
                vec.wait_ge(qk_kept, b * PAIRS + g + 1)
                vec.wait_ge(qk_lo_done, b * PAIRS + g)
                vec.scalar_tensor_tensor(qk[:], qk_exp[:], 1.0, qk_relu[:], ALU.min, ALU.add).then_inc(qk_done, 1)

            def weigh(b, g):
                vec.wait_ge(s_made, b * PAIRS + g + 1)
                vec.wait_ge(o_made, b * PAIRS + g)
                for h in range(2):
                    vec.wait_ge(decay_masked[h], b * PAIRS + g + 1)
                    vec.tensor_tensor(probs[h][:], ps_s[h][:, 0:TRI], decay[h][:], ALU.mult)\
                        .then_inc(probs_done[h], 1)

            def normalise(b, g):
                n = b * PAIRS + g
                vec.wait_ge(o_made, n + 1)
                vec.tensor_scalar(den[:], o_view[:, :, :, DH], EPS, None, ALU.add).then_inc(den_step, 1)
                vec.wait_ge(den_step, 2 * n + 1)
                vec.reciprocal(rden[:], den[:]).then_inc(den_step, 1)
                vec.wait_ge(den_step, 2 * n + 2)
                vec.wait_ge(oT_made, n)
                vec.tensor_tensor(o_norm[:], o_view[:, :, :, 0:DH],
                                  rden[:].unsqueeze(3).to_broadcast([P, NB, 2, DH]), ALU.mult).then_inc(o_normed, 1)

            def low_oT(b, g):
                vec.wait_ge(oT_hi_done, b * PAIRS + g + 1)
                vec.tensor_tensor(oT_lo[g % 2][:], ps_t[:, 0:NB * P], oT_hi[g % 2][:].bitcast(F32), ALU.subtract).then_inc(oT_lo_done, 1)

            def add_residual(b):
                vec.wait_ge(y_added, (b + 1) * PAIRS)
                vec.wait_ge(x_res_loaded, 16 * (b + 1))
                vec.wait_ge(x1_ready, b)
                vec.tensor_tensor(resid[:], ps_y[:], x_res[:], ALU.add).then_inc(resid_done, 1)
                vec.wait_ge(resid_done, b + 1)
                for blk in range(NB):
                    vec.bn_stats(stats[:, blk, :], resid[:, blk, :]).then_inc(ln_step, 1)
                vec.wait_ge(ln_step, NB * b + NB)
                vec.sem_inc(vec_turns, 1)
                for blk in range(NB):
                    last = vec.bn_aggr(mv[:, blk, :], stats[:, blk, :])
                last.then_inc(var_ready, 1)

            def scale_x1(b):
                vec.wait_ge(rstd_step, 2 * b + 2)
                vec.wait_ge(x1_stored, 16 * b)
                for blk in range(NB):
                    last = vec.tensor_scalar(x1[:, blk, :], resid[:, blk, :], mv[:, blk, 0:1], rstd[:, blk:blk + 1],
                                             ALU.subtract, ALU.mult)
                last.then_inc(x1_ready, 1)

            def sequence(b, par):
                for g in range(PAIRS):
                    if g == 1 and has(b, 1):
                        keep_z(b + 1)
                    if g == 6 and has(b, 1):
                        split_c(b + 1)
                    if g == 0 or has(b, 1):
                        finish_qk(*projected_before(b, g))
                    if g == 5 and has(b, 1):
                        keep_dec(b + 1)
                    weigh(b, g)
                    if exists(b, g, 1):
                        before, _, pair = back(b, par, g, 1)
                        normalise(before, pair)
                    if exists(b, g, 2):
                        before, _, pair = back(b, par, g, 2)
                        low_oT(before, pair)
                    if g == 2 and has(b, -1):
                        add_residual(b - 1)
                    if g == 4 and has(b, -1):
                        scale_x1(b - 1)
                if has(b, 2):
                    x_lo(b + 2)

            low_weights(0)
            vec.wait_ge(wa_hi_done, 1)
            vec.tensor_tensor(wa_lo[:], wa_raw[:], wa_hi[:].bitcast(F32), ALU.subtract).then_inc(wa_lo_done, 1)
            vec.tensor_scalar(ba_shift[:], ba_col[:], DECAY_SHIFT, None, ALU.add).then_inc(wa_lo_done, 1)
            low_weights(1)
            x_lo(0)
            keep_z(0)
            vec.wait_ge(consts_ready, 1)
            for g in range(PAIRS - 1):
                finish_qk(0, g)
                if g in (0, 1):
                    low_weights(2 + g)
            keep_dec(0)
            split_c(0)
            x_lo(1)
            all_sequences(vec, sequence)
            normalise(B - 1, PAIRS - 1)
            low_oT(B - 1, PAIRS - 2)
            low_oT(B - 1, PAIRS - 1)
            add_residual(B - 1)
            scale_x1(B - 1)

        @block.tensor
        def _(pe):
            def split_product(out, pairs):
                steps = [(lh, rh, ll, rl) for (lh, ll), (rh, rl) in pairs]
                todo = [p for lh, rh, ll, rl in steps for p in ((lh, rh), (lh, rl), (ll, rh))]
                for n, (l, r) in enumerate(todo):
                    mm = pe.matmul(out, l, r, start=(n == 0), stop=(n == len(todo) - 1))
                return mm

            def turn_x(b):
                pe.wait_ge(x_in_loaded, 16 * (b + 1))
                pe.wait_ge(cT_kept, b)
                for k in range(KC):
                    for blk in range(NB):
                        mm = pe.transpose(ps_mix[:, k * N + blk * P:k * N + (blk + 1) * P],
                                          x_in[:, blk, k * P:(k + 1) * P], ident[:])
                mm.then_inc(xT_made, 1)

            def project_qk(b, g):
                pe.wait_ge(x_lo_done, b + 1)
                pe.wait_ge(qk_kept, b * PAIRS + g)
                cols = slice(g * P, (g + 1) * P)
                for n in range(2):
                    mm = split_product(ps_qk[:, n, :], [
                        ((w_hi[n][:, k, cols], w_lo[n][:, k, cols]), (xT_hi[:, k, :], xT_lo[:, k, :]))
                        for k in range(KC)])
                mm.then_inc(qk_made, 1)

            def project_z(b):
                pe.wait_ge(x_lo_done, b + 1)
                split_product(zT_view, [((wa_hi[:, k, :], wa_lo[:, k, :]), (xT_hi[:, k, :], xT_lo[:, k, :]))
                                        for k in range(KC)]).then_inc(z_made, 1)

            def turn_dec(b):
                pe.wait_ge(dec_done, b + 1)
                pe.wait_ge(v_done, VU * (b + 1))
                pe.sem_inc(pe_turns, 1)
                for blk in range(NB):
                    mm = pe.transpose(c_view[:, blk, :], decT[:, blk * P:(blk + 1) * P], ident[0:H, 0:H])
                mm.then_inc(dec_turned, 1)

            def sum_decay(b):
                pe.wait_ge(dec_kept, b + 1)
                pe.matmul(c_view[:, 0, :], upto[:], dec[:, 0, :], start=True, stop=True)
                for blk in range(1, NB):
                    for j in range(blk):
                        pe.matmul(c_view[:, blk, :], ones[:], dec[:, j, :], start=(j == 0), stop=False)
                    mm = pe.matmul(c_view[:, blk, :], upto[:], dec[:, blk, :], start=False, stop=True)
                mm.then_inc(c_made, 1)

            def turn_c(b):
                pe.wait_ge(c_split, b + 1)
                pe.sem_inc(pe_turns, 1)
                for blk in range(NB):
                    mm = pe.transpose(cT_view[0:CP, blk * P:(blk + 1) * P],
                                      c_parts[:, blk, :, :].rearrange("p t h -> p (t h)"), ident_bf[:])
                mm.then_inc(cT_made, 1)

            def project_v(b, half, blk):
                if (half, blk) == (0, 0):
                    pe.wait_ge(z_kept, b + 1)
                pe.wait_ge(v_done, VU * b + half * NB + blk)
                rows, cols = slice(blk * P, (blk + 1) * P), slice(half * HALF, (half + 1) * HALF)
                split_product(ps_mix[:], [
                    ((xT_hi[:, k, rows], xT_lo[:, k, rows]), (w_hi[2][:, k, cols], w_lo[2][:, k, cols]))
                    for k in range(KC)]).then_inc(v_made, 1)

            def spread_c(b, g):
                pe.wait_ge(c_switched, 2 * b + 2)
                pe.wait_ge(decay_exp[1], b * PAIRS + g)
                for h in range(2):
                    mm = pe.matmul(ps_c[:, h, :], pick_head[:, 2 * g + h, :], cT_now[:], start=True, stop=True)
                mm.then_inc(c_spread, 1)

            def score(b, g):
                pe.wait_ge(qk_lo_done, b * PAIRS + g + 1)
                for h in range(2):
                    pe.wait_ge(probs_done[h], b * PAIRS + g)
                    rows = slice(h * DH, (h + 1) * DH)
                    for out, j, i in ((slice(0, N), slice(0, P), slice(0, N)), (slice(N, TRI), slice(P, N), slice(P, N))):
                        mm = split_product(ps_s[h][:, out], [((qk_hi[g][rows, 1, j], qk_lo[g][rows, 1, j]),
                                                              (qk_hi[g][rows, 0, i], qk_lo[g][rows, 0, i]))])
                mm.then_inc(s_made, 1)

            def weighted_values(b, par, g):
                pe.wait_ge(v_done, VU * (b + 1))
                pe.wait_ge(o_normed, b * PAIRS + g)
                for h in range(2):
                    pe.wait_ge(probs_done[h], b * PAIRS + g + 1)
                    v = [v_aug[par][:, j, 2 * g + h, :] for j in range(NB)]
                    pe.matmul(o_view[:, 0, h, :], probs[h][:, 0:P], v[0], start=True, stop=True)
                    pe.matmul(o_view[:, 1, h, :], probs[h][:, P:N], v[0], start=True, stop=False)
                    mm = pe.matmul(o_view[:, 1, h, :], probs[h][:, N:TRI], v[1], start=False, stop=True)
                mm.then_inc(o_made, 1)

            def turn_o(b, g):
                pe.wait_ge(o_normed, b * PAIRS + g + 1)
                pe.wait_ge(oT_lo_done, b * PAIRS + g)
                for blk in range(NB):
                    mm = pe.transpose(ps_t[:, blk * P:(blk + 1) * P],
                                      o_norm[:, blk, :, :].rearrange("p h d -> p (h d)"), ident[:])
                mm.then_inc(oT_made, 1)

            def add_y(b, g):
                if g == 0:
                    pe.wait_ge(resid_done, b)
                pe.wait_ge(oT_lo_done, b * PAIRS + g + 1)
                for blk in range(NB):
                    rows = slice(blk * P, (blk + 1) * P)
                    for n, (l, r) in enumerate(((oT_hi[g % 2], wo_hi), (oT_hi[g % 2], wo_lo), (oT_lo[g % 2], wo_hi))):
                        mm = pe.matmul(ps_y[:, blk, :], l[:, rows], r[:, g, :], start=(g == 0 and blk == 0 and n == 0),
                                       stop=(g == PAIRS - 1 and n == 2), skip_group_check=True)
                mm.then_inc(y_added, 1)

            def sequence(b, par):
                for g in range(PAIRS):
                    spread_c(b, g)
                    score(b, g)
                    if has(b, 1) and g in (1, 2):
                        project_v(b + 1, g - 1, 0)
                    if exists(b, g, 1):
                        weighted_values(*back(b, par, g, 1))
                    if exists(b, g, 2):
                        before, _, pair = back(b, par, g, 2)
                        turn_o(before, pair)
                    if exists(b, g, 3):
                        before, _, pair = back(b, par, g, 3)
                        add_y(before, pair)
                    if has(b, 1):
                        project_qk(b + 1, g)
                        if g == 0:
                            project_z(b + 1)
                        if g in (1, 2):
                            project_v(b + 1, g - 1, 1)
                        if g == 4:
                            turn_dec(b + 1)
                        if g == 5:
                            sum_decay(b + 1)
                        if g == 6:
                            turn_c(b + 1)
                if has(b, 2):
                    turn_x(b + 2)

            pe.wait_ge(ident_ready, 1)
            turn_x(0)
            pe.wait_ge(consts_ready, 1)
            pe.wait_ge(wa_lo_done, 2)
            project_z(0)
            pe.wait_ge(w_lo_done, 2)
            for g in range(PAIRS):
                project_qk(0, g)
                if 1 <= g <= VU:
                    pe.wait_ge(w_lo_done, 3)
                    project_v(0, (g - 1) // NB, (g - 1) % NB)
                if g == VU + 2:
                    turn_dec(0)
            sum_decay(0)
            turn_c(0)
            turn_x(1)
            pe.wait_ge(w_lo_done, 4)
            all_sequences(pe, sequence)
            weighted_values(B - 1, (B - 1) % 2, PAIRS - 1)
            turn_o(B - 1, PAIRS - 2)
            add_y(B - 1, PAIRS - 3)
            turn_o(B - 1, PAIRS - 1)
            add_y(B - 1, PAIRS - 2)
            add_y(B - 1, PAIRS - 1)


def cross_attention(nc, sh, x1_dram, ctx_in, mask, wq, bq, wk, bk, wv, bv, wo, bo, router_w, x2_dram, x2_all, logitsT):
    B, N, D, H, NB, KC, S2, E = sh.B, sh.N, sh.D, sh.H, sh.NB, sh.KC, sh.S2, sh.E
    DK = D // H
    TH = P // DK
    G = 4
    GROUPS = H // G
    HALVES = TH // G
    GW = G * S2
    SCALE = float(DK) ** -0.5
    MASKED, OPEN = -1.0e9, 3.0e38
    with ExitStack() as ctx:
        def sb(name, shape, dt=F32):
            return ctx.enter_context(nc.sbuf_tensor(name, shape, dt))

        def ps(name, shape, dt=F32):
            return ctx.enter_context(nc.psum_tensor(name, shape, dt))

        def sem(name):
            return sh.semaphore(nc, name)

        ident, head_mask = sb("b_ident", [P, P]), sb("b_head_mask", [P, TH])
        w_raw = [sb(f"b_w_raw{n}", [P, KC, D]) for n in range(4)]
        wT = [sb(f"b_wT{n}", [P, KC, D]) for n in range(4)]
        wqT, wkT, wvT, woT = wT
        bq_col, bk_col = sb("b_bq_col", [P, KC]), sb("b_bk_col", [P, KC])
        bv_rows, bo_rows = sb("b_bv_rows", [P, D]), sb("b_bo_rows", [P, D])
        eps_col = sb("b_eps_col", [P, 1])
        x_in, x_res, x_bo = sb("b_x_in", [P, NB, D]), sb("b_x_res", [P, NB, D]), sb("b_x_bo", [P, NB, D])
        ctx_rows, ctxT = sb("b_ctx_rows", [P, D]), sb("b_ctxT", [P, KC, S2])
        mask_in, mask_cap = sb("b_mask_in", [P, NB, S2], I32), sb("b_mask_cap", [P, NB, S2])
        xT, qT, v = sb("b_xT", [P, KC, N]), sb("b_qT", [P, KC, N]), sb("b_v", [P, D])
        k_blocks = sb("b_k_blocks", [P, KC, TH, S2])
        probs = [sb(f"b_probs{n}", [P, H, S2]) for n in range(NB)]
        top = [sb(f"b_top{n}", [P, H]) for n in range(NB)]
        den = [sb(f"b_den{n}", [P, H]) for n in range(NB)]
        rden = [sb(f"b_rden{n}", [P, H]) for n in range(NB)]
        pT = [sb(f"b_pT{n}", [P, G, P]) for n in range(2)]
        o_norm = [sb(f"b_o_norm{n}", [P, D]) for n in range(NB)]
        oT = sb("b_oT", [P, KC, P])
        resid = sb("b_resid", [P, NB, D])
        stats, mv = sb("b_stats", [P, NB, 6]), sb("b_mv", [P, NB, 2])
        ln_var, rstd = sb("b_ln_var", [P, NB]), sb("b_rstd", [P, NB])
        x2, x2T = sb("b_x2", [P, NB, D]), sb("b_x2T", [P, KC, N])
        rw_rows, rwT = sb("b_rw_rows", [E, D]), sb("b_rwT", [P, KC, E])

        ps_s = ps("b_ps_s", [P, GROUPS, 512])
        ps_o_turns = ps("b_ps_o_turns", [P, 512])
        ps_mix = ps("b_ps_mix", [P, 512])
        ps_t = ps("b_ps_t", [P, G, P])
        ps_o = ps("b_ps_o", [P, 512])
        ps_oT = ps_y = ps_o_turns[:, 0:D]
        ps_lg = ps_o_turns[0:E, 0:N]
        ps_cT = ps_s[:, 0, 0:KC * S2].rearrange("p (k n) -> p k n", k=KC)
        ps_k = ps_s[:, 1, 0:KC * S2].rearrange("p (k n) -> p k n", k=KC)
        mix_rows = ps_mix[:].rearrange("p (k n) -> p k n", k=KC)

        loaded, consts_step, consts_ready = sem("b_loaded"), sem("b_consts_step"), sem("b_consts_ready")
        w_turned, w_kept = sem("b_w_turned"), sem("b_w_kept")
        x_in_loaded, x_res_loaded = sem("b_x_in_loaded"), sem("b_x_res_loaded")
        ctx_loaded, mask_loaded, x2_stored = sem("b_ctx_loaded"), sem("b_mask_loaded"), sem("b_x2_stored")
        vec_turns, pe_turns = sem("b_vec_turns"), sem("b_pe_turns")
        cap_step, cap_ready = sem("b_cap_step"), sem("b_cap_ready")
        xT_made, cT_made, q_made, k_made = sem("b_xT_made"), sem("b_cT_made"), sem("b_q_made"), sem("b_k_made")
        xT_kept, cT_kept, q_kept, k_kept = sem("b_xT_kept"), sem("b_cT_kept"), sem("b_q_kept"), sem("b_k_kept")
        v_made, x2T_made, lg_made = sem("b_v_made"), sem("b_x2T_made"), sem("b_lg_made")
        v_kept, x2T_kept, lg_kept = sem("b_v_kept"), sem("b_x2T_kept"), sem("b_lg_kept")
        x_bo_done, ln_step, var_ready, rstd_step, x2_ready = (
            sem("b_x_bo_done"), sem("b_ln_step"), sem("b_var_ready"), sem("b_rstd_step"), sem("b_x2_ready"))
        s_made, s_kept, top_done, shifted = sem("b_s_made"), sem("b_s_kept"), sem("b_top_done"), sem("b_shifted")
        exp_done, den_done, rden_done = sem("b_exp_done"), sem("b_den_done"), sem("b_rden_done")
        o_normed, oT_made, oT_kept, y_made, y_kept = (
            sem("b_o_normed"), sem("b_oT_made"), sem("b_oT_kept"), sem("b_y_made"), sem("b_y_kept"))
        pT_made, pT_kept, pT_used = sem("b_pT_made"), sem("b_pT_kept"), sem("b_pT_used")

        block = ctx.enter_context(nc.Block())
        x1_rows = x1_dram.rearrange("b (k p) d -> b p k d", p=P)
        x2_rows = x2_dram.rearrange("b (k p) d -> b p k d", p=P)
        mask_rows = mask.rearrange("b (k p) s -> b p k s", p=P)
        N_LOADS = 5 + 2 + 2

        def unit(b, blk):
            return b * NB + blk

        def all_sequences(eng, sequence):
            sequence(0, True, False)
            with eng.Fori(1, B - 1) as b:
                sequence(b, False, False)
            sequence(B - 1, False, True)

        @block.sync
        def _(sp):
            def load_x(b):
                sp.wait_ge(xT_made, b)
                sp.dma_start(x_in[:], x1_rows[b]).then_inc(x_in_loaded, 16)

            def load_ctx(b):
                sp.wait_ge(cT_made, b)
                sp.dma_start(ctx_rows[0:S2, :], ctx_in[b]).then_inc(ctx_loaded, 16)

            def load_mask(b):
                sp.wait_ge(cap_ready, b)
                sp.dma_start(mask_in[:], mask_rows[b]).then_inc(mask_loaded, 16)

            def load_residual(b):
                sp.wait_ge(x_bo_done, b)
                sp.dma_start(x_res[:], x1_rows[b]).then_inc(x_res_loaded, 16)

            def store_x2(b):
                sp.wait_ge(x2_ready, b + 1)
                sp.dma_start(x2_all[:, bass.ts(b, NB), :], x2[:]).then_inc(x2_stored, 16)
                sp.dma_start(x2_rows[b], x2[:]).then_inc(x2_stored, 16)

            sp.dma_start(x_in[:], x1_rows[0]).then_inc(x_in_loaded, 16)
            sp.dma_start(ctx_rows[0:S2, :], ctx_in[0]).then_inc(ctx_loaded, 16)
            for n, w in enumerate((wq, wk, wv, wo)):
                sp.dma_start(w_raw[n][:], w.rearrange("(k p) n -> p k n", p=P)).then_inc(loaded, 16)
            sp.dma_start(rw_rows[:], router_w).then_inc(loaded, 16)
            for col, b_in in ((bq_col, bq), (bk_col, bk)):
                sp.dma_start(col[:], b_in.rearrange("(k p) -> p k", p=P), allow_slow_non_contiguous=True)\
                    .then_inc(loaded, 16)
            for rows, b_in in ((bv_rows, bv), (bo_rows, bo)):
                sp.dma_start(rows[:], b_in.rearrange("(a n) -> a n", a=1).to_broadcast([P, D])).then_inc(loaded, 16)
            sp.dma_start(mask_in[:], mask_rows[0]).then_inc(mask_loaded, 16)
            sp.dma_start(x_res[:], x1_rows[0]).then_inc(x_res_loaded, 16)
            load_x(1)
            load_ctx(1)
            load_mask(1)
            load_residual(1)

            def sequence(b):
                load_x(b + 1)
                load_ctx(b + 1)
                load_mask(b + 1)
                load_residual(b + 1)
                store_x2(b - 1)

            with sp.Fori(1, B - 1) as b:
                sequence(b)
            store_x2(B - 2)
            store_x2(B - 1)
            sp.wait_ge(x2_stored, 32 * B)

        @block.gpsimd
        def _(pool):
            pool.memset(ident[:], 0.0).then_inc(consts_step, 1)
            pool.memset(head_mask[:], 1.0).then_inc(consts_step, 1)
            pool.wait_ge(consts_step, 2)
            pool.affine_select(out=ident[:], in_=ident[:], compare_op=ALU.not_equal, fill=1.0, base=0,
                               pattern=[[-1, P]], channel_multiplier=1).then_inc(consts_step, 1)
            pool.affine_select(out=head_mask[:], in_=head_mask[:], compare_op=ALU.is_ge, fill=0.0, base=0,
                               pattern=[[-DK, TH]], channel_multiplier=1).then_inc(consts_step, 1)
            pool.wait_ge(consts_step, 4)
            pool.affine_select(out=head_mask[:], in_=head_mask[:], compare_op=ALU.is_ge, fill=0.0, base=DK - 1,
                               pattern=[[DK, TH]], channel_multiplier=-1).then_inc(consts_step, 1)
            pool.memset(eps_col[:], LN_EPS).then_inc(consts_step, 1)
            pool.wait_ge(consts_step, 6)
            pool.memset(x_bo[:], 0.0).then_inc(consts_ready, 1)
            pool.wait_ge(loaded, 16 * N_LOADS)
            pool.wait_ge(consts_ready, 1)

            def add_bias(b, first):
                pool.wait_ge(x_res_loaded, 16 * (b + 1))
                if not first:
                    pool.wait_ge(y_kept, unit(b, 0))
                pool.tensor_tensor(x_bo[:], x_res[:], bo_rows[:].unsqueeze(1).to_broadcast([P, NB, D]), ALU.add)\
                    .then_inc(x_bo_done, 1)

            def shift(b, blk):
                pool.wait_ge(top_done, unit(b, blk) + 1)
                pool.tensor_tensor(probs[blk][:], probs[blk][:], top[blk][:].unsqueeze(2).to_broadcast([P, H, S2]),
                                   ALU.subtract).then_inc(shifted, 1)

            def sequence(b, first, last):
                shift(b, 1)
                add_bias(b, first)
                if not last:
                    shift(b + 1, 0)

            shift(0, 0)
            all_sequences(pool, sequence)

        @block.scalar
        def _(act):
            act.wait_ge(loaded, 16 * N_LOADS)
            act.wait_ge(consts_ready, 1)
            for n in range(4):
                for k in range(KC):
                    act.wait_ge(w_turned, n * KC + k + 1)
                    act.copy(wT[n][:, k, :], (ps_o_turns, ps_mix)[k][:, 0:D]).then_inc(w_kept, 1)
            act.wait_ge(w_turned, 4 * KC + 1)
            act.copy(rwT[:], ps_t[:, 0, 0:KC * E].rearrange("p (k e) -> p k e", k=KC)).then_inc(w_kept, 1)

            def keep_xT(b):
                act.wait_ge(xT_made, b + 1)
                act.copy(xT[:], mix_rows).then_inc(xT_kept, 1)

            def keep_ctxT(b):
                act.wait_ge(cT_made, b + 1)
                act.copy(ctxT[:], ps_cT).then_inc(cT_kept, 1)

            def keep_q(b):
                act.wait_ge(q_made, b + 1)
                for k in range(KC):
                    ins = act.activation(qT[:, k, :], mix_rows[:, k, :], ACT.Identity, bias=bq_col[:, k:k + 1])
                ins.then_inc(q_kept, 1)

            def keep_x2T(b):
                act.wait_ge(x2T_made, b + 1)
                act.copy(x2T[:], mix_rows).then_inc(x2T_kept, 1)

            def exponentials(b, blk):
                act.wait_ge(shifted, unit(b, blk) + 1)
                act.activation(probs[blk][:], probs[blk][:], ACT.Exp).then_inc(exp_done, 1)

            def keep_pT(b, blk, g):
                n = unit(b, blk) * GROUPS + g
                act.wait_ge(pT_made, n + 1)
                if not isinstance(n, int) or n >= 2:
                    act.wait_ge(pT_used, n - 1)
                act.copy(pT[g % 2][0:S2, :, :], ps_t[0:S2, :, :]).then_inc(pT_kept, 1)

            def root(b):
                act.wait_ge(var_ready, b + 1)
                act.activation(ln_var[:], mv[:, :, 1], ACT.Ln, bias=eps_col[:]).then_inc(rstd_step, 1)
                act.wait_ge(rstd_step, 2 * b + 1)
                act.activation(rstd[:], ln_var[:], ACT.Exp, scale=-0.5).then_inc(rstd_step, 1)

            def sequence(b, first, last):
                if not last:
                    keep_xT(b + 1)
                for g in range(GROUPS):
                    keep_pT(b, 0, g)
                    if not last and g == 1:
                        keep_ctxT(b + 1)
                    if not last and g == 2:
                        keep_q(b + 1)
                exponentials(b, 1)
                if not first:
                    root(b - 1)
                for g in range(GROUPS):
                    keep_pT(b, 1, g)
                    if not first and g == 3:
                        keep_x2T(b - 1)
                if not last:
                    exponentials(b + 1, 0)

            keep_xT(0)
            keep_ctxT(0)
            keep_q(0)
            exponentials(0, 0)
            all_sequences(act, sequence)
            root(B - 1)
            keep_x2T(B - 1)

        @block.vector
        def _(vec):
            vec.wait_ge(loaded, 16 * N_LOADS)
            vec.wait_ge(consts_ready, 1)

            def keep_k(b):
                vec.wait_ge(k_made, b + 1)
                for k in range(KC):
                    ins = vec.scalar_tensor_tensor(
                        k_blocks[:, k, :, :], ps_k[:, k, :].unsqueeze(1).to_broadcast([P, TH, S2]), bk_col[:, k:k + 1],
                        head_mask[:].unsqueeze(2).to_broadcast([P, TH, S2]), ALU.add, ALU.mult)
                ins.then_inc(k_kept, 1)

            def keep_v(b):
                vec.wait_ge(v_made, b + 1)
                vec.tensor_tensor(v[0:S2, :], ps_mix[0:S2, 0:D], bv_rows[0:S2, :], ALU.add).then_inc(v_kept, 1)

            def mask_caps(b):
                vec.wait_ge(mask_loaded, 16 * (b + 1))
                if not isinstance(b, int) or b:
                    vec.wait_ge(s_kept, unit(b, 0))
                vec.tensor_scalar(mask_cap[:], mask_in[:], 0.0, OPEN, ALU.not_equal, ALU.mult).then_inc(cap_step, 1)
                vec.wait_ge(cap_step, b + 1)
                vec.tensor_scalar(mask_cap[:], mask_cap[:], MASKED, None, ALU.add).then_inc(cap_ready, 1)

            def keep_scores(b, blk):
                n = unit(b, blk)
                vec.wait_ge(s_made, n + 1)
                vec.wait_ge(cap_ready, b + 1)
                if not isinstance(n, int) or n >= NB:
                    vec.wait_ge(pT_made, (n - NB + 1) * GROUPS)
                    vec.wait_ge(den_done, n - NB + 1)
                for g in range(GROUPS):
                    ins = vec.scalar_tensor_tensor(
                        probs[blk][:, g * G:(g + 1) * G, :], ps_s[:, g, 0:GW].rearrange("p (h k) -> p h k", h=G), SCALE,
                        mask_cap[:, blk, :].unsqueeze(1).to_broadcast([P, G, S2]), ALU.mult, ALU.min)
                ins.then_inc(s_kept, 1)
                vec.wait_ge(s_kept, n + 1)
                vec.tensor_reduce(top[blk][:], probs[blk][:], AX.X, ALU.max).then_inc(top_done, 1)

            def sums(b, blk):
                n = unit(b, blk)
                vec.wait_ge(exp_done, n + 1)
                vec.tensor_reduce(den[blk][:], probs[blk][:], AX.X, ALU.add).then_inc(den_done, 1)
                vec.wait_ge(den_done, n + 1)
                vec.reciprocal(rden[blk][:], den[blk][:]).then_inc(rden_done, 1)

            def normalise(b, blk):
                n = unit(b, blk)
                vec.wait_ge(pT_used, (n + 1) * GROUPS)
                vec.wait_ge(rden_done, n + 1)
                if not isinstance(n, int) or n >= NB:
                    vec.wait_ge(oT_made, n - NB + 1)
                vec.tensor_tensor(o_norm[blk][:].rearrange("p (h d) -> p h d", d=DK),
                                  ps_o[:, 0:D].rearrange("p (h d) -> p h d", d=DK),
                                  rden[blk][:].unsqueeze(2).to_broadcast([P, H, DK]), ALU.mult).then_inc(o_normed, 1)

            def keep_oT(b, blk):
                vec.wait_ge(oT_made, unit(b, blk) + 1)
                vec.tensor_copy(oT[:], ps_oT.rearrange("p (k n) -> p k n", k=KC)).then_inc(oT_kept, 1)

            def add_residual(b, blk):
                vec.wait_ge(x_bo_done, b + 1)
                vec.wait_ge(y_made, unit(b, blk) + 1)
                if blk == 0 and (not isinstance(b, int) or b):
                    vec.wait_ge(x2_ready, b)
                vec.tensor_tensor(resid[:, blk, :], ps_y, x_bo[:, blk, :], ALU.add).then_inc(y_kept, 1)

            def statistics(b):
                vec.wait_ge(y_kept, unit(b, NB))
                for blk in range(NB):
                    vec.bn_stats(stats[:, blk, :], resid[:, blk, :]).then_inc(ln_step, 1)
                vec.wait_ge(ln_step, NB * b + NB)
                vec.sem_inc(vec_turns, 1)
                for blk in range(NB):
                    ins = vec.bn_aggr(mv[:, blk, :], stats[:, blk, :])
                ins.then_inc(var_ready, 1)

            def scale_x2(b):
                vec.wait_ge(rstd_step, 2 * b + 2)
                if not isinstance(b, int) or b:
                    vec.wait_ge(x2_stored, 32 * b)
                    vec.wait_ge(x2T_made, b)
                for blk in range(NB):
                    ins = vec.tensor_scalar(x2[:, blk, :], resid[:, blk, :], mv[:, blk, 0:1], rstd[:, blk:blk + 1],
                                            ALU.subtract, ALU.mult)
                ins.then_inc(x2_ready, 1)

            def keep_logits(b):
                vec.wait_ge(lg_made, b + 1)
                vec.tensor_copy(logitsT[:, bass.ts(b, N)], ps_lg).then_inc(lg_kept, 1)

            def sequence(b, first, last):
                if not first:
                    keep_oT(b - 1, 1)
                keep_scores(b, 1)
                if not last:
                    mask_caps(b + 1)
                sums(b, 0)
                if not first:
                    add_residual(b - 1, 1)
                    statistics(b - 1)
                if not last:
                    keep_k(b + 1)
                normalise(b, 0)
                keep_oT(b, 0)
                if not last:
                    keep_scores(b + 1, 0)
                if not first:
                    scale_x2(b - 1)
                sums(b, 1)
                add_residual(b, 0)
                normalise(b, 1)
                if not first:
                    keep_logits(b - 1)
                if not last:
                    keep_v(b + 1)

            mask_caps(0)
            keep_k(0)
            keep_v(0)
            keep_scores(0, 0)
            all_sequences(vec, sequence)
            keep_oT(B - 1, 1)
            add_residual(B - 1, 1)
            statistics(B - 1)
            scale_x2(B - 1)
            keep_logits(B - 1)

        @block.tensor
        def _(pe):
            pe.wait_ge(loaded, 16 * N_LOADS)
            pe.wait_ge(consts_ready, 1)
            for n in range(4):
                for k in range(KC):
                    if n:
                        pe.wait_ge(w_kept, (n - 1) * KC + k + 1)
                    for o in range(KC):
                        mm = pe.transpose((ps_o_turns, ps_mix)[k][:, o * P:(o + 1) * P], w_raw[n][:, o, k * P:(k + 1) * P], ident[:])
                    mm.then_inc(w_turned, 1)
            for k in range(KC):
                mm = pe.transpose(ps_t[:, 0, k * E:(k + 1) * E], rw_rows[:, k * P:(k + 1) * P], ident[0:E, 0:E])
            mm.then_inc(w_turned, 1)
            pe.wait_ge(w_kept, 4 * KC + 1)

            def turn_x1(b):
                pe.wait_ge(x_in_loaded, 16 * (b + 1))
                if not isinstance(b, int) or b:
                    pe.wait_ge(v_kept, b)
                for k in range(KC):
                    for blk in range(NB):
                        mm = pe.transpose(mix_rows[:, k, blk * P:(blk + 1) * P], x_in[:, blk, k * P:(k + 1) * P], ident[:])
                mm.then_inc(xT_made, 1)

            def turn_ctx(b):
                pe.wait_ge(ctx_loaded, 16 * (b + 1))
                if not isinstance(b, int) or b:
                    pe.wait_ge(s_kept, unit(b, 0))
                for k in range(KC):
                    pe.sem_inc(pe_turns, 1)
                    mm = pe.transpose(ps_cT[:, k, :], ctx_rows[0:S2, k * P:(k + 1) * P], ident[0:S2, 0:S2])
                mm.then_inc(cT_made, 1)

            def project_qk(b):
                pe.wait_ge(xT_kept, b + 1)
                for t in range(KC):
                    for k in range(KC):
                        mm = pe.matmul(mix_rows[:, t, :], wqT[:, k, t * P:(t + 1) * P], xT[:, k, :],
                                       start=(k == 0), stop=(k == KC - 1))
                mm.then_inc(q_made, 1)
                pe.wait_ge(cT_kept, b + 1)
                for t in range(KC):
                    for k in range(KC):
                        mm = pe.matmul(ps_k[:, t, :], wkT[:, k, t * P:(t + 1) * P], ctxT[:, k, :],
                                       start=(k == 0), stop=(k == KC - 1))
                mm.then_inc(k_made, 1)

            def project_v(b):
                pe.wait_ge(q_kept, b + 1)
                if not isinstance(b, int) or b >= 2:
                    pe.wait_ge(x2T_kept, b - 1)
                for k in range(KC):
                    mm = pe.matmul(ps_mix[0:S2, 0:D], ctxT[:, k, :], wvT[:, k, :], start=(k == 0), stop=(k == KC - 1))
                mm.then_inc(v_made, 1)

            def score(b, blk):
                n = unit(b, blk)
                pe.wait_ge(q_kept, b + 1)
                pe.wait_ge(k_kept, b + 1)
                if not isinstance(n, int) or n:
                    pe.wait_ge(s_kept, n)
                for g in range(GROUPS):
                    t, half = g // HALVES, g % HALVES
                    mm = pe.matmul(ps_s[:, g, 0:GW], qT[:, t, blk * P:(blk + 1) * P],
                                   k_blocks[:, t, half * G:(half + 1) * G, :].rearrange("p h k -> p (h k)"),
                                   start=True, stop=True)
                mm.then_inc(s_made, 1)

            def turn_probs(b, blk, g):
                n = unit(b, blk) * GROUPS + g
                if g == 0:
                    pe.wait_ge(exp_done, unit(b, blk) + 1)
                if not isinstance(n, int) or n:
                    pe.wait_ge(pT_kept, n)
                for s in range(G):
                    mm = pe.transpose(ps_t[0:S2, s, :], probs[blk][:, g * G + s, :], ident[:])
                mm.then_inc(pT_made, 1)

            def weigh_values(b, blk, g):
                n = unit(b, blk)
                if g == 0:
                    pe.wait_ge(v_kept, b + 1)
                    if not isinstance(n, int) or n:
                        pe.wait_ge(o_normed, n)
                pe.wait_ge(pT_kept, n * GROUPS + g + 1)
                for s in range(G):
                    h = g * G + s
                    mm = pe.matmul(ps_o[:, h * DK:(h + 1) * DK], pT[g % 2][0:S2, s, :],
                                   v[0:S2, h * DK:(h + 1) * DK], start=True, stop=True)
                mm.then_inc(pT_used, 1)

            def turn_o(b, blk):
                n = unit(b, blk)
                pe.wait_ge(o_normed, n + 1)
                if not isinstance(n, int) or n:
                    pe.wait_ge(y_kept, n)
                if blk == 1 and (not isinstance(b, int) or b):
                    pe.wait_ge(lg_kept, b)
                for k in range(KC):
                    mm = pe.transpose(ps_oT[:, k * P:(k + 1) * P], o_norm[blk][:, k * P:(k + 1) * P], ident[:])
                mm.then_inc(oT_made, 1)

            def project_o(b, blk):
                n = unit(b, blk)
                pe.wait_ge(oT_kept, n + 1)
                for k in range(KC):
                    mm = pe.matmul(ps_y, oT[:, k, :], woT[:, k, :], start=(k == 0), stop=(k == KC - 1))
                mm.then_inc(y_made, 1)

            def turn_x2(b):
                pe.wait_ge(x2_ready, b + 1)
                if not isinstance(b, int) or b < B - 2:
                    pe.wait_ge(q_kept, b + 3)
                elif b == B - 1:
                    pe.wait_ge(x2T_kept, b)
                for k in range(KC):
                    for blk in range(NB):
                        mm = pe.transpose(mix_rows[:, k, blk * P:(blk + 1) * P], x2[:, blk, k * P:(k + 1) * P], ident[:])
                mm.then_inc(x2T_made, 1)

            def route(b):
                pe.wait_ge(x2T_kept, b + 1)
                pe.wait_ge(y_kept, unit(b, 3) if not isinstance(b, int) or b < B - 1 else unit(B, 0))
                for k in range(KC):
                    mm = pe.matmul(ps_lg, rwT[:, k, :], x2T[:, k, :], start=(k == 0), stop=(k == KC - 1))
                mm.then_inc(lg_made, 1)

            def sequence(b, first, last):
                score(b, 1)
                if not first:
                    turn_o(b - 1, 1)
                if not last:
                    turn_x1(b + 1)
                turn_probs(b, 0, 0)
                if not first:
                    project_o(b - 1, 1)
                for g in range(1, GROUPS):
                    turn_probs(b, 0, g)
                    weigh_values(b, 0, g - 1)
                    if not last and g == 1:
                        turn_ctx(b + 1)
                    if not last and g == 2:
                        project_qk(b + 1)
                weigh_values(b, 0, GROUPS - 1)
                if not last:
                    score(b + 1, 0)
                turn_o(b, 0)
                turn_probs(b, 1, 0)
                project_o(b, 0)
                for g in range(1, GROUPS):
                    turn_probs(b, 1, g)
                    weigh_values(b, 1, g - 1)
                    if not first and g == 3:
                        turn_x2(b - 1)
                weigh_values(b, 1, GROUPS - 1)
                if not first:
                    route(b - 1)
                if not last:
                    project_v(b + 1)

            turn_x1(0)
            turn_ctx(0)
            project_qk(0)
            project_v(0)
            score(0, 0)
            all_sequences(pe, sequence)
            turn_o(B - 1, 1)
            project_o(B - 1, 1)
            turn_x2(B - 1)
            route(B - 1)


class Plan:

    def __init__(self, sh):
        self.T = 512
        self.SHIFT = self.T.bit_length() - 1
        self.TOKENS = sh.B * sh.N
        self.BLOCKS = self.TOKENS // P
        self.TILES = (2 * self.TOKENS - sh.E) // self.T + sh.E
        self.ROWS = self.TILES * self.T
        self.COLS = self.ROWS // P
        assert self.TOKENS <= 4096


def route_tokens(nc, sh, plan, logitsT, slots, slot_col, slot_row, gates, tile_table):
    E, D = sh.E, sh.D
    NBK, T, TILES = plan.BLOCKS, plan.T, plan.TILES
    with ExitStack() as ctx:
        def sb(name, shape, dt=F32):
            return ctx.enter_context(nc.sbuf_tensor(name, shape, dt))

        def sem(name):
            return sh.semaphore(nc, name)

        shifted, probs, rest = sb("r_shifted", [P, NBK, E]), sb("r_probs", [P, NBK, E]), sb("r_rest", [P, NBK, E])
        same, key = sb("r_same", [P, NBK, E]), sb("r_key", [P, NBK, E])
        picked = [sb(f"r_picked{k}", [P, NBK, E]) for k in range(2)]
        both = sb("r_both", [P, NBK, E])
        top, tot = [sb(f"r_top{k}", [P, NBK]) for k in range(2)], sb("r_tot", [P, NBK])
        col, rcol = sb("r_col", [P, NBK]), sb("r_rcol", [P, NBK])
        order = sb("r_order", [P, E])
        order_i = sb("r_order_i", [P, E], I32)
        first_row = sb("r_first_row", [P, E])
        tile_no, tile_no_i = sb("r_tile_no", [P, TILES]), sb("r_tile_no_i", [P, TILES], I32)
        before, ones = sb("r_before", [P, P]), sb("r_ones", [P, P])
        ident = sb("r_ident", [E, E])
        logits = ctx.enter_context(nc.psum_tensor("r_ps_logits", [P, NBK, E], F32))
        sums = [sb(f"r_sums{k}", [P, NBK, E]) for k in range(2)]
        in_block, rank = sb("r_in_block", [P, NBK, E]), sb("r_rank", [P, NBK, E])
        slot_f, slot_i = sb("r_slot_f", [P, NBK]), sb("r_slot_i", [P, NBK], I32)
        tiles_i, n_tiles = sb("r_tiles_i", [P, E], I32), sb("r_n_tiles", [P, E])
        ends = [sb(f"r_ends{k}", [P, E]) for k in range(2)]
        expert_of = sb("r_expert_of", [P, TILES])
        ps_rank = ctx.enter_context(nc.psum_tensor("r_ps_rank", [P, 2, NBK * E], F32))

        consts_step, consts_ready, step = sem("r_consts_step"), sem("r_consts_ready"), sem("r_step")
        ident_step, ident_ready, logits_turned = sem("r_ident_step"), sem("r_ident_ready"), sem("r_logits_turned")
        shifted_done, exp_done, picks_ready, ranked = (
            sem("r_shifted_done"), sem("r_exp_done"), sem("r_picks_ready"), sem("r_ranked"))
        slots_ready = sem("r_slots_ready")

        block = ctx.enter_context(nc.Block())

        @block.gpsimd
        def _(pool):
            pool.memset(ident[:], 0.0).then_inc(ident_step, 1)
            pool.wait_ge(ident_step, 1)
            pool.affine_select(out=ident[:], in_=ident[:], compare_op=ALU.not_equal, fill=1.0, base=0,
                               pattern=[[-1, E]], channel_multiplier=1).then_inc(ident_ready, 1)
            pool.iota(order_i[:], pattern=[[-1, E]], base=E, channel_multiplier=0).then_inc(consts_step, 1)
            pool.iota(tile_no_i[:], pattern=[[1, TILES]], base=0, channel_multiplier=0).then_inc(consts_step, 1)
            pool.memset(ones[:], 1.0).then_inc(consts_step, 1)
            pool.wait_ge(consts_step, 3)
            pool.affine_select(out=before[:], in_=ones[:], compare_op=ALU.is_gt, fill=0.0, base=0,
                               pattern=[[1, P]], channel_multiplier=-1).then_inc(consts_ready, 1)

        @block.scalar
        def _(act):
            act.wait_ge(shifted_done, 1)
            act.activation(probs[:], shifted[:], ACT.Exp).then_inc(exp_done, 1)

        @block.tensor
        def _(pe):
            pe.wait_ge(ident_ready, 1)
            for n in range(NBK):
                mm = pe.transpose(logits[:, n, :], logitsT[:, n * P:(n + 1) * P], ident[:])
            mm.then_inc(logits_turned, 1)
            pe.wait_ge(picks_ready, 1)
            pe.wait_ge(consts_ready, 1)
            flat = both[:].rearrange("p n e -> p (n e)")
            pe.matmul(ps_rank[:, 0, :], before[:], flat, start=True, stop=True)
            pe.matmul(ps_rank[:, 1, :], ones[:], flat, start=True, stop=True).then_inc(ranked, 1)

        @block.vector
        def _(vec):
            steps = [0]

            def link(ins):
                steps[0] += 1
                ins.then_inc(step, 1)
                vec.wait_ge(step, steps[0])

            def over(cols):
                return cols.unsqueeze(2).to_broadcast([P, NBK, E])

            def each_block(row):
                return row.unsqueeze(1).to_broadcast([P, NBK, E])

            vec.wait_ge(consts_ready, 1)
            link(vec.tensor_copy(order[:], order_i[:]))
            link(vec.tensor_copy(tile_no[:], tile_no_i[:]))
            vec.wait_ge(logits_turned, 1)
            link(vec.tensor_reduce(col[:], logits[:], AX.X, ALU.max))
            vec.tensor_tensor(shifted[:], logits[:], over(col[:]), ALU.subtract).then_inc(shifted_done, 1)
            vec.wait_ge(exp_done, 1)
            link(vec.tensor_reduce(col[:], probs[:], AX.X, ALU.add))
            link(vec.reciprocal(rcol[:], col[:]))
            link(vec.tensor_tensor(probs[:], probs[:], over(rcol[:]), ALU.mult))
            for k, left in ((0, probs), (1, rest)):
                link(vec.tensor_reduce(top[k][:], left[:], AX.X, ALU.max))
                link(vec.tensor_tensor(same[:], left[:], over(top[k][:]), ALU.is_equal))
                link(vec.tensor_tensor(key[:], same[:], each_block(order[:]), ALU.mult))
                link(vec.tensor_reduce(col[:], key[:], AX.X, ALU.max))
                link(vec.tensor_tensor(picked[k][:], key[:], over(col[:]), ALU.is_equal))
                if k == 0:
                    link(vec.scalar_tensor_tensor(rest[:], picked[0][:], -2.0, probs[:], ALU.mult, ALU.add))
            link(vec.tensor_tensor(both[:], picked[0][:], picked[1][:], ALU.add))
            vec.tensor_tensor(tot[:], top[0][:], top[1][:], ALU.add).then_inc(picks_ready, 1)
            vec.wait_ge(picks_ready, 1)
            link(vec.tensor_scalar(tot[:], tot[:], 1e-9, None, ALU.add))
            link(vec.reciprocal(rcol[:], tot[:]))
            for k in range(2):
                link(vec.tensor_tensor(gates[k][:], top[k][:], rcol[:], ALU.mult))
            vec.wait_ge(ranked, 1)
            link(vec.tensor_copy(in_block[:], ps_rank[:, 0, :].rearrange("p (n e) -> p n e", e=E)))
            link(vec.tensor_copy(sums[0][:], ps_rank[:, 1, :].rearrange("p (n e) -> p n e", e=E)))
            a, b = sums
            d = 1
            while d < NBK:
                link(vec.tensor_copy(b[:, 0:d, :], a[:, 0:d, :]))
                link(vec.tensor_tensor(b[:, d:NBK, :], a[:, d:NBK, :], a[:, 0:NBK - d, :], ALU.add))
                a, b = b, a
                d *= 2
            link(vec.tensor_tensor(rank[:], a[:], ps_rank[:, 1, :].rearrange("p (n e) -> p n e", e=E), ALU.subtract))
            link(vec.tensor_tensor(rank[:], rank[:], in_block[:], ALU.add))
            link(vec.tensor_scalar(n_tiles[:], a[:, NBK - 1, :], float(T - 1), None, ALU.add))
            link(vec.tensor_copy(tiles_i[:], n_tiles[:]))
            link(vec.tensor_scalar(tiles_i[:], tiles_i[:], plan.SHIFT, None, ALU.logical_shift_right))
            link(vec.tensor_copy(n_tiles[:], tiles_i[:]))
            a, b = ends
            link(vec.tensor_copy(a[:], n_tiles[:]))
            d = 1
            while d < E:
                link(vec.tensor_copy(b[:, 0:d], a[:, 0:d]))
                link(vec.tensor_tensor(b[:, d:E], a[:, d:E], a[:, 0:E - d], ALU.add))
                a, b = b, a
                d *= 2
            link(vec.tensor_tensor(first_row[:], a[:], n_tiles[:], ALU.subtract))
            link(vec.tensor_scalar(first_row[:], first_row[:], float(T), None, ALU.mult))
            link(vec.tensor_tensor(rank[:], rank[:], each_block(first_row[:]), ALU.add))
            for k in range(2):
                link(vec.tensor_tensor(key[:], picked[k][:], rank[:], ALU.mult))
                link(vec.tensor_reduce(slot_f[:], key[:], AX.X, ALU.add))
                vec.tensor_copy(slots[k][:], slot_f[:]).then_inc(slots_ready, 1)
                vec.wait_ge(slots_ready, k + 1)
                link(vec.tensor_copy(slot_i[:], slot_f[:]))
                link(vec.tensor_scalar(slot_i[:], slot_i[:], P.bit_length() - 1, None, ALU.logical_shift_right))
                link(vec.tensor_copy(slot_col[k][:], slot_i[:]))
                link(vec.scalar_tensor_tensor(slot_row[k][:], slot_col[k][:], -float(P), slot_f[:], ALU.mult, ALU.add))
            link(vec.tensor_scalar(expert_of[:], tile_no[:], a[:, 0:1], None, ALU.is_ge))
            for e in range(1, E - 1):
                link(vec.scalar_tensor_tensor(expert_of[:], tile_no[:], a[:, e:e + 1], expert_of[:], ALU.is_ge, ALU.add))
            link(vec.tensor_copy(tile_table[:], expert_of[0:1, :]))


def run_experts(nc, sh, plan, x2_dram, slot_col, slot_row, tile_table, gate_w, gate_b, up_w, up_b, down_w, down_b, y_sorted):
    E, D, FF, KC = sh.E, sh.D, sh.FF, sh.KC
    T, TILES = plan.T, plan.TILES
    TB, FC = T // P, FF // P
    NBK, COLS = plan.BLOCKS, plan.COLS
    HOT = 8
    BATCHES = 2 * NBK // HOT
    with ExitStack() as ctx:
        def sb(name, shape, dt=F32):
            return ctx.enter_context(nc.sbuf_tensor(name, shape, dt))

        def ps(name, shape, dt=F32):
            return ctx.enter_context(nc.psum_tensor(name, shape, dt))

        def sem(name):
            return sh.semaphore(nc, name)

        def sems(name):
            return [sem(f"{name}{n}") for n in range(2)]

        ident = sb("e_ident", [P, P])
        bias_rows, bias_table = sb("e_bias_rows", [2 * E * FC, P]), sb("e_bias_table", [P, 2, E, FC])
        where = sb("e_where", [1, 2], I32)
        gu_raw = [sb(f"e_gu_raw{n}", [P, KC, 2 * FF]) for n in range(2)]
        dn_raw = [sb(f"e_dn_raw{n}", [P, FC, D]) for n in range(2)]
        gu_hi, gu_lo = ([sb(f"e_gu_{x}{n}", [P, KC, 2 * FF], F32R) for n in range(2)] for x in ("hi", "lo"))
        dn_hi, dn_lo = ([sb(f"e_dn_{x}{n}", [P, FC, D], F32R) for n in range(2)] for x in ("hi", "lo"))
        bias = [sb(f"e_bias{n}", [P, 2, FC]) for n in range(2)]
        dn_bias = [sb(f"e_dn_bias{n}", [P, D]) for n in range(2)]
        x_in = [sb(f"e_x_in{n}", [P, TB, D]) for n in range(2)]
        count_i, count = sb("e_count_i", [P, P], I32), sb("e_count", [P, P])
        number_i, number = sb("e_number_i", [P, NBK], I32), sb("e_number", [P, NBK])
        row_hot = [sb(f"e_row_hot{n}", [P, HOT, P], F32R) for n in range(2)]
        col_hot = [sb(f"e_col_hot{n}", [P, HOT, COLS], F32R) for n in range(2)]
        token = sb("e_token", [P, COLS])
        index = [sb(f"e_index{n}", [P, TB], U32) for n in range(2)]
        xT_hi, xT_lo = ([sb(f"e_xT_{x}{n}", [P, KC, T], F32R) for n in range(2)] for x in ("hi", "lo"))
        gate = [sb(f"e_gate{n}", [P, T]) for n in range(2)]
        hid = [sb(f"e_hid{n}", [P, T]) for n in range(2)]
        hid_hi, hid_lo = sb("e_hid_hi", [P, FC, T], F32R), sb("e_hid_lo", [P, FC, T], F32R)
        y_out = [sb(f"e_y_out{n}", [P, TB, D]) for n in range(2)]
        ps_x = [ps(f"e_ps_x{k}", [P, T]) for k in range(KC)]
        ps_g, ps_u, ps_y = ([ps(f"e_ps_{x}{n}", [P, 512]) for n in range(2)] for x in "guy")

        consts_step, rows_loaded, table_turned, table_ready = (
            sem("e_consts_step"), sem("e_rows_loaded"), sem("e_table_turned"), sem("e_table_ready"))
        where_loaded, sp_turns, pool_turns = sem("e_where_loaded"), sem("e_sp_turns"), sem("e_pool_turns")
        w_loaded, b_loaded = sems("e_w_loaded"), sems("e_b_loaded")
        x_loaded, y_stored = sems("e_x_loaded"), sems("e_y_stored")
        counts_ready, count_step = sem("e_counts_ready"), sem("e_count_step")
        hot_ready, hot_used, token_kept, index_ready = (
            sem("e_hot_ready"), sem("e_hot_used"), sem("e_token_kept"), sems("e_index_ready"))
        gu_hi_done, gu_lo_done, dn_hi_done, dn_lo_done = (
            sems("e_gu_hi_done"), sems("e_gu_lo_done"), sems("e_dn_hi_done"), sems("e_dn_lo_done"))
        x_turned, x_hi, x_lo = sem("e_x_turned"), sem("e_x_hi"), sem("e_x_lo")
        gu_made, gate_done, hid_done, hid_hi_done, hid_lo_done = (
            sems("e_gu_made"), sems("e_gate_done"), sems("e_hid_done"), sems("e_hid_hi_done"), sems("e_hid_lo_done"))
        y_made, y_kept = sems("e_y_made"), sems("e_y_kept")

        block = ctx.enter_context(nc.Block())
        W_LOADS, B_LOADS = 3, 2

        def all_tiles(eng, tile):
            for t in range(2):
                tile(t, t, 0)
            with eng.Fori(1, (TILES - 2) // 2) as i:
                for par in range(2):
                    tile(2 * i + par, par, i)
            for t in range((TILES - 2) // 2 * 2, TILES):
                tile(t, t % 2, t // 2)

        def has(t, ahead):
            return not isinstance(t, int) or 0 <= t + ahead < TILES

        @block.sync
        def _(sp):
            for n, b in enumerate((gate_b, up_b)):
                sp.dma_start(bias_rows[n * E * FC:(n + 1) * E * FC, :], b.rearrange("e (f p) -> (e f) p", p=P))\
                    .then_inc(rows_loaded, 16)

            def experts(t, first, count, loads):
                sp.dma_start(where[0:1, 0:count], tile_table[0:1, bass.ds(t + first, count)]).then_inc(where_loaded, 16)
                sp.wait_ge(where_loaded, 16 * loads)
                sp.sem_inc(sp_turns, 1)
                return [sp.value_load(where[0:1, n:n + 1], min_val=0, max_val=E - 1) for n in range(count)]

            def load_weights(e, par):
                for n, w in enumerate((gate_w, up_w)):
                    sp.dma_start(gu_raw[par][:, :, n * FF:(n + 1) * FF],
                                 w[bass.ds(e, 1)].rearrange("a (k p) f -> p (a k) f", p=P)).then_inc(w_loaded[par], 16)
                sp.dma_start(dn_raw[par][:], down_w[bass.ds(e, 1)].rearrange("a (f p) d -> p (a f) d", p=P))\
                    .then_inc(w_loaded[par], 16)

            def load_biases(e, par):
                sp.dma_start(bias[par][:], bias_table[:, :, bass.ds(e, 1), :].rearrange("p n a f -> p n (a f)"))\
                    .then_inc(b_loaded[par], 16)
                sp.dma_start(dn_bias[par][:], down_b[bass.ds(e, 1), :].to_broadcast([P, D])).then_inc(b_loaded[par], 16)

            def store(t, par):
                for n in range(2):
                    sp.wait_ge(y_kept[n], (t + 1) * (TB // 2))
                sp.dma_start(y_sorted[bass.ts(t, T), :].rearrange("(k p) d -> p k d", p=P), y_out[par][:])\
                    .then_inc(y_stored[par], 16)

            def tile(t, par, turn):
                if has(t, 2):
                    sp.wait_ge(gu_lo_done[par], turn + 1)
                    sp.wait_ge(dn_lo_done[par], turn + 1)
                    e_next, e = experts(t, 1, 2, t + 2)
                    load_weights(e, par)
                elif has(t, 1):
                    e_next, = experts(t, 1, 1, t + 2)
                if has(t, -1):
                    store(t - 1, 1 - par)
                if has(t, 1):
                    load_biases(e_next, 1 - par)

            e0, e1 = experts(0, 0, 2, 1)
            load_weights(e0, 0)
            load_weights(e1, 1)
            sp.wait_ge(table_ready, 1)
            load_biases(e0, 0)
            all_tiles(sp, tile)
            store(TILES - 1, (TILES - 1) % 2)
            for par in range(2):
                sp.wait_ge(y_stored[par], 16 * ((TILES + 1 - par) // 2))

        @block.gpsimd
        def _(pool):
            pool.memset(ident[:], 0.0).then_inc(consts_step, 1)
            pool.wait_ge(consts_step, 1)
            pool.affine_select(out=ident[:], in_=ident[:], compare_op=ALU.not_equal, fill=1.0, base=0,
                               pattern=[[-1, P]], channel_multiplier=1).then_inc(consts_step, 1)
            pool.iota(count_i[:], pattern=[[1, P]], base=0, channel_multiplier=0).then_inc(counts_ready, 1)
            pool.iota(number_i[:], pattern=[[P, NBK]], base=0, channel_multiplier=1).then_inc(counts_ready, 1)

            def gather_rows(par, turn):
                pool.wait_ge(index_ready[par], turn + 1)
                pool.sem_inc(pool_turns, 1)
                for blk in range(TB):
                    pool.indirect_dma_start(x_in[par][:, blk, :], None, x2_dram,
                                            bass.IndirectOffsetOnAxis(index[par][:, blk:blk + 1], 0))\
                        .then_inc(x_loaded[par], 16)

            def low_parts(par, turn):
                pool.wait_ge(gu_hi_done[par], turn + 1)
                pool.sem_inc(pool_turns, 1)
                pool.tensor_tensor(gu_lo[par][:], gu_raw[par][:], gu_hi[par][:].bitcast(F32), ALU.subtract)\
                    .then_inc(gu_lo_done[par], 1)
                pool.wait_ge(dn_hi_done[par], turn + 1)
                pool.sem_inc(pool_turns, 1)
                pool.tensor_tensor(dn_lo[par][:], dn_raw[par][:], dn_hi[par][:].bitcast(F32), ALU.subtract)\
                    .then_inc(dn_lo_done[par], 1)

            def tile(t, par, turn):
                if has(t, 1):
                    low_parts(1 - par, turn + par)
                if has(t, 2):
                    gather_rows(par, turn + 1)

            low_parts(0, 0)
            gather_rows(0, 0)
            gather_rows(1, 0)
            all_tiles(pool, tile)

        @block.scalar
        def _(act):
            def gu_high(t, par, turn):
                act.wait_ge(w_loaded[par], 16 * W_LOADS * (turn + 1))
                if has(t, -2):
                    act.wait_ge(gu_made[1], (t - 1) * (FC // 2))
                act.copy(gu_hi[par][:], gu_raw[par][:]).then_inc(gu_hi_done[par], 1)

            def dn_high(t, par):
                if has(t, -2):
                    act.wait_ge(y_made[1], (t - 1) * (TB // 2))
                act.copy(dn_hi[par][:], dn_raw[par][:]).then_inc(dn_hi_done[par], 1)

            def x_high(t, par):
                act.wait_ge(x_turned, t + 1)
                for k in range(KC):
                    ins = act.copy(xT_hi[par][:, k, :], ps_x[k][:])
                ins.then_inc(x_hi, 1)

            def tile(t, par, turn):
                def gates(f):
                    n, m = f % 2, t * (FC // 2) + f // 2
                    act.wait_ge(gu_made[n], m + 1)
                    act.wait_ge(hid_done[n], m)
                    act.activation(gate[n][:], ps_g[n][:], ACT.Silu, bias=bias[par][:, 0, f:f + 1]).then_inc(gate_done[n], 1)

                def hid_high(f):
                    n, m = f % 2, t * (FC // 2) + f // 2
                    act.wait_ge(hid_done[n], m + 1)
                    act.wait_ge(y_made[1], t * (TB // 2))
                    act.copy(hid_hi[:, f, :], hid[n][:]).then_inc(hid_hi_done[n], 1)

                if has(t, 1):
                    gu_high(t + 1, 1 - par, turn + par)
                act.wait_ge(b_loaded[par], 16 * B_LOADS * (turn + 1))
                gates(0)
                gates(1)
                hid_high(0)
                hid_high(1)
                if has(t, 1):
                    x_high(t + 1, 1 - par)
                    dn_high(t + 1, 1 - par)
                for f in range(2, FC):
                    gates(f)
                    hid_high(f)

            act.wait_ge(table_turned, 1)
            act.copy(bias_table[:].rearrange("p n e f -> p (n e f)"), ps_y[0][:, 0:2 * E * FC]).then_inc(table_ready, 1)
            gu_high(0, 0, 0)
            dn_high(0, 0)
            x_high(0, 0)
            all_tiles(act, tile)

        @block.vector
        def _(vec):
            def x_low(t, par):
                vec.wait_ge(x_hi, t + 1)
                for k in range(KC):
                    ins = vec.tensor_tensor(xT_lo[par][:, k, :], ps_x[k][:], xT_hi[par][:, k, :].bitcast(F32), ALU.subtract)
                ins.then_inc(x_lo, 1)

            def keep_y(t, par, turn):
                vec.wait_ge(y_stored[par], 16 * turn)
                for blk in range(TB):
                    n = blk % 2
                    vec.wait_ge(y_made[n], t * (TB // 2) + blk // 2 + 1)
                    vec.tensor_tensor(y_out[par][:, blk, :], ps_y[n][:, 0:D], dn_bias[par][:], ALU.add).then_inc(y_kept[n], 1)

            def tile_index(t, par):
                if has(t, -2):
                    vec.wait_ge(x_turned, t - 1)
                vec.tensor_copy(index[par][:], token[:, bass.ds(t * TB, TB)]).then_inc(index_ready[par], 1)

            def tile(t, par, turn):
                def hidden(f):
                    n, m = f % 2, t * (FC // 2) + f // 2
                    vec.wait_ge(gate_done[n], m + 1)
                    vec.wait_ge(hid_lo_done[n], m)
                    vec.scalar_tensor_tensor(hid[n][:], ps_u[n][:], bias[par][:, 1, f:f + 1], gate[n][:],
                                             ALU.add, ALU.mult).then_inc(hid_done[n], 1)

                def hid_low(f):
                    n, m = f % 2, t * (FC // 2) + f // 2
                    vec.wait_ge(hid_hi_done[n], m + 1)
                    vec.tensor_tensor(hid_lo[:, f, :], hid[n][:], hid_hi[:, f, :].bitcast(F32), ALU.subtract)\
                        .then_inc(hid_lo_done[n], 1)

                hidden(0)
                hidden(1)
                if has(t, -1):
                    keep_y(t - 1, 1 - par, turn - 1 + par)
                hid_low(0)
                hid_low(1)
                if has(t, 2):
                    tile_index(t + 2, par)
                if has(t, 1):
                    x_low(t + 1, 1 - par)
                for f in range(2, FC):
                    hidden(f)
                    hid_low(f)

            vec.wait_ge(counts_ready, 2)
            vec.tensor_copy(count[:], count_i[:]).then_inc(count_step, 1)
            vec.tensor_copy(number[:], number_i[:]).then_inc(count_step, 1)
            vec.wait_ge(count_step, 2)
            for i in range(BATCHES):
                k, first = i // (BATCHES // 2), i % (BATCHES // 2) * HOT
                if i >= 2:
                    vec.wait_ge(hot_used, i - 1)
                vec.tensor_tensor(row_hot[i % 2][:], count[:].unsqueeze(1).to_broadcast([P, HOT, P]),
                                  slot_row[k][:, first:first + HOT].unsqueeze(2).to_broadcast([P, HOT, P]), ALU.is_equal)
                for j in range(HOT):
                    n = first + j
                    ins = vec.tensor_scalar(col_hot[i % 2][:, j, :], count[:, 0:COLS], slot_col[k][:, n:n + 1],
                                            number[:, n:n + 1], ALU.is_equal, ALU.mult)
                ins.then_inc(hot_ready, 1)
            vec.wait_ge(hot_used, BATCHES)
            vec.tensor_copy(token[:], ps_u[0][:, 0:COLS]).then_inc(token_kept, 1)
            vec.wait_ge(token_kept, 1)
            tile_index(0, 0)
            tile_index(1, 1)
            x_low(0, 0)
            all_tiles(vec, tile)
            keep_y(TILES - 1, (TILES - 1) % 2, (TILES - 1) // 2)

        @block.tensor
        def _(pe):
            pe.wait_ge(consts_step, 2)
            pe.wait_ge(rows_loaded, 32)
            pe.transpose(ps_y[0][:, 0:2 * E * FC], bias_rows[:], ident[0:2 * E * FC, 0:2 * E * FC]).then_inc(table_turned, 1)
            pe.wait_ge(table_ready, 1)

            def turn_x(t, par, turn):
                pe.wait_ge(x_loaded[par], 16 * TB * (turn + 1))
                pe.wait_ge(x_lo, t)
                for k in range(KC):
                    for blk in range(TB):
                        mm = pe.transpose(ps_x[k][:, blk * P:(blk + 1) * P], x_in[par][:, blk, k * P:(k + 1) * P], ident[:])
                mm.then_inc(x_turned, 1)

            def gate_up(t, par, f):
                n, m = f % 2, t * (FC // 2) + f // 2
                pe.wait_ge(hid_done[n], m)
                for out, first in ((ps_g[n], 0), (ps_u[n], FF)):
                    cols = slice(first + f * P, first + (f + 1) * P)
                    todo = [p for k in range(KC) for p in ((gu_hi, xT_hi, k), (gu_hi, xT_lo, k), (gu_lo, xT_hi, k))]
                    for s, (w, x, k) in enumerate(todo):
                        mm = pe.matmul(out[:], w[par][:, k, cols], x[par][:, k, :], start=(s == 0), stop=(s == len(todo) - 1))
                mm.then_inc(gu_made[n], 1)

            def down(t, par, turn):
                pe.wait_ge(dn_lo_done[par], turn + 1)
                for n in range(2):
                    pe.wait_ge(hid_lo_done[n], (t + 1) * (FC // 2))
                for blk in range(TB):
                    n, rows = blk % 2, slice(blk * P, (blk + 1) * P)
                    pe.wait_ge(y_kept[n], t * (TB // 2) + blk // 2)
                    todo = [p for f in range(FC) for p in ((hid_hi, dn_hi, f), (hid_hi, dn_lo, f), (hid_lo, dn_hi, f))]
                    for s, (h, w, f) in enumerate(todo):
                        mm = pe.matmul(ps_y[n][:, 0:D], h[:, f, rows], w[par][:, f, :], start=(s == 0), stop=(s == len(todo) - 1))
                    mm.then_inc(y_made[n], 1)

            def tile(t, par, turn):
                pe.wait_ge(x_lo, t + 1)
                pe.wait_ge(gu_lo_done[par], turn + 1)
                gate_up(t, par, 0)
                gate_up(t, par, 1)
                if has(t, -1):
                    down(t - 1, 1 - par, turn - 1 + par)
                if has(t, 1):
                    turn_x(t + 1, 1 - par, turn + par)
                for f in range(2, FC):
                    gate_up(t, par, f)

            for i in range(BATCHES):
                pe.wait_ge(hot_ready, i + 1)
                for j in range(HOT):
                    mm = pe.matmul(ps_u[0][:, 0:COLS], row_hot[i % 2][:, j, :], col_hot[i % 2][:, j, :],
                                   start=(i == 0 and j == 0), stop=(i == BATCHES - 1 and j == HOT - 1))
                mm.then_inc(hot_used, 1)
            turn_x(0, 0, 0)
            all_tiles(pe, tile)
            down(TILES - 1, (TILES - 1) % 2, (TILES - 1) // 2)


def combine(nc, sh, plan, x2_all, slots, gates, y_sorted, out):
    D, NBK = sh.D, plan.BLOCKS
    G = 2
    GROUPS = NBK // G
    BUFS = 4
    with ExitStack() as ctx:
        def sb(name, shape, dt=F32):
            return ctx.enter_context(nc.sbuf_tensor(name, shape, dt))

        def sem(name):
            return sh.semaphore(nc, name)

        def sems(name):
            return [sem(f"{name}{n}") for n in range(BUFS)]

        y = [[sb(f"f_y{par}_{k}", [P, G, D]) for k in range(2)] for par in range(BUFS)]
        resid = [sb(f"f_resid{par}", [P, G, D]) for par in range(BUFS)]
        stats = [sb(f"f_stats{par}", [P, G, 6]) for par in range(BUFS)]
        mv = [sb(f"f_mv{par}", [P, G, 2]) for par in range(BUFS)]
        ln_var, rstd = ([sb(f"f_{x}{par}", [P, G]) for par in range(BUFS)] for x in ("ln_var", "rstd"))
        eps_col = sb("f_eps_col", [P, 1])
        gathered, added, normed, var_ready, stored = (
            sems("f_gathered"), sems("f_added"), sems("f_normed"), sems("f_var_ready"), sems("f_stored"))
        eps_ready, step, ln_step, rstd_ready = sem("f_eps_ready"), sem("f_step"), sem("f_ln_step"), sems("f_rstd_ready")
        vec_turns = sem("f_vec_turns")
        block = ctx.enter_context(nc.Block())
        out_rows = out.rearrange("b (k p) d -> p (b k) d", p=P)

        @block.gpsimd
        def _(pool):
            pool.memset(eps_col[:], LN_EPS).then_inc(eps_ready, 1)
            for i in range(GROUPS):
                par, turn = i % BUFS, i // BUFS
                if turn:
                    pool.wait_ge(added[par], turn * G)
                for j in range(G):
                    for k in range(2):
                        n = i * G + j
                        pool.indirect_dma_start(y[par][k][:, j, :], None, y_sorted,
                                                bass.IndirectOffsetOnAxis(slots[k][:, n:n + 1], 0))\
                            .then_inc(gathered[par], 16)

        @block.scalar
        def _(act):
            act.wait_ge(eps_ready, 1)
            with act.Fori(0, GROUPS // BUFS) as turn:
                for par in range(BUFS):
                    act.wait_ge(var_ready[par], turn + 1)
                    act.activation(ln_var[par][:], mv[par][:, :, 1], ACT.Ln, bias=eps_col[:]).then_inc(ln_step, 1)
                    act.wait_ge(ln_step, turn * BUFS + par + 1)
                    act.activation(rstd[par][:], ln_var[par][:], ACT.Exp, scale=-0.5).then_inc(rstd_ready[par], 1)

        @block.vector
        def _(vec):
            def add_rows(turn, par):
                first = (turn * BUFS + par) * G
                vec.wait_ge(gathered[par], 16 * 2 * G * (turn + 1))
                vec.wait_ge(stored[par], 16 * turn)
                for j in range(G):
                    n = first + j
                    vec.scalar_tensor_tensor(resid[par][:, j, :], y[par][0][:, j, :], gates[0][:, bass.ds(n, 1)],
                                             x2_all[:, bass.ds(n, 1), :].rearrange("p n d -> p (n d)"),
                                             ALU.mult, ALU.add).then_inc(step, 1)
                for j in range(G):
                    n = first + j
                    vec.wait_ge(step, (turn * BUFS + par) * 2 * G + G + j)
                    ins = vec.scalar_tensor_tensor(resid[par][:, j, :], y[par][1][:, j, :], gates[1][:, bass.ds(n, 1)],
                                                   resid[par][:, j, :], ALU.mult, ALU.add)
                    ins.then_inc(step, 1)
                vec.wait_ge(step, (turn * BUFS + par + 1) * 2 * G)
                for j in range(G):
                    vec.bn_stats(stats[par][:, j, :], resid[par][:, j, :]).then_inc(added[par], 1)
                vec.wait_ge(added[par], G * (turn + 1))
                vec.sem_inc(vec_turns, 1)
                for j in range(G):
                    ins = vec.bn_aggr(mv[par][:, j, :], stats[par][:, j, :])
                ins.then_inc(var_ready[par], 1)

            def normalise(turn, par):
                vec.wait_ge(rstd_ready[par], turn + 1)
                for j in range(G):
                    ins = vec.tensor_scalar(resid[par][:, j, :], resid[par][:, j, :], mv[par][:, j, 0:1],
                                            rstd[par][:, j:j + 1], ALU.subtract, ALU.mult)
                ins.then_inc(normed[par], 1)

            def groups(turn, first):
                for par in range(BUFS):
                    add_rows(turn, par)
                    if par:
                        normalise(turn, par - 1)
                    elif not first:
                        normalise(turn - 1, BUFS - 1)

            groups(0, True)
            with vec.Fori(1, GROUPS // BUFS) as turn:
                groups(turn, False)
            normalise(GROUPS // BUFS - 1, BUFS - 1)

        @block.sync
        def _(sp):
            with sp.Fori(0, GROUPS // BUFS) as turn:
                for par in range(BUFS):
                    sp.wait_ge(normed[par], turn + 1)
                    sp.dma_start(out_rows[:, bass.ds((turn * BUFS + par) * G, G), :], resid[par][:]).then_inc(stored[par], 16)
            for par in range(BUFS):
                sp.wait_ge(stored[par], 16 * GROUPS // BUFS)


def decoder_layer(nc, x, ctx_1024, mask, Wq, Wk, Wv, Wo, Wa, ba, xWq, xbq, xWk, xbk, xWv, xbv, xWo, xbo,
                  router_w, gate_w, gate_b, up_w, up_b, down_w, down_b, out):
    with ExitStack() as ctx:
        sh = Shapes(x, Wq, ctx_1024, gate_w)
        plan = Plan(sh)
        x1_dram = nc.dram_tensor("x1_rows", list(x.shape), F32).ap()
        x2_dram = nc.dram_tensor("x2_rows", list(x.shape), F32).ap()
        y_sorted = nc.dram_tensor("y_sorted", [plan.ROWS, sh.D], F32).ap()

        def sb(name, shape, dt=F32):
            return ctx.enter_context(nc.sbuf_tensor(name, shape, dt))

        slots = [sb(f"slots{k}", [P, plan.BLOCKS], U32) for k in range(2)]
        slot_col, slot_row = ([sb(f"slot_{x}{k}", [P, plan.BLOCKS]) for k in range(2)] for x in ("col", "row"))
        gates = [sb(f"gates{k}", [P, plan.BLOCKS]) for k in range(2)]
        tile_table = sb("tile_table", [1, plan.TILES], I32)
        linear_attention(nc, sh, x, Wq, Wk, Wv, Wo, Wa, ba, x1_dram)
        sh.end_stage(nc)
        x2_all = sb("x2_all", [P, plan.BLOCKS, sh.D])
        logitsT = sb("logitsT", [sh.E, plan.TOKENS])
        cross_attention(nc, sh, x1_dram, ctx_1024, mask, xWq, xbq, xWk, xbk, xWv, xbv, xWo, xbo,
                        router_w, x2_dram, x2_all, logitsT)
        sh.end_stage(nc)
        route_tokens(nc, sh, plan, logitsT, slots, slot_col, slot_row, gates, tile_table)
        run_experts(nc, sh, plan, x2_dram.rearrange("b n d -> (b n) d"), slot_col, slot_row, tile_table,
                    gate_w, gate_b, up_w, up_b, down_w, down_b, y_sorted)
        combine(nc, sh, plan, x2_all, slots, gates, y_sorted, out)


_INS = ["x", "ctx_1024", "mask_BxSxS2_if1"] + ["L0_attn_" + n for n in ("Wq", "Wk", "Wv", "Wo", "Wa", "ba")] \
    + ["L0_xattn_" + n for n in ("Wq", "bq", "Wk", "bk", "Wv", "bv", "Wo", "bo")] \
    + ["L0_ffn_" + n for n in ("router_w", "gate_w", "gate_b", "up_w", "up_b", "down_w", "down_b")]


def kernel(**inputs):
    import numpy as _np
    import concourse.bacc as _bacc
    from concourse.bass_utils import run_bass_kernel_spmd as _run

    nc = _bacc.Bacc("TRN2", target_bir_lowering=False, num_devices=1)
    arrays, args = {}, []
    for name in _INS:
        a = _np.ascontiguousarray(inputs[name])
        arrays[f"in_{name}"] = a
        args.append(nc.dram_tensor(f"in_{name}", a.shape, mybir.dt.from_np(a.dtype), kind="ExternalInput").ap())
    args.append(nc.dram_tensor("out", inputs["x"].shape, F32, kind="ExternalOutput").ap())
    decoder_layer(nc, *args)
    return _run(nc, [arrays], core_ids=[0]).results[0]["out"]
```
